# Optimizing a Trainium2 kernel written in Bass

```python
import numpy as np
import jax
import jax.numpy as jnp

def _softmax(x, axis=-1):
    return jax.nn.softmax(x, axis=axis)

def _gelu(x):
    return jax.nn.gelu(x, approximate=True)

def _silu(x):
    return jax.nn.silu(x)

def _sigmoid(x):
    return jax.nn.sigmoid(x)

def _layernorm(x, axis=-1, eps=1e-05):
    m = jnp.mean(x, axis=axis, keepdims=True)
    v = jnp.var(x, axis=axis, keepdims=True)
    return (x - m) / jnp.sqrt(v + eps)

def _scatter_add(tgt, idx, src, axis=0):
    return tgt.at[idx].add(src)

def _segment_sum(src, seg, n):
    return jax.ops.segment_sum(src, seg, n)
kernel_name = 'mk_adaln_d1_jaxref_r8_92bda3'

def setup_inputs(seed: int=0):
    np.random.seed(seed)
    _w = jnp.asarray

    def _L0_attn_setup():
        import jax, jax.numpy as jnp
        import numpy as np
        import math
        N_HEADS = 16

        def _rope_tables(seq_len, head_dim):
            pos = jnp.arange(seq_len, dtype=jnp.float32)
            freqs = jnp.exp(jnp.arange(0, head_dim, 2, dtype=jnp.float32) * (-math.log(10000.0) / head_dim))
            angles = pos[:, None] * freqs[None, :]
            cos_emb = jnp.zeros((seq_len, head_dim), jnp.float32).at[:, 0::2].set(jnp.cos(angles))
            sin_emb = jnp.zeros((seq_len, head_dim), jnp.float32).at[:, 1::2].set(jnp.sin(angles))
            return (cos_emb, sin_emb)
        key = jax.random.key(seed)
        ks = jax.random.split(key, 5)
        B, S, D = (2, 256, 128)
        scale = 1.0 / math.sqrt(D)
        return {'x': jax.random.normal(ks[0], (B, S, D), jnp.float32), 'Wq': jax.random.normal(ks[1], (D, D), jnp.float32) * scale, 'Wk': jax.random.normal(ks[2], (D, D), jnp.float32) * scale, 'Wv': jax.random.normal(ks[3], (D, D), jnp.float32) * scale, 'Wo': jax.random.normal(ks[4], (D, D), jnp.float32) * scale}
    _L0_attn_in = _L0_attn_setup()

    def _L0_ffn_setup():
        import jax, jax.numpy as jnp
        import numpy as np
        B, T, D, E, H, K = (2, 256, 128, 8, 512, 2)
        key = jax.random.key(seed)
        ks = jax.random.split(key, 8)
        s = 0.02
        return {'x': jax.random.normal(ks[0], (B, T, D), jnp.float32), 'rw1': jax.random.normal(ks[1], (D, D), jnp.float32) * s, 'rb1': jnp.zeros((D,), jnp.float32), 'rw2': jax.random.normal(ks[2], (D, E), jnp.float32) * s, 'rb2': jnp.zeros((E,), jnp.float32), 'we1': jax.random.normal(ks[3], (E, D, H), jnp.float32) * s, 'be1': jnp.zeros((E, H), jnp.float32), 'we2': jax.random.normal(ks[4], (E, H, D), jnp.float32) * s, 'be2': jnp.zeros((E, D), jnp.float32)}
    _L0_ffn_in = _L0_ffn_setup()
    _L0_c = _w((lambda *s: np.random.randn(*s).astype(np.float32) * 0.05)(4, 128))
    _L0_wmod = _w((lambda *s: np.random.randn(*s).astype(np.float32) * 0.05)(128, 6 * 128) * 128 ** (-0.5))
    _d = {'L0_attn_x': _L0_attn_in['x'], 'L0_attn_Wq': _L0_attn_in['Wq'], 'L0_attn_Wk': _L0_attn_in['Wk'], 'L0_attn_Wv': _L0_attn_in['Wv'], 'L0_attn_Wo': _L0_attn_in['Wo'], 'L0_ffn_rw1': _L0_ffn_in['rw1'], 'L0_ffn_rb1': _L0_ffn_in['rb1'], 'L0_ffn_rw2': _L0_ffn_in['rw2'], 'L0_ffn_rb2': _L0_ffn_in['rb2'], 'L0_ffn_we1': _L0_ffn_in['we1'], 'L0_ffn_be1': _L0_ffn_in['be1'], 'L0_ffn_we2': _L0_ffn_in['we2'], 'L0_ffn_be2': _L0_ffn_in['be2'], 'L0_c': _L0_c, 'L0_wmod': _L0_wmod}
    _x0 = _d['L0_attn_x']
    _d['L0_attn_x'] = jax.random.normal(jax.random.fold_in(jax.random.key(seed), 1), (4, 1024, 128), dtype=_x0.dtype)
    del _x0
    return _d

def reference(L0_attn_x, L0_attn_Wq, L0_attn_Wk, L0_attn_Wv, L0_attn_Wo, L0_ffn_rw1, L0_ffn_rb1, L0_ffn_rw2, L0_ffn_rb2, L0_ffn_we1, L0_ffn_be1, L0_ffn_we2, L0_ffn_be2, L0_c, L0_wmod):

    def _L0_attn_ref(x, Wq, Wk, Wv, Wo):
        import jax, jax.numpy as jnp
        import numpy as np
        import math
        N_HEADS = 16

        def _rope_tables(seq_len, head_dim):
            pos = jnp.arange(seq_len, dtype=jnp.float32)
            freqs = jnp.exp(jnp.arange(0, head_dim, 2, dtype=jnp.float32) * (-math.log(10000.0) / head_dim))
            angles = pos[:, None] * freqs[None, :]
            cos_emb = jnp.zeros((seq_len, head_dim), jnp.float32).at[:, 0::2].set(jnp.cos(angles))
            sin_emb = jnp.zeros((seq_len, head_dim), jnp.float32).at[:, 1::2].set(jnp.sin(angles))
            return (cos_emb, sin_emb)
        B, S, D = x.shape
        H = N_HEADS
        hd = D // H
        q = (x @ Wq.T).reshape(B, S, H, hd)
        k = (x @ Wk.T).reshape(B, S, H, hd)
        v = (x @ Wv.T).reshape(B, S, H, hd)
        cos_emb, sin_emb = _rope_tables(S, hd)
        cos = cos_emb[None, :, None, :]
        sin = sin_emb[None, :, None, :]
        q = q * cos - jnp.roll(q, 1, axis=-1) * sin
        k = k * cos - jnp.roll(k, 1, axis=-1) * sin
        q = q.transpose(0, 2, 1, 3)
        k = k.transpose(0, 2, 1, 3)
        v = v.transpose(0, 2, 1, 3)
        scores = jnp.einsum('bhqd,bhkd->bhqk', q, k) / math.sqrt(hd)
        attn = jax.nn.softmax(scores, axis=-1)
        ctx = jnp.einsum('bhqk,bhkd->bhqd', attn, v)
        ctx = ctx.transpose(0, 2, 1, 3).reshape(B, S, D)
        return ctx @ Wo.T

    def _L0_ffn_ref(x, rw1, rb1, rw2, rb2, we1, be1, we2, be2):
        import jax, jax.numpy as jnp
        import numpy as np
        B, T, D, E, H, K = (2, 256, 128, 8, 512, 2)
        b, t, d = x.shape
        xt = x.reshape(b * t, d)
        n = xt.shape[0]
        logits = jax.nn.silu(xt @ rw1 + rb1) @ rw2 + rb2
        _, idx = jax.lax.top_k(logits, K)
        mask = jnp.zeros((n, E), bool).at[jnp.arange(n)[:, None], idx].set(True)
        w = jax.nn.softmax(jnp.where(mask, logits, -jnp.inf), axis=1)
        h = jax.nn.silu(jnp.einsum('nd,edh->enh', xt, we1) + be1[:, None, :])
        eo = jnp.einsum('enh,ehd->end', h, we2) + be2[:, None, :]
        y = xt + jnp.einsum('ne,end->nd', w, eo)
        return y.reshape(b, t, d)
    x = L0_attn_x
    mod = (_silu(L0_c) @ L0_wmod).reshape(L0_c.shape[0], 6, 1, -1)
    sa, ca, ga, sb, cb, gb = (mod[:, 0], mod[:, 1], mod[:, 2], mod[:, 3], mod[:, 4], mod[:, 5])
    ga = (2 * (ga >= 0) - 1) * jnp.maximum(jnp.abs(ga), 0.25)
    gb = (2 * (gb >= 0) - 1) * jnp.maximum(jnp.abs(gb), 0.25)
    h = _layernorm(x, axis=-1) * (1 + ca) + sa
    x = x + ga * _L0_attn_ref(h, L0_attn_Wq, L0_attn_Wk, L0_attn_Wv, L0_attn_Wo)
    h = _layernorm(x, axis=-1) * (1 + cb) + sb
    x = x + gb * _L0_ffn_ref(h, L0_ffn_rw1, L0_ffn_rb1, L0_ffn_rw2, L0_ffn_rb2, L0_ffn_we1, L0_ffn_be1, L0_ffn_we2, L0_ffn_be2)
    return x

_drawn_inputs = setup_inputs


def setup_inputs(seed=0):
    import zlib

    import numpy as np

    out = dict(_drawn_inputs(seed))
    spreads = {'L0_ffn_rb1': (0.0, 0.8),
     'L0_ffn_rb2': (0.0, 0.396),
     'L0_ffn_be1': (0.0, 0.8),
     'L0_ffn_be2': (0.0, 2.0)}
    factors = {'L0_attn_Wq': 6.361,
     'L0_attn_Wk': 6.312,
     'L0_attn_Wv': 4.394,
     'L0_attn_Wo': 4.568,
     'L0_ffn_rw1': 5.123,
     'L0_ffn_rw2': 5.31,
     'L0_ffn_we1': 6.286,
     'L0_ffn_we2': 5.646}
    for name, (base, spread) in spreads.items():
        noise = np.random.default_rng([zlib.crc32(name.encode()), seed]).standard_normal(out[name].shape)
        drawn = base * np.exp(spread * noise) if base else spread * noise
        out[name] = jnp.asarray(drawn.astype(out[name].dtype))
    for name, factor in factors.items():
        out[name] = (out[name] * factor).astype(out[name].dtype)
    return out
```

```python
from contextlib import ExitStack

import concourse.bass as bass
import concourse.mybir as mybir
import numpy as np

F32 = mybir.dt.float32
BF16 = mybir.dt.bfloat16
U32 = mybir.dt.uint32
ALU = mybir.AluOpType
ACT = mybir.ActivationFunctionType
AX = mybir.AxisListType

P = 128
B, S, D = 4, 1024, 128
HEADS, HD = 16, 8
NE, HID = 8, 512
NT = S // P
GH = 4
GROUPS = HEADS // GH
NG = B * GROUPS
GF = GH * HD
EPS = 1e-5
BANK = 512

TERMS = ((0, 0), (0, 1), (1, 0), (1, 1), (0, 2), (2, 0))
HALF_ROWS = 3 * HD
MAX_ROW = HALF_ROWS

STEPS = 16
PAIR = 2 * STEPS
LEAD = 6
UNITS = GH * NT
RING = 4


class Count:

    def __init__(self):
        self.seen = 0

    def at(self, n):
        self.seen = max(self.seen, n)
        return n

    def more(self, n=1):
        return self.at(self.seen + n)

    def back(self, n=None):
        n = self.seen if n is None else n
        self.seen -= n
        return -n


def build(nc, t):
    with ExitStack() as ctx:
        def sb(name, shape, dt=F32):
            return ctx.enter_context(nc.sbuf_tensor(name, shape, dt))

        def scratch(name, shape, dt):
            return nc.dram_tensor(name, shape, dt, kind="Internal").ap()

        k = {
            "q_terms": scratch("q_terms", [NG, 2, len(TERMS) // 2, 2, HD, 2, S], BF16),
            "k_terms": scratch("k_terms", [NG, 2, len(TERMS) // 2, 2, HD, 2, S], BF16),
            "x": sb("x_sb", [P, B, NT, D]),
            "mod": sb("mod", [P, B, 6, D]),
            "ident": sb("ident", [P, P]),
            "ident16": sb("ident16", [P, P], BF16),
            "rsqrt_exp": sb("rsqrt_exp", [P, NT]),
            "h_t": sb("h_t", [P, B, S]),
            "v": sb("v", [P, NG, NT, GF]),
            "ctx": sb("ctx", [P, NG, NT, GF]),
        }
        with ExitStack() as operands:
            for name, blocks in (("q_max", 2), ("q_exp", 2), ("k_max", GH), ("k_exp", GH)):
                k[name] = [operands.enter_context(nc.sbuf_tensor(f"{name}{i}", [P, blocks, S], BF16))
                           for i in range(2)]
            k["v_grp"] = [operands.enter_context(nc.sbuf_tensor(f"v_grp{i}", [P, NT, GH, 32], F32))
                          for i in range(2)]
            prepare(nc, t, k)
            attend(nc, t, k)
        k["logits"] = sb("logits", [P, B, NT, NE])
        k["weight"] = sb("weight", [P, B, NT, NE])
        route(nc, t, k)
        experts(nc, t, k)


def prepare(nc, t, k):
    with ExitStack() as ctx:
        def sb(name, shape, dt=F32):
            return ctx.enter_context(nc.sbuf_tensor(name, shape, dt))

        def sem(name):
            return ctx.enter_context(nc.semaphore(name))

        c_t = sb("c_t", [P, B])
        silu_c = sb("silu_c", [P, B])
        silu_cb = sb("silu_cb", [P, B, P])
        wmod = sb("wmod", [P, 6 * D])
        wq, wk, wv = sb("wq", [P, D]), sb("wk", [P, D]), sb("wv", [P, D])
        rope = sb("rope", [P, S])
        g_sign = sb("g_sign", [P, B * 2, D])
        g_size = sb("g_size", [P, B * 2, D])
        stats = sb("stats", [P, NT, 6])
        mean_var = sb("mean_var", [P, NT, 2])
        var_eps = sb("var_eps", [P, NT])
        scale = sb("scale", [P, NT])
        xn = sb("xn", [P, NT, D])
        xm = sb("xm", [P, NT, D])
        h = sb("h", [P, NT, D])
        h_t = sb("h_t1", [P, S])
        rot = [sb(f"rot{i}", [P, S]) for i in range(2)]
        rest = [sb(f"rest{i}", [P, S]) for i in range(2)]
        parts = [sb(f"parts{i}", [P, 3, S], BF16) for i in range(2)]
        ps = [ctx.enter_context(nc.psum_tensor(f"prep{i}", [P, 2 * BANK], F32)) for i in range(4)]
        ps_t, ps_q, ps_k, ps_v = ps

        consts_in = sem("consts_in")
        x_in = sem("x_in")
        ident_ready = sem("ident_ready")
        silu_c_ready = sem("silu_c_ready")
        zeros_ready = sem("zeros_ready")
        silu_cb_ready = sem("silu_cb_ready")
        mod_ps_ready = sem("mod_ps_ready")
        mod_ready = sem("mod_ready")
        dve_done = sem("prep_dve_done")
        pool_done = sem("prep_pool_done")
        var_ready = sem("var_ready")
        scale_ready = sem("scale_ready")
        xn_ready = sem("xn_ready")
        h_ready = sem("h_ready")
        h_t_ps_ready = sem("h_t_ps_ready")
        h_t_ready = sem("h_t_ready")
        qk_ps_ready = sem("qk_ps_ready")
        v_ps_ready = sem("v_ps_ready")
        rot_ready = sem("rot_ready")
        part0_ready = sem("part0_ready")
        rest_ready = sem("rest_ready")
        part1_ready = sem("part1_ready")
        parts_ready = sem("parts_ready")
        parts_stored = sem("parts_stored")
        block = ctx.enter_context(nc.Block())

        loads = [(c_t, t["c_t"]), (wmod, t["wmod"]), (wq, t["wq_t"]), (wk, t["wk_t"]), (wv, t["wv_t"]),
                 (rope, t["rope"])]
        terms = [k[m].rearrange("(b g) h t r f u n -> b h t g (r f u) n", b=B) for m in ("q_terms", "k_terms")]

        @block.sync
        def _(sp):
            for dst, src in loads:
                sp.dma_start(dst[:], src).then_inc(consts_in, 16)
            sp.dma_start(k["x"][:], t["x"].rearrange("b (t p) d -> p b t d", p=P)).then_inc(x_in, 16)
            parts_of = Count()
            with sp.Fori(0, B) as b:
                for qk in range(2):
                    sp.wait_ge(parts_ready, parts_of.more())
                    for n, term in enumerate(TERMS):
                        sp.dma_start(terms[qk][b, n // 3, n % 3],
                                     parts[qk][:, term[qk], :]).then_inc(parts_stored, 16)
                sp.sem_inc(parts_ready, parts_of.back(2))

        @block.gpsimd
        def _(pool):
            own = Count()
            for i in range(2):
                for name in ("q_max", "q_exp", "k_max", "k_exp", "v_grp"):
                    pool.memset(k[name][i][:], 0.0).then_inc(zeros_ready, 1)
            pool.memset(k["rsqrt_exp"][:], -0.5).then_inc(pool_done, 1)
            pool.memset(k["ident"][:], 0.0).then_inc(pool_done, 1)
            pool.memset(k["ident16"][:], 0.0).then_inc(pool_done, 1)
            pool.wait_ge(pool_done, own.more(3))
            for m in ("ident", "ident16"):
                pool.affine_select(out=k[m][:], in_=k[m][:], compare_op=ALU.not_equal, fill=1.0, base=0,
                                   pattern=[[-1, P]], channel_multiplier=1).then_inc(ident_ready, 1)
            pool.sem_inc(pool_done, own.back())
            pool.wait_ge(mod_ready, 1)
            var, normed = Count(), Count()
            with pool.Fori(0, B) as b:
                pool.wait_ge(var_ready, var.more())
                pool.tensor_tensor(scale[:], var_eps[:], k["rsqrt_exp"][:], ALU.pow).then_inc(scale_ready, 1)
                pool.wait_ge(xn_ready, normed.more())
                shape = [P, NT, D]
                pool.tensor_tensor(xm[:], xn[:], k["mod"][:, b, 1, :].unsqueeze(1).to_broadcast(shape),
                                   ALU.mult).then_inc(pool_done, 1)
                pool.wait_ge(pool_done, own.more())
                pool.tensor_tensor(h[:], xm[:], k["mod"][:, b, 0, :].unsqueeze(1).to_broadcast(shape),
                                   ALU.add).then_inc(h_ready, 1)
                pool.sem_inc(var_ready, var.back(1))
                pool.sem_inc(xn_ready, normed.back(1))
                pool.sem_inc(pool_done, own.back(1))

        @block.scalar
        def _(act):
            act.wait_ge(consts_in, 16 * len(loads))
            act.activation(silu_c[:], c_t[:], ACT.Silu).then_inc(silu_c_ready, 1)
            h_t_ps, v_ps = Count(), Count()
            rotated, rests, stored = Count(), Count(), Count()
            act.sem_inc(parts_stored, 16 * 2 * len(TERMS))
            with act.Fori(0, B) as b:
                for c in range(2):
                    act.wait_ge(h_t_ps_ready, h_t_ps.more())
                    act.copy(h_t[:, c * BANK:(c + 1) * BANK],
                             ps_t[:, c * BANK:(c + 1) * BANK]).then_inc(h_t_ready, 1)
                act.wait_ge(parts_stored, stored.more(16 * 2 * len(TERMS)))
                for qk in range(2):
                    act.wait_ge(rot_ready, rotated.more())
                    act.copy(parts[qk][:, 0, :], rot[qk][:]).then_inc(part0_ready, 1)
                for qk in range(2):
                    act.wait_ge(rest_ready, rests.more())
                    act.copy(parts[qk][:, 1, :], rest[qk][:]).then_inc(part1_ready, 1)
                act.wait_ge(v_ps_ready, v_ps.more())
                v_of = k["v"].rearrange("p (b g) t f -> p b g t f", b=B)
                act.copy(v_of[:, b], ps_v[:].rearrange("p (t g f) -> p g t f", t=NT, g=GROUPS))
                act.sem_inc(h_t_ps_ready, h_t_ps.back(2))
                act.sem_inc(parts_stored, stored.back(16 * 2 * len(TERMS)))
                act.sem_inc(rot_ready, rotated.back(2))
                act.sem_inc(rest_ready, rests.back(2))
                act.sem_inc(v_ps_ready, v_ps.back(1))
            act.wait_ge(parts_stored, stored.more(16 * 2 * len(TERMS)))

        @block.vector
        def _(dve):
            own = Count()

            def link(ins):
                ins.then_inc(dve_done, 1)
                dve.wait_ge(dve_done, own.more())

            dve.wait_ge(silu_c_ready, 1)
            dve.tensor_copy(silu_cb[:], silu_c[:].unsqueeze(2).to_broadcast([P, B, P])).then_inc(silu_cb_ready, 1)
            mod = k["mod"][:].rearrange("p b s d -> p (b s d)")
            for b in range(B):
                dve.wait_ge(mod_ps_ready, b + 1)
                for half in range(2):
                    at = (2 * b + half) * 3 * D
                    dve.tensor_copy(mod[:, at:at + 3 * D],
                                    ps[b][:, half * BANK:half * BANK + 3 * D]).then_inc(dve_done, 1)
            dve.wait_ge(dve_done, own.more(2 * B))
            trio = k["mod"][:].rearrange("p b (u s) d -> p (b u) s d", u=2)
            gate, one_c = trio[:, :, 2, :], trio[:, :, 1, :]
            link(dve.tensor_scalar(g_sign[:], gate, 0.0, 2.0, ALU.is_ge, ALU.mult))
            link(dve.scalar_tensor_tensor(out=g_size[:], in0=gate, scalar=-1.0, in1=gate, op0=ALU.mult, op1=ALU.max))
            link(dve.tensor_scalar(g_size[:], g_size[:], 0.25, None, ALU.max))
            link(dve.tensor_scalar(one_c, one_c, 1.0, None, ALU.add))
            dve.scalar_tensor_tensor(out=gate, in0=g_sign[:], scalar=-1.0, in1=g_size[:], op0=ALU.add,
                                     op1=ALU.mult).then_inc(mod_ready, 1)
            dve.sem_inc(dve_done, own.back())
            dve.wait_ge(zeros_ready, 10)
            for i in range(2):
                dve.memset(k["v_grp"][i][:, :, :, HD:HD + 1], 1.0)
                for r in range(2):
                    dve.memset(k["k_exp"][i][64 * r:64 * r + 32, 2 * r:2 * r + 2, :], 1.0)
            dve.wait_ge(x_in, 16)
            dve.wait_ge(consts_in, 16 * len(loads))
            scaled, qk_ps = Count(), Count()
            part0, part1 = Count(), Count()
            with dve.Fori(0, B) as b:
                for i in range(NT):
                    dve.bn_stats(stats[:, i, :], k["x"][:, b, i, :]).then_inc(dve_done, 1)
                dve.wait_ge(dve_done, own.more(NT))
                for i in range(NT):
                    dve.bn_aggr(mean_var[:, i, :], stats[:, i, :]).then_inc(dve_done, 1)
                dve.wait_ge(dve_done, own.more(NT))
                dve.tensor_scalar(var_eps[:], mean_var[:, :, 1], EPS, None, ALU.add).then_inc(var_ready, 1)
                dve.wait_ge(scale_ready, scaled.more())
                for i in range(NT):
                    ins = dve.tensor_scalar(xn[:, i, :], k["x"][:, b, i, :], mean_var[:, i, 0:1],
                                            scale[:, i:i + 1], ALU.subtract, ALU.mult)
                ins.then_inc(xn_ready, 1)
                for qk in range(2):
                    dve.wait_ge(qk_ps_ready, qk_ps.more())
                    dve.tensor_tensor(rot[qk][:], ps[1 + qk][:], rope[:], ALU.mult).then_inc(rot_ready, 1)
                for qk in range(2):
                    dve.wait_ge(part0_ready, part0.more())
                    dve.tensor_tensor(rest[qk][:], rot[qk][:], parts[qk][:, 0, :],
                                      ALU.subtract).then_inc(rest_ready, 1)
                for qk in range(2):
                    dve.wait_ge(part1_ready, part1.more())
                    dve.tensor_tensor(parts[qk][:, 2, :], rest[qk][:], parts[qk][:, 1, :],
                                      ALU.subtract).then_inc(parts_ready, 1)
                dve.sem_inc(dve_done, own.back(2 * NT))
                dve.sem_inc(scale_ready, scaled.back(1))
                dve.sem_inc(qk_ps_ready, qk_ps.back(2))
                dve.sem_inc(part0_ready, part0.back(2))
                dve.sem_inc(part1_ready, part1.back(2))

        @block.tensor
        def _(pe):
            pe.wait_ge(silu_cb_ready, 1)
            pe.wait_ge(consts_in, 16 * len(loads))
            for b in range(B):
                for half in range(2):
                    ins = pe.matmul(ps[b][:, half * BANK:half * BANK + 3 * D], silu_cb[:, b, :],
                                    wmod[:, half * 3 * D:(half + 1) * 3 * D], start=True, stop=True)
                ins.then_inc(mod_ps_ready, 1)
            pe.wait_ge(ident_ready, 2)
            pe.wait_ge(mod_ready, 1)
            h_in, h_t_in = Count(), Count()
            with pe.Fori(0, B):
                pe.wait_ge(h_ready, h_in.more())
                for i in range(NT):
                    ins = pe.transpose(ps_t[:, i * P:(i + 1) * P], h[:, i, :], k["ident"][:])
                    if i % 4 == 3:
                        ins.then_inc(h_t_ps_ready, 1)
                pe.wait_ge(h_t_ready, h_t_in.more(2))
                for w, out in ((wq, ps_q), (wk, ps_k)):
                    for c in range(2):
                        ins = pe.matmul(out[:, c * BANK:(c + 1) * BANK], w[:], h_t[:, c * BANK:(c + 1) * BANK],
                                        start=True, stop=True)
                    ins.then_inc(qk_ps_ready, 1)
                for i in range(NT):
                    ins = pe.matmul(ps_v[:, i * P:(i + 1) * P], h_t[:, i * P:(i + 1) * P], wv[:],
                                    start=True, stop=True)
                ins.then_inc(v_ps_ready, 1)
                pe.sem_inc(h_ready, h_in.back(1))
                pe.sem_inc(h_t_ready, h_t_in.back(2))


def attend(nc, t, k):
    with ExitStack() as ctx:
        def sb(name, shape, dt=F32):
            return ctx.enter_context(nc.sbuf_tensor(name, shape, dt))

        def psum(name, shape, dt=F32):
            return ctx.enter_context(nc.psum_tensor(name, shape, dt))

        def sem(name):
            return ctx.enter_context(nc.semaphore(name))

        q_max, k_max, q_exp, k_exp, v_grp = (k[name] for name in ("q_max", "k_max", "q_exp", "k_exp", "v_grp"))
        probs = sb("probs", [P, RING, GH, BANK])
        row_max = [sb(f"row_max{i}", [P, GH, NT]) for i in range(2)]
        neg_rest = sb("neg_rest", [P, GH, NT])
        neg_parts = [sb(f"neg_parts{i}", [P, GH, 3, NT], BF16) for i in range(2)]
        neg_rows = [sb(f"neg_rows{i}", [GH * 3 * NT, P], BF16) for i in range(2)]
        ctx_t = [sb(f"ctx_t{i}", [P, BANK]) for i in range(2)]
        inv_sum = sb("inv_sum", [P, 4 * GH])
        ps_max = [psum(f"ps_max{i}", [P, 2 * BANK]) for i in range(2)]
        ps_scores = [psum(f"ps_scores{i}", [P, BANK]) for i in range(2)]
        ps_ctx = psum("ps_ctx", [P, BANK])
        ps_turn = psum("ps_turn", [P, BANK])

        max_in = [sem(f"max_in{i}") for i in range(2)]
        exp_in = [sem(f"exp_in{i}") for i in range(2)]
        rows_in = [sem(f"rows_in{i}") for i in range(2)]
        v_ready = sem("v_ready")
        v_used = sem("v_used")
        exp_operands_used = sem("exp_operands_used")
        max_scores_ready = sem("max_scores_ready")
        max_taken = sem("max_taken")
        neg_step = sem("neg_step")
        neg_parts_ready = sem("neg_parts_ready")
        neg_turned = sem("neg_turned")
        neg_rows_ready = sem("neg_rows_ready")
        scores_ready = sem("scores_ready")
        probs_ready = sem("probs_ready")
        ctx_added = sem("ctx_added")
        ctx_t_ready = sem("ctx_t_ready")
        ctx_turned = sem("ctx_turned")
        sums_inverted = sem("sums_inverted")
        ctx_ready = sem("ctx_ready")
        block = ctx.enter_context(nc.Block())

        SETS = ((q_max, k_max, max_in), (q_exp, k_exp, exp_in))
        LOADS = 8
        PAIRS = NG // 2
        FIRST = 2

        def unit(n):
            n %= UNITS
            return 2 * (n // 2 % 2) + 1 - n % 2, n // 4

        def units(s):
            return (UNITS + LEAD + 2 * s, UNITS + LEAD + 2 * s + 1)

        def chain_step(s):
            return (s + 4) // STEPS if (s + 4) % STEPS == 0 else None

        @block.sync
        def _(sp):
            def load(which, parity, group):
                q_of, k_of, loaded = SETS[which]
                for dst, src, blocks in ((q_of[parity], k["q_terms"], 1), (k_of[parity], k["k_terms"], 2)):
                    for r in range(2):
                        block = 2 * r * (blocks - 1)
                        for half in range(2):
                            row = 64 * r + 32 * half
                            sp.dma_start(dst[row:row + HALF_ROWS, block:block + 2, :],
                                         src[group, half, :, r].rearrange("t f u n -> t f (u n)")).then_inc(loaded[parity], 16)

            def negated_rows(parity):
                for head in range(GH):
                    row = 64 * (head % 2) + MAX_ROW
                    sp.dma_start(q_exp[parity][row:row + 3, head // 2, :],
                                 neg_rows[parity][head * 3 * NT:(head + 1) * 3 * NT, :]).then_inc(rows_in[parity], 16)

            rows, used = Count(), Count()
            for g in range(2):
                load(0, g, g)
                load(1, g, g)
            sp.wait_ge(neg_rows_ready, rows.more())
            negated_rows(0)
            load(0, 0, 2)
            sp.sem_inc(neg_rows_ready, rows.back())
            with sp.Fori(0, PAIRS - 1) as p:
                sp.wait_ge(neg_rows_ready, rows.more())
                negated_rows(1)
                load(0, 1, 2 * p + 3)
                sp.wait_ge(exp_operands_used, used.more())
                load(1, 0, 2 * p + 2)
                sp.wait_ge(neg_rows_ready, rows.more())
                negated_rows(0)
                load(0, 0, (2 * p + 4) % NG)
                sp.wait_ge(exp_operands_used, used.more())
                load(1, 1, 2 * p + 3)
                sp.sem_inc(neg_rows_ready, rows.back(2))
                sp.sem_inc(exp_operands_used, used.back(2))
            sp.wait_ge(neg_rows_ready, rows.more())
            negated_rows(1)

        @block.gpsimd
        def _(pool):
            def fill(parity, group):
                pool.tensor_copy(v_grp[parity][:, :, :, 0:HD].rearrange("p t h f -> p (t h) f"),
                                 k["v"][:, group].rearrange("p t (h f) -> p (t h) f", h=GH)).then_inc(v_ready, 1)

            for g in range(2):
                fill(g, g)
            used = Count()
            with pool.Fori(0, PAIRS - 1) as p:
                for g in range(2):
                    pool.wait_ge(v_used, used.more())
                    fill(g, 2 * p + 2 + g)
                pool.sem_inc(v_used, used.back(2))

        @block.tensor
        def _(pe):
            maxima_in = [Count(), Count()]
            exps_in = [Count(), Count()]
            rows = [Count(), Count()]
            taken, probs_in = Count(), Count()
            negs, v_in = Count(), Count()
            evacuated, normed = Count(), Count()

            def max_scores(n):
                head, tile = unit(n)
                g = n // UNITS
                if n % UNITS == 0:
                    pe.wait_ge(max_in[g % 2], maxima_in[g % 2].at(16 * LOADS * (g // 2 + 1)))
                if n >= 2:
                    pe.wait_ge(max_taken, taken.at(n - 1))
                r, u = head % 2, head // 2
                for c in range(2):
                    ins = pe.matmul(ps_max[n % 2][:, c * BANK:(c + 1) * BANK],
                                    q_max[g % 2][:, u, tile * P:(tile + 1) * P],
                                    k_max[g % 2][:, 2 * r + u, c * BANK:(c + 1) * BANK],
                                    start=True, stop=True)
                ins.then_inc(max_scores_ready, 1)

            def scores(s, place):
                head, g, c, tile = place, s // STEPS, s // NT % 2, s % NT
                if s % STEPS == 0 and place == 0:
                    pe.wait_ge(exp_in[g % 2], exps_in[g % 2].at(16 * LOADS * (g // 2 + 1)))
                    pe.wait_ge(rows_in[g % 2], rows[g % 2].at(16 * GH * (g // 2 + 1)))
                n = GH * s + place
                if n >= 2:
                    pe.wait_ge(probs_ready, probs_in.at(n - 1))
                r, u = head % 2, head // 2
                pe.matmul(ps_scores[n % 2][:], k_exp[g % 2][:, 2 * r + u, tile * P:(tile + 1) * P],
                          q_exp[g % 2][:, u, c * BANK:(c + 1) * BANK],
                          start=True, stop=True).then_inc(scores_ready, 1)

            def add_ctx(s, signal_v):
                g, tile = s // STEPS, s % NT
                pe.wait_ge(probs_ready, probs_in.at(GH * (s + 1)))
                if s % STEPS == 0:
                    pe.wait_ge(v_ready, v_in.at(g + 1))
                if tile == 0 and s:
                    pe.wait_ge(ctx_t_ready, evacuated.at(s // NT))
                for place in range(GH):
                    head = place
                    ins = pe.matmul(ps_ctx[32 * head:32 * head + 32, :], v_grp[g % 2][:, tile, head, :],
                                    probs[:, s % RING, head, :], start=tile == 0, stop=tile == NT - 1)
                    if place == 0 and s % STEPS == STEPS - 1:
                        ins.then_inc(exp_operands_used, 1)
                    if place == 0 and signal_v:
                        ins.then_inc(v_used, 1)
                ins.then_inc(ctx_added, 1)

            def turn_negated(g):
                pe.wait_ge(neg_parts_ready, negs.at(g + 1))
                pe.transpose(ps_turn[:].bitcast(BF16)[0:GH * 3 * NT, 0:P],
                             neg_parts[g % 2][:].rearrange("p h c t -> p (h c t)"),
                             k["ident16"][:]).then_inc(neg_turned, 1)

            def turn_ctx(chunk):
                pe.wait_ge(ctx_t_ready, evacuated.at(chunk + 1))
                pe.wait_ge(ctx_ready, normed.at(chunk + 1))
                for i in range(4):
                    ins = pe.transpose(ps_turn[:, i * P:(i + 1) * P], ctx_t[chunk % 2][:, i * P:(i + 1) * P],
                                       k["ident"][:])
                ins.then_inc(ctx_turned, 1)

            def step(s, last=False, signal_v=False):
                more_scores = not (last and s == PAIR - 1)
                more_units = not (last and units(s)[0] >= 2 * UNITS)
                if more_scores:
                    scores(s + 1, 0)
                    scores(s + 1, 1)
                add_ctx(s, signal_v)
                if more_scores:
                    scores(s + 1, 2)
                    scores(s + 1, 3)
                if more_units:
                    max_scores(units(s)[0])
                    max_scores(units(s)[1])
                if s % NT == 0 and s:
                    turn_ctx(s // NT - 1)
                if (g := chain_step(s - 1)) is not None and not (last and g == 2):
                    pe.wait_ge(ctx_ready, normed.at(s // NT + 1))
                    turn_negated(g)

            pe.sem_inc(ctx_ready, 1)
            for n in range(UNITS):
                max_scores(n)
            turn_negated(0)
            for n in range(UNITS, UNITS + LEAD):
                max_scores(n)
            for place in range(GH):
                scores(0, place)
            for s in range(FIRST):
                step(s)
            with pe.Fori(0, PAIRS - 1):
                for s in range(FIRST, FIRST + PAIR):
                    step(s, signal_v=s % STEPS == 0)
                pe.sem_inc(max_taken, taken.back(2 * UNITS))
                pe.sem_inc(probs_ready, probs_in.back(GH * PAIR))
                pe.sem_inc(neg_parts_ready, negs.back(2))
                pe.sem_inc(v_ready, v_in.back(2))
                pe.sem_inc(ctx_t_ready, evacuated.back(4))
                pe.sem_inc(ctx_ready, normed.back(4))
                for i in range(2):
                    pe.sem_inc(max_in[i], maxima_in[i].back(16 * LOADS))
                    pe.sem_inc(exp_in[i], exps_in[i].back(16 * LOADS))
                    pe.sem_inc(rows_in[i], rows[i].back(16 * GH))
            for s in range(FIRST, PAIR):
                step(s, last=True)
            turn_ctx(3)
            pe.wait_ge(max_in[0], maxima_in[0].more(16 * LOADS))

        @block.scalar
        def _(act):
            scores_in, added, turned = Count(), Count(), Count()

            def exps(s, evacuate=None):
                for place in range(GH):
                    if place == 2 and evacuate is not None:
                        copy_ctx(evacuate)
                    n = GH * s + place
                    act.wait_ge(scores_ready, scores_in.at(n + 1))
                    if s >= RING and place == 0:
                        act.wait_ge(ctx_added, added.at(s - RING + 1))
                    act.activation(probs[:, s % RING, place, :], ps_scores[n % 2][:], ACT.Exp,
                                   scale=float(HD) ** -0.5).then_inc(probs_ready, 1)

            def copy_ctx(chunk):
                act.wait_ge(ctx_added, added.at(NT * (chunk + 1)))
                act.copy(ctx_t[chunk % 2][:], ps_ctx[:]).then_inc(ctx_t_ready, 1)

            def copy_negated(g):
                act.wait_ge(neg_turned, turned.at(g + 1))
                act.copy(neg_rows[g % 2][:], ps_turn[:].bitcast(BF16)[0:GH * 3 * NT, 0:P]).then_inc(neg_rows_ready, 1)

            def step(s, last=False):
                if (g := chain_step(s - 2)) is not None and not (last and g == 2):
                    copy_negated(g)
                chunk = s // NT if s % NT == NT - 1 else None
                if last and s == PAIR - 1:
                    copy_ctx(chunk)
                else:
                    exps(s + 1, chunk)

            copy_negated(0)
            exps(0)
            for s in range(FIRST):
                step(s)
            with act.Fori(0, PAIRS - 1):
                for s in range(FIRST, FIRST + PAIR):
                    step(s)
                act.sem_inc(scores_ready, scores_in.back(GH * PAIR))
                act.sem_inc(ctx_added, added.back(PAIR))
                act.sem_inc(neg_turned, turned.back(2))
            for s in range(FIRST, PAIR):
                step(s, last=True)

        @block.vector
        def _(dve):
            scored, own = Count(), Count()
            turned, inverted = Count(), Count()

            def take_max(n):
                head, tile = unit(n)
                g = n // UNITS
                dve.wait_ge(max_scores_ready, scored.at(n + 1))
                dve.reduce_max(row_max[g % 2][:, head, tile:tile + 1], ps_max[n % 2][:],
                               axis=AX.X).then_inc(max_taken, 1)

            def split_negated(g):
                top, out = row_max[g % 2], neg_parts[g % 2]
                dve.drain().then_inc(neg_step, 1)
                dve.wait_ge(neg_step, own.more())
                dve.tensor_scalar(out[:, :, 0, :], top[:], -1.0, None, ALU.mult).then_inc(neg_step, 1)
                dve.wait_ge(neg_step, own.more())
                dve.scalar_tensor_tensor(out=neg_rest[:], in0=top[:], scalar=-1.0, in1=out[:, :, 0, :],
                                         op0=ALU.mult, op1=ALU.subtract).then_inc(neg_step, 1)
                dve.wait_ge(neg_step, own.more())
                dve.tensor_copy(out[:, :, 1, :], neg_rest[:]).then_inc(neg_step, 1)
                dve.wait_ge(neg_step, own.more())
                dve.tensor_tensor(out[:, :, 2, :], neg_rest[:], out[:, :, 1, :],
                                  ALU.subtract).then_inc(neg_parts_ready, 1)

            def norm_ctx(chunk, pair):
                dve.wait_ge(ctx_turned, turned.at(chunk + 1))
                view = ps_turn[:].rearrange("p (t c) -> p t c", c=32)
                dve.reciprocal(inv_sum[:], view[:, :, HD]).then_inc(sums_inverted, 1)
                dve.wait_ge(sums_inverted, inverted.more())
                out = k["ctx"][:, 2 * pair + chunk // 2].rearrange("p (c t) (h f) -> p c (t h) f", c=2, h=GH)
                dve.tensor_tensor(out[:, chunk % 2], view[:, :, 0:HD],
                                  inv_sum[:].unsqueeze(2).to_broadcast([P, 4 * GH, HD]),
                                  ALU.mult).then_inc(ctx_ready, 1)

            def step(s, pair, last=False):
                more_units = not (last and units(s)[0] >= 2 * UNITS)
                if more_units:
                    take_max(units(s)[0])
                if s % NT == 1 and s > NT:
                    norm_ctx(s // NT - 1, pair)
                if more_units:
                    take_max(units(s)[1])
                if (g := chain_step(s)) is not None and not (last and g == 2):
                    split_negated(g)

            for n in range(UNITS):
                take_max(n)
            split_negated(0)
            for n in range(UNITS, UNITS + LEAD):
                take_max(n)
            for s in range(FIRST):
                step(s, 0)
            dve.sem_inc(neg_step, own.back())
            with dve.Fori(0, PAIRS - 1) as p:
                for s in range(FIRST, FIRST + PAIR):
                    step(s, p)
                dve.sem_inc(max_scores_ready, scored.back(2 * UNITS))
                dve.sem_inc(neg_step, own.back(8))
                dve.sem_inc(ctx_turned, turned.back(4))
                dve.sem_inc(sums_inverted, inverted.back(4))
            for s in range(FIRST, PAIR):
                step(s, PAIRS - 1, last=True)
            norm_ctx(3, PAIRS - 1)


def route(nc, t, k):
    with ExitStack() as ctx:
        def sb(name, shape, dt=F32):
            return ctx.enter_context(nc.sbuf_tensor(name, shape, dt))

        def sem(name):
            return ctx.enter_context(nc.semaphore(name))

        wo, rw1, rw2 = sb("wo", [P, D]), sb("rw1", [P, D]), sb("rw2", [P, NE])
        rb1, rb2 = sb("rb1", [P, 1]), sb("rb2", [P, NE])
        ctx_s = sb("ctx_s", [P, NT, GROUPS, GF])
        ctx_t = sb("ctx_t_all", [P, S])
        gated = sb("gated", [P, NT, D])
        stats = sb("stats2", [P, NT, 6])
        mean_var = sb("mean_var2", [P, NT, 2])
        var_eps = sb("var_eps2", [P, NT])
        scale = sb("scale2", [P, NT])
        xn = sb("xn2", [P, NT, D])
        xm = sb("xm2", [P, NT, D])
        h = sb("h2", [P, NT, D])
        gh = sb("gh", [P, NT, D])
        ggh = sb("ggh", [P, NT, D])
        act1 = sb("router_act", [P, S])
        TILES = B * NT
        wide = [P, TILES, NE]
        order = sb("order", [P, NE])
        cand = sb("cand", wide)
        left = sb("left", wide)
        chosen = [sb(f"chosen{i}", wide) for i in range(2)]
        top = [sb(f"top{i}", [P, TILES]) for i in range(2)]
        first = sb("first", [P, TILES])
        gap, e_gap = sb("gap", [P, TILES]), sb("e_gap", [P, TILES])
        w = [sb(f"weight{i}", [P, TILES]) for i in range(2)]
        ps = [ctx.enter_context(nc.psum_tensor(f"route{i}", [P, 2 * BANK], F32)) for i in range(4)]
        ps_t, ps_o, ps_r, ps_l = ps

        consts_in = sem("route_consts_in")
        ctx_s_ready = sem("ctx_s_ready")
        turned = sem("route_turned")
        copied = sem("route_copied")
        attn_ready = sem("attn_ready")
        dve_done = sem("route_dve_done")
        pool_done = sem("route_pool_done")
        var_ready = sem("var2_ready")
        scale_ready = sem("scale2_ready")
        xn_ready = sem("xn2_ready")
        h_ready = sem("h2_ready")
        x_updated = sem("x_updated")
        router_ps_ready = sem("router_ps_ready")
        router_act_ready = sem("router_act_ready")
        logits_ps_ready = sem("logits_ps_ready")
        order_ready = sem("order_ready")
        gap_ready = sem("gap_ready")
        e_gap_ready = sem("e_gap_ready")
        block = ctx.enter_context(nc.Block())
        loads = [(wo, t["wo_t"]), (rw1, t["rw1"]), (rw2, t["rw2"]), (rb1, t["rb1"]),
                 (rb2, t["rb2"].to_broadcast([P, NE]))]

        @block.sync
        def _(sp):
            for dst, src in loads:
                sp.dma_start(dst[:], src).then_inc(consts_in, 16)

        @block.gpsimd
        def _(pool):
            for i in range(NE):
                ins = pool.memset(order[:, i:i + 1], float(NE - i))
            ins.then_inc(order_ready, 1)
            own, var, normed = Count(), Count(), Count()
            shape = [P, NT, D]
            with pool.Fori(0, B) as b:
                def mod(i):
                    return k["mod"][:, b, i, :].unsqueeze(1).to_broadcast(shape)

                pool.wait_ge(var_ready, var.more())
                pool.tensor_tensor(scale[:], var_eps[:], k["rsqrt_exp"][:], ALU.pow).then_inc(scale_ready, 1)
                pool.wait_ge(xn_ready, normed.more())
                pool.tensor_tensor(xm[:], xn[:], mod(4), ALU.mult).then_inc(pool_done, 1)
                pool.wait_ge(pool_done, own.more())
                pool.tensor_tensor(h[:], xm[:], mod(3), ALU.add).then_inc(h_ready, 1)
                pool.tensor_tensor(gh[:], xm[:], mod(3), ALU.add).then_inc(pool_done, 1)
                pool.wait_ge(pool_done, own.more())
                pool.tensor_tensor(ggh[:], gh[:], mod(5), ALU.mult).then_inc(pool_done, 1)
                pool.wait_ge(pool_done, own.more())
                pool.tensor_tensor(k["x"][:, b], k["x"][:, b], ggh[:], ALU.add).then_inc(x_updated, 1)
                pool.sem_inc(pool_done, own.back(3))
                pool.sem_inc(var_ready, var.back(1))
                pool.sem_inc(xn_ready, normed.back(1))

        @block.scalar
        def _(act):
            act.wait_ge(consts_in, 16 * len(loads))
            turns, routed = Count(), Count()
            ctx_of = k["ctx"].rearrange("p (b g) t f -> p b t g f", b=B)
            with act.Fori(0, B) as b:
                act.copy(ctx_s[:], ctx_of[:, b]).then_inc(ctx_s_ready, 1)
                for c in range(2):
                    act.wait_ge(turned, turns.more())
                    act.copy(ctx_t[:, c * BANK:(c + 1) * BANK], ps_t[:, c * BANK:(c + 1) * BANK]).then_inc(copied, 1)
                for c in range(2):
                    act.wait_ge(turned, turns.more())
                    act.copy(k["h_t"][:, b, c * BANK:(c + 1) * BANK],
                             ps_t[:, c * BANK:(c + 1) * BANK]).then_inc(copied, 1)
                for c in range(2):
                    act.wait_ge(router_ps_ready, routed.more())
                    act.activation(act1[:, c * BANK:(c + 1) * BANK], ps_r[:, c * BANK:(c + 1) * BANK], ACT.Silu,
                                   bias=rb1[:]).then_inc(router_act_ready, 1)
                act.sem_inc(turned, turns.back(4))
                act.sem_inc(router_ps_ready, routed.back(2))
            act.wait_ge(gap_ready, 1)
            act.activation(e_gap[:], gap[:], ACT.Exp).then_inc(e_gap_ready, 1)

        @block.vector
        def _(dve):
            dve.wait_ge(consts_in, 16 * len(loads))
            own, scaled = Count(), Count()
            attn, logits = Count(), Count()
            updated = Count()

            def link(ins):
                ins.then_inc(dve_done, 1)
                dve.wait_ge(dve_done, own.more())

            with dve.Fori(0, B) as b:
                dve.wait_ge(attn_ready, attn.more())
                link(dve.tensor_tensor(gated[:], ps_o[:].rearrange("p (t d) -> p t d", d=D),
                                       k["mod"][:, b, 2, :].unsqueeze(1).to_broadcast([P, NT, D]), ALU.mult))
                link(dve.tensor_tensor(k["x"][:, b], k["x"][:, b], gated[:], ALU.add))
                for i in range(NT):
                    dve.bn_stats(stats[:, i, :], k["x"][:, b, i, :]).then_inc(dve_done, 1)
                dve.wait_ge(dve_done, own.more(NT))
                for i in range(NT):
                    dve.bn_aggr(mean_var[:, i, :], stats[:, i, :]).then_inc(dve_done, 1)
                dve.wait_ge(dve_done, own.more(NT))
                dve.tensor_scalar(var_eps[:], mean_var[:, :, 1], EPS, None, ALU.add).then_inc(var_ready, 1)
                dve.wait_ge(scale_ready, scaled.more())
                for i in range(NT):
                    ins = dve.tensor_scalar(xn[:, i, :], k["x"][:, b, i, :], mean_var[:, i, 0:1],
                                            scale[:, i:i + 1], ALU.subtract, ALU.mult)
                ins.then_inc(xn_ready, 1)
                dve.wait_ge(logits_ps_ready, logits.more())
                dve.tensor_tensor(k["logits"][:, b], ps_l[:, 0:NT * NE].rearrange("p (t e) -> p t e", e=NE),
                                  rb2[:].unsqueeze(1).to_broadcast([P, NT, NE]), ALU.add).then_inc(dve_done, 1)
                dve.wait_ge(dve_done, own.more())
                dve.wait_ge(x_updated, updated.more())
                dve.sem_inc(dve_done, own.back(2 * NT + 3))
                dve.sem_inc(scale_ready, scaled.back(1))
                dve.sem_inc(attn_ready, attn.back(1))
                dve.sem_inc(logits_ps_ready, logits.back(1))
                dve.sem_inc(x_updated, updated.back(1))
            dve.wait_ge(order_ready, 1)
            logit = k["logits"][:].rearrange("p b t e -> p (b t) e")

            def over(v):
                return v[:].unsqueeze(2).to_broadcast(wide)

            for n in range(2):
                of = logit if n == 0 else left[:]
                link(dve.tensor_reduce(top[n][:], of, axis=AX.X, op=ALU.max))
                link(dve.tensor_tensor(cand[:], of, over(top[n]), ALU.is_equal))
                link(dve.tensor_tensor(cand[:], cand[:], order[:].unsqueeze(1).to_broadcast(wide), ALU.mult))
                link(dve.tensor_reduce(first[:], cand[:], axis=AX.X, op=ALU.max))
                link(dve.tensor_tensor(chosen[n][:], cand[:], over(first), ALU.is_equal))
                if n == 0:
                    link(dve.scalar_tensor_tensor(out=left[:], in0=chosen[0][:], scalar=-3e38, in1=logit,
                                                  op0=ALU.mult, op1=ALU.add))
            dve.tensor_tensor(gap[:], top[1][:], top[0][:], ALU.subtract).then_inc(gap_ready, 1)
            dve.wait_ge(e_gap_ready, 1)
            link(dve.tensor_scalar(first[:], e_gap[:], 1.0, None, ALU.add))
            link(dve.reciprocal(w[0][:], first[:]))
            link(dve.tensor_tensor(w[1][:], e_gap[:], w[0][:], ALU.mult))
            for n in range(2):
                link(dve.tensor_tensor(chosen[n][:], chosen[n][:], over(w[n]), ALU.mult))
            dve.tensor_tensor(k["weight"][:].rearrange("p b t e -> p (b t) e"), chosen[0][:], chosen[1][:], ALU.add)

        @block.tensor
        def _(pe):
            pe.wait_ge(consts_in, 16 * len(loads))
            staged, copies = Count(), Count()
            h_in, acts = Count(), Count()
            with pe.Fori(0, B) as b:
                def turn(src):
                    for i in range(NT):
                        ins = pe.transpose(ps_t[:, i * P:(i + 1) * P], src[:, i], k["ident"][:])
                        if i % 4 == 3:
                            ins.then_inc(turned, 1)

                pe.wait_ge(ctx_s_ready, staged.more())
                turn(ctx_s[:].rearrange("p t g f -> p t (g f)"))
                pe.wait_ge(copied, copies.more(2))
                for i in range(NT):
                    ins = pe.matmul(ps_o[:, i * P:(i + 1) * P], ctx_t[:, i * P:(i + 1) * P], wo[:],
                                    start=True, stop=True)
                ins.then_inc(attn_ready, 1)
                pe.wait_ge(h_ready, h_in.more())
                turn(h[:])
                pe.wait_ge(copied, copies.more(2))
                for c in range(2):
                    pe.matmul(ps_r[:, c * BANK:(c + 1) * BANK], rw1[:], k["h_t"][:, b, c * BANK:(c + 1) * BANK],
                              start=True, stop=True).then_inc(router_ps_ready, 1)
                for i in range(NT):
                    if i % 4 == 0:
                        pe.wait_ge(router_act_ready, acts.more())
                    ins = pe.matmul(ps_l[:, i * NE:(i + 1) * NE], act1[:, i * P:(i + 1) * P], rw2[:],
                                    start=True, stop=True)
                ins.then_inc(logits_ps_ready, 1)
                pe.sem_inc(ctx_s_ready, staged.back(1))
                pe.sem_inc(copied, copies.back(4))
                pe.sem_inc(h_ready, h_in.back(1))
                pe.sem_inc(router_act_ready, acts.back(2))


def experts(nc, t, k):
    with ExitStack() as ctx:
        def sb(name, shape, dt=F32):
            return ctx.enter_context(nc.sbuf_tensor(name, shape, dt))

        def sem(name):
            return ctx.enter_context(nc.semaphore(name))

        HC = HID // P
        TC = BANK // P
        w1, w2 = sb("w1", [P, NE, HID]), sb("w2", [P, NE, HC, D])
        b1, b2 = sb("b1", [P, NE, HC]), sb("b2", [NE, D])
        hid = [sb(f"hid{i}", [P, HC, BANK]) for i in range(2)]
        w_s = sb("w_s", [P, TC, NE])
        w_t = sb("w_t", [NE, BANK])
        part = sb("part", [P, TC, D])
        acc = sb("acc", [P, TC, D])
        ps_up = [ctx.enter_context(nc.psum_tensor(f"ps_up{i}", [P, BANK], F32)) for i in range(4)]
        ps_down = [ctx.enter_context(nc.psum_tensor(f"ps_down{i}", [P, BANK], F32)) for i in range(2)]
        ps_w = ctx.enter_context(nc.psum_tensor("ps_w", [NE, BANK], F32))
        ps_b = ctx.enter_context(nc.psum_tensor("ps_b", [P, BANK], F32))

        consts_in = sem("expert_consts_in")
        w_s_ready = sem("w_s_ready")
        w_turned = sem("w_turned")
        w_t_ready = sem("w_t_ready")
        bias_ready = sem("bias_ready")
        up_ready = sem("up_ready")
        hid_ready = sem("hid_ready")
        down_ready = sem("down_ready")
        down_taken = sem("down_taken")
        dve_done = sem("expert_dve_done")
        chunk_done = sem("chunk_done")
        stored = sem("out_stored")
        block = ctx.enter_context(nc.Block())
        loads = [(w1, t["we1"].rearrange("e d h -> d e h")), (w2, t["we2"].rearrange("e (c p) d -> p e c d", p=P)),
                 (b1, t["be1"]), (b2, t["be2"])]

        @block.sync
        def _(sp):
            for dst, src in loads:
                sp.dma_start(dst[:], src).then_inc(consts_in, 16)
            done = Count()
            out = t["out"].rearrange("b (t p) d -> b p t d", p=P)
            with sp.Fori(0, B) as b:
                sp.wait_ge(chunk_done, done.more(2))
                sp.dma_start(out[b], k["x"][:, b]).then_inc(stored, 16)
                sp.sem_inc(chunk_done, done.back(2))
            sp.wait_ge(stored, 16 * B)

        @block.scalar
        def _(act):
            act.wait_ge(consts_in, 16 * len(loads))
            ups, turns = Count(), Count()
            with act.Fori(0, B) as b:
                for half in range(2):
                    act.copy(w_s[:], k["weight"][:, b, half * TC:(half + 1) * TC, :]).then_inc(w_s_ready, 1)
                    act.wait_ge(w_turned, turns.more())
                    act.copy(w_t[:], ps_w[:]).then_inc(w_t_ready, 1)
                    for e in range(NE):
                        for c in range(HC):
                            act.wait_ge(up_ready, ups.more())
                            act.activation(hid[e % 2][:, c, :], ps_up[c][:], ACT.Silu,
                                           bias=b1[:, e, c:c + 1]).then_inc(hid_ready, 1)
                act.sem_inc(up_ready, ups.back(2 * NE * HC))
                act.sem_inc(w_turned, turns.back(2))

        @block.vector
        def _(dve):
            own, downs, biases = Count(), Count(), Count()

            def link(ins):
                ins.then_inc(dve_done, 1)
                dve.wait_ge(dve_done, own.more())

            with dve.Fori(0, B) as b:
                for half in range(2):
                    rows = slice(half * TC, (half + 1) * TC)
                    dve.wait_ge(bias_ready, biases.more())
                    link(dve.tensor_copy(acc[:].rearrange("p t d -> p (t d)"), ps_b[:]))
                    for e in range(NE):
                        dve.wait_ge(down_ready, downs.more())
                        weight = k["weight"][:, b, rows, e:e + 1].to_broadcast([P, TC, D])
                        dve.tensor_tensor(part[:], ps_down[e % 2][:].rearrange("p (t d) -> p t d", d=D), weight,
                                          ALU.mult).then_inc(down_taken, 1)
                        dve.drain().then_inc(dve_done, 1)
                        dve.wait_ge(dve_done, own.more())
                        link(dve.tensor_tensor(acc[:], acc[:], part[:], ALU.add))
                    gate = k["mod"][:, b, 5, :].unsqueeze(1).to_broadcast([P, TC, D])
                    link(dve.tensor_tensor(part[:], acc[:], gate, ALU.mult))
                    dve.tensor_tensor(k["x"][:, b, rows], k["x"][:, b, rows], part[:], ALU.add).then_inc(chunk_done, 1)
                dve.sem_inc(dve_done, own.back(2 * (2 + 2 * NE)))
                dve.sem_inc(down_ready, downs.back(2 * NE))
                dve.sem_inc(bias_ready, biases.back(2))

        @block.tensor
        def _(pe):
            pe.wait_ge(consts_in, 16 * len(loads))
            ws, wt, hids, taken = (Count() for _ in range(4))
            pe.sem_inc(down_taken, 2)
            with pe.Fori(0, B) as b:
                for half in range(2):
                    pe.wait_ge(w_s_ready, ws.more())
                    for i in range(TC):
                        ins = pe.transpose(ps_w[:, i * P:(i + 1) * P], w_s[:, i, :], k["ident"][:])
                    ins.then_inc(w_turned, 1)
                    pe.wait_ge(w_t_ready, wt.more())
                    for i in range(TC):
                        ins = pe.matmul(ps_b[:, i * P:(i + 1) * P], w_t[:, i * P:(i + 1) * P], b2[:],
                                        start=True, stop=True)
                    ins.then_inc(bias_ready, 1)

                    def up(e):
                        for c in range(HC):
                            pe.matmul(ps_up[c][:], w1[:, e, c * P:(c + 1) * P],
                                      k["h_t"][:, b, half * BANK:(half + 1) * BANK],
                                      start=True, stop=True).then_inc(up_ready, 1)

                    up(0)
                    for e in range(NE):
                        pe.wait_ge(hid_ready, hids.more(HC))
                        if e + 1 < NE:
                            up(e + 1)
                        pe.wait_ge(down_taken, taken.more())
                        for i in range(TC):
                            for c in range(HC):
                                ins = pe.matmul(ps_down[e % 2][:, i * P:(i + 1) * P],
                                                hid[e % 2][:, c, i * P:(i + 1) * P], w2[:, e, c, :],
                                                start=c == 0, stop=c == HC - 1)
                        ins.then_inc(down_ready, 1)
                pe.sem_inc(w_s_ready, ws.back(2))
                pe.sem_inc(w_t_ready, wt.back(2))
                pe.sem_inc(hid_ready, hids.back(2 * NE * HC))
                pe.sem_inc(down_taken, taken.back(2 * NE))


def head_order():
    order, angle, is_sin = [], [], []
    for g in range(GROUPS):
        for r in range(2):
            for f in range(HD):
                for u in range(2):
                    order.append((GH * g + 2 * u + r) * HD + f // 2 * 2)
                    angle.append(f // 2)
                    is_sin.append(f % 2)
    return np.array(order), np.array(angle), np.array(is_sin)


def rope_table():
    _, angle, is_sin = head_order()
    freqs = np.exp(np.arange(0, HD, 2, dtype=np.float32) * np.float32(-np.log(10000.0) / HD)).astype(np.float32)
    angles = (np.arange(S, dtype=np.float32)[None, :] * freqs[angle][:, None]).astype(np.float32).astype(np.float64)
    return np.where(is_sin[:, None] == 1, -np.sin(angles), np.cos(angles)).astype(np.float32)


def kernel(**inputs):
    from concourse import bacc
    from concourse.bass_utils import run_bass_kernel_spmd

    i = {name.removeprefix("L0_"): np.asarray(a) for name, a in inputs.items()}
    order, _, _ = head_order()
    arrays = {
        "x": i["attn_x"], "c_t": i["c"].T, "wmod": i["wmod"],
        "wq_t": i["attn_Wq"][order].T, "wk_t": i["attn_Wk"][order].T, "wv_t": i["attn_Wv"].T,
        "wo_t": i["attn_Wo"].T, "rope": rope_table(),
        "rw1": i["ffn_rw1"], "rb1": i["ffn_rb1"][:, None], "rw2": i["ffn_rw2"], "rb2": i["ffn_rb2"][None, :],
        "we1": i["ffn_we1"], "we2": i["ffn_we2"],
        "be1": i["ffn_be1"].reshape(NE, HID // P, P).transpose(2, 0, 1), "be2": i["ffn_be2"],
    }
    arrays = {name: np.ascontiguousarray(a) for name, a in arrays.items()}
    nc = bacc.Bacc("TRN2", target_bir_lowering=False, num_devices=1)
    t = {name: nc.dram_tensor(f"in_{name}", a.shape, F32, kind="ExternalInput").ap() for name, a in arrays.items()}
    t["out"] = nc.dram_tensor("out", (B, S, D), F32, kind="ExternalOutput").ap()
    build(nc, t)
    return run_bass_kernel_spmd(nc, [{f"in_{name}": a for name, a in arrays.items()}], core_ids=[0]).results[0]["out"]
```

```python
from contextlib import ExitStack

import concourse.bass as bass
import concourse.mybir as mybir
import numpy as np

F32 = mybir.dt.float32
BF16 = mybir.dt.bfloat16
I32 = mybir.dt.int32
ALU = mybir.AluOpType
ACT = mybir.ActivationFunctionType
AX = mybir.AxisListType

P = 128
B, S, D = 4, 1024, 128
HEADS, HD = 16, 8
NE, HID = 8, 512
NT = S // P
GH = 4
GROUPS = HEADS // GH
NG = B * GROUPS
GF = GH * HD
EPS = 1e-5
BANK = 512

TERMS = ((0, 0), (0, 1), (1, 0), (1, 1), (0, 2), (2, 0))
HALF_ROWS = 3 * HD
MAX_ROW = HALF_ROWS

STEPS = 16
PAIR = 2 * STEPS
LEAD = 8
UNITS = GH * NT
RING = 4

HC = HID // P
QUAD = 4
TILES_B = -(-(2 * S // P + NE - 1) // QUAD) * QUAD
QUADS = TILES_B // QUAD
SLOTS_B = TILES_B * P
WRING = 4
assert TILES_B % WRING == 0 and QUADS % 2 == 0
AT_CTX, AT_H, AT_ROUTER, AT_COUNT = 0, 6, 7, 12


class Count:

    def __init__(self):
        self.seen = 0

    def at(self, n):
        self.seen = max(self.seen, n)
        return n

    def more(self, n=1):
        return self.at(self.seen + n)

    def back(self, n=None):
        n = self.seen if n is None else n
        self.seen -= n
        return -n


def build(nc, t):
    with ExitStack() as ctx:
        def sb(name, shape, dt=F32):
            return ctx.enter_context(nc.sbuf_tensor(name, shape, dt))

        def scratch(name, shape, dt):
            return nc.dram_tensor(name, shape, dt, kind="Internal").ap()

        k = {
            "q_terms": scratch("q_terms", [NG, 2, len(TERMS) // 2, 2, HD, 2, S], BF16),
            "k_terms": scratch("k_terms", [NG, 2, len(TERMS) // 2, 2, HD, 2, S], BF16),
            "slots": scratch("slots", [B * SLOTS_B, D], F32),
            "y_slots": scratch("y_slots", [B * SLOTS_B, D], F32),
            "x": sb("x_sb", [P, B, NT, D]),
            "mod": sb("mod", [P, B, 6, D]),
            "ident": sb("ident", [P, P]),
            "ident16": sb("ident16", [P, P], BF16),
            "rsqrt_exp": sb("rsqrt_exp", [P, NT]),
            "v": sb("v", [P, NG, NT, GF]),
            "ctx": sb("ctx", [P, NG, NT, GF]),
        }
        with ExitStack() as operands:
            for name, blocks in (("q_max", 2), ("q_exp", 2), ("k_max", GH), ("k_exp", GH)):
                k[name] = [operands.enter_context(nc.sbuf_tensor(f"{name}{i}", [P, blocks, S], BF16))
                           for i in range(2)]
            k["v_grp"] = [operands.enter_context(nc.sbuf_tensor(f"v_grp{i}", [P, NT, GH, 32], F32))
                          for i in range(2)]
            prepare(nc, t, k)
            attend(nc, t, k)
        mix(nc, t, k)


def prepare(nc, t, k):
    with ExitStack() as ctx:
        def sb(name, shape, dt=F32):
            return ctx.enter_context(nc.sbuf_tensor(name, shape, dt))

        def sem(name):
            return ctx.enter_context(nc.semaphore(name))

        c_t = sb("c_t", [P, B])
        silu_c = sb("silu_c", [P, B])
        silu_cb = sb("silu_cb", [P, B, P])
        wmod = sb("wmod", [P, 6 * D])
        wq, wk, wv = sb("wq", [P, D]), sb("wk", [P, D]), sb("wv", [P, D])
        rope = sb("rope", [P, S])
        g_sign = sb("g_sign", [P, B * 2, D])
        g_size = sb("g_size", [P, B * 2, D])
        stats = sb("stats", [P, NT, 6])
        mean_var = sb("mean_var", [P, NT, 2])
        var_eps = sb("var_eps", [P, NT])
        scale = sb("scale", [P, NT])
        xn = sb("xn", [P, NT, D])
        xm = sb("xm", [P, NT, D])
        h = sb("h", [P, NT, D])
        h_t = sb("h_t1", [P, S])
        rot = [sb(f"rot{i}", [P, S]) for i in range(2)]
        rest = [sb(f"rest{i}", [P, S]) for i in range(2)]
        parts = [sb(f"parts{i}", [P, 3, S], BF16) for i in range(2)]
        CLEAR = 8
        CLEARS = B * SLOTS_B // (P * CLEAR)
        zero_rows = sb("zero_rows", [P, CLEAR * D])
        ps = [ctx.enter_context(nc.psum_tensor(f"prep{i}", [P, 2 * BANK], F32)) for i in range(4)]
        ps_t, ps_q, ps_k, ps_v = ps

        consts_in = sem("consts_in")
        x_in = sem("x_in")
        ident_ready = sem("ident_ready")
        silu_c_ready = sem("silu_c_ready")
        zero_rows_ready = sem("zero_rows_ready")
        slots_cleared = sem("slots_cleared")
        zeros_ready = sem("zeros_ready")
        silu_cb_ready = sem("silu_cb_ready")
        mod_ps_ready = sem("mod_ps_ready")
        mod_ready = sem("mod_ready")
        dve_done = sem("prep_dve_done")
        pool_done = sem("prep_pool_done")
        var_ready = sem("var_ready")
        scale_ready = sem("scale_ready")
        xn_ready = sem("xn_ready")
        h_ready = sem("h_ready")
        h_t_ps_ready = sem("h_t_ps_ready")
        h_t_ready = sem("h_t_ready")
        qk_ps_ready = sem("qk_ps_ready")
        v_ps_ready = sem("v_ps_ready")
        rot_ready = sem("rot_ready")
        part0_ready = sem("part0_ready")
        rest_ready = sem("rest_ready")
        part1_ready = sem("part1_ready")
        parts_ready = sem("parts_ready")
        parts_stored = sem("parts_stored")
        block = ctx.enter_context(nc.Block())

        loads = [(c_t, t["c_t"]), (wmod, t["wmod"]), (wq, t["wq_t"]), (wk, t["wk_t"]), (wv, t["wv_t"]),
                 (rope, t["rope"])]
        terms = [k[m].rearrange("(b g) h t r f u n -> b h t g (r f u) n", b=B) for m in ("q_terms", "k_terms")]

        @block.sync
        def _(sp):
            for dst, src in loads:
                sp.dma_start(dst[:], src).then_inc(consts_in, 16)
            sp.dma_start(k["x"][:], t["x"].rearrange("b (t p) d -> p b t d", p=P)).then_inc(x_in, 16)
            sp.wait_ge(zero_rows_ready, 1)
            for name in ("slots", "y_slots"):
                clear = k[name].rearrange("(n p r) d -> n p (r d)", p=P, r=CLEAR)
                for n in range(CLEARS):
                    sp.dma_start(clear[n], zero_rows[:]).then_inc(slots_cleared, 16)
            parts_of = Count()
            with sp.Fori(0, B) as b:
                for qk in range(2):
                    sp.wait_ge(parts_ready, parts_of.more())
                    for n, term in enumerate(TERMS):
                        sp.dma_start(terms[qk][b, n // 3, n % 3],
                                     parts[qk][:, term[qk], :]).then_inc(parts_stored, 16)
                sp.sem_inc(parts_ready, parts_of.back(2))
            sp.wait_ge(slots_cleared, 16 * 2 * CLEARS)

        @block.gpsimd
        def _(pool):
            own = Count()
            pool.memset(zero_rows[:], 0.0).then_inc(zero_rows_ready, 1)
            for i in range(2):
                for name in ("q_max", "q_exp", "k_max", "k_exp", "v_grp"):
                    pool.memset(k[name][i][:], 0.0).then_inc(zeros_ready, 1)
            pool.memset(k["rsqrt_exp"][:], -0.5).then_inc(pool_done, 1)
            pool.memset(k["ident"][:], 0.0).then_inc(pool_done, 1)
            pool.memset(k["ident16"][:], 0.0).then_inc(pool_done, 1)
            pool.wait_ge(pool_done, own.more(3))
            for m in ("ident", "ident16"):
                pool.affine_select(out=k[m][:], in_=k[m][:], compare_op=ALU.not_equal, fill=1.0, base=0,
                                   pattern=[[-1, P]], channel_multiplier=1).then_inc(ident_ready, 1)
            pool.sem_inc(pool_done, own.back())
            pool.wait_ge(mod_ready, 1)
            var, normed = Count(), Count()
            with pool.Fori(0, B) as b:
                pool.wait_ge(var_ready, var.more())
                pool.tensor_tensor(scale[:], var_eps[:], k["rsqrt_exp"][:], ALU.pow).then_inc(scale_ready, 1)
                pool.wait_ge(xn_ready, normed.more())
                shape = [P, NT, D]
                pool.tensor_tensor(xm[:], xn[:], k["mod"][:, b, 1, :].unsqueeze(1).to_broadcast(shape),
                                   ALU.mult).then_inc(pool_done, 1)
                pool.wait_ge(pool_done, own.more())
                pool.tensor_tensor(h[:], xm[:], k["mod"][:, b, 0, :].unsqueeze(1).to_broadcast(shape),
                                   ALU.add).then_inc(h_ready, 1)
                pool.sem_inc(var_ready, var.back(1))
                pool.sem_inc(xn_ready, normed.back(1))
                pool.sem_inc(pool_done, own.back(1))

        @block.scalar
        def _(act):
            act.wait_ge(consts_in, 16 * len(loads))
            act.activation(silu_c[:], c_t[:], ACT.Silu).then_inc(silu_c_ready, 1)
            h_t_ps, v_ps = Count(), Count()
            rotated, rests, stored = Count(), Count(), Count()
            act.sem_inc(parts_stored, 16 * 2 * len(TERMS))
            with act.Fori(0, B) as b:
                for c in range(2):
                    act.wait_ge(h_t_ps_ready, h_t_ps.more())
                    act.copy(h_t[:, c * BANK:(c + 1) * BANK],
                             ps_t[:, c * BANK:(c + 1) * BANK]).then_inc(h_t_ready, 1)
                act.wait_ge(parts_stored, stored.more(16 * 2 * len(TERMS)))
                for qk in range(2):
                    act.wait_ge(rot_ready, rotated.more())
                    act.copy(parts[qk][:, 0, :], rot[qk][:]).then_inc(part0_ready, 1)
                for qk in range(2):
                    act.wait_ge(rest_ready, rests.more())
                    act.copy(parts[qk][:, 1, :], rest[qk][:]).then_inc(part1_ready, 1)
                act.wait_ge(v_ps_ready, v_ps.more())
                v_of = k["v"].rearrange("p (b g) t f -> p b g t f", b=B)
                act.copy(v_of[:, b], ps_v[:].rearrange("p (t g f) -> p g t f", t=NT, g=GROUPS))
                act.sem_inc(h_t_ps_ready, h_t_ps.back(2))
                act.sem_inc(parts_stored, stored.back(16 * 2 * len(TERMS)))
                act.sem_inc(rot_ready, rotated.back(2))
                act.sem_inc(rest_ready, rests.back(2))
                act.sem_inc(v_ps_ready, v_ps.back(1))
            act.wait_ge(parts_stored, stored.more(16 * 2 * len(TERMS)))

        @block.vector
        def _(dve):
            own = Count()

            def link(ins):
                ins.then_inc(dve_done, 1)
                dve.wait_ge(dve_done, own.more())

            dve.wait_ge(silu_c_ready, 1)
            dve.tensor_copy(silu_cb[:], silu_c[:].unsqueeze(2).to_broadcast([P, B, P])).then_inc(silu_cb_ready, 1)
            mod = k["mod"][:].rearrange("p b s d -> p (b s d)")
            for b in range(B):
                dve.wait_ge(mod_ps_ready, b + 1)
                for half in range(2):
                    at = (2 * b + half) * 3 * D
                    dve.tensor_copy(mod[:, at:at + 3 * D],
                                    ps[b][:, half * BANK:half * BANK + 3 * D]).then_inc(dve_done, 1)
            dve.wait_ge(dve_done, own.more(2 * B))
            trio = k["mod"][:].rearrange("p b (u s) d -> p (b u) s d", u=2)
            gate, one_c = trio[:, :, 2, :], trio[:, :, 1, :]
            link(dve.tensor_scalar(g_sign[:], gate, 0.0, 2.0, ALU.is_ge, ALU.mult))
            link(dve.scalar_tensor_tensor(out=g_size[:], in0=gate, scalar=-1.0, in1=gate, op0=ALU.mult, op1=ALU.max))
            link(dve.tensor_scalar(g_size[:], g_size[:], 0.25, None, ALU.max))
            link(dve.tensor_scalar(one_c, one_c, 1.0, None, ALU.add))
            dve.scalar_tensor_tensor(out=gate, in0=g_sign[:], scalar=-1.0, in1=g_size[:], op0=ALU.add,
                                     op1=ALU.mult).then_inc(mod_ready, 1)
            dve.sem_inc(dve_done, own.back())
            dve.wait_ge(zeros_ready, 10)
            for i in range(2):
                dve.memset(k["v_grp"][i][:, :, :, HD:HD + 1], 1.0)
                for r in range(2):
                    dve.memset(k["k_exp"][i][64 * r:64 * r + 32, 2 * r:2 * r + 2, :], 1.0)
            dve.wait_ge(x_in, 16)
            dve.wait_ge(consts_in, 16 * len(loads))
            scaled, qk_ps = Count(), Count()
            part0, part1 = Count(), Count()
            with dve.Fori(0, B) as b:
                for i in range(NT):
                    dve.bn_stats(stats[:, i, :], k["x"][:, b, i, :]).then_inc(dve_done, 1)
                dve.wait_ge(dve_done, own.more(NT))
                for i in range(NT):
                    dve.bn_aggr(mean_var[:, i, :], stats[:, i, :]).then_inc(dve_done, 1)
                dve.wait_ge(dve_done, own.more(NT))
                dve.tensor_scalar(var_eps[:], mean_var[:, :, 1], EPS, None, ALU.add).then_inc(var_ready, 1)
                dve.wait_ge(scale_ready, scaled.more())
                for i in range(NT):
                    ins = dve.tensor_scalar(xn[:, i, :], k["x"][:, b, i, :], mean_var[:, i, 0:1],
                                            scale[:, i:i + 1], ALU.subtract, ALU.mult)
                ins.then_inc(xn_ready, 1)
                for qk in range(2):
                    dve.wait_ge(qk_ps_ready, qk_ps.more())
                    dve.tensor_tensor(rot[qk][:], ps[1 + qk][:], rope[:], ALU.mult).then_inc(rot_ready, 1)
                for qk in range(2):
                    dve.wait_ge(part0_ready, part0.more())
                    dve.tensor_tensor(rest[qk][:], rot[qk][:], parts[qk][:, 0, :],
                                      ALU.subtract).then_inc(rest_ready, 1)
                for qk in range(2):
                    dve.wait_ge(part1_ready, part1.more())
                    dve.tensor_tensor(parts[qk][:, 2, :], rest[qk][:], parts[qk][:, 1, :],
                                      ALU.subtract).then_inc(parts_ready, 1)
                dve.sem_inc(dve_done, own.back(2 * NT))
                dve.sem_inc(scale_ready, scaled.back(1))
                dve.sem_inc(qk_ps_ready, qk_ps.back(2))
                dve.sem_inc(part0_ready, part0.back(2))
                dve.sem_inc(part1_ready, part1.back(2))

        @block.tensor
        def _(pe):
            pe.wait_ge(silu_cb_ready, 1)
            pe.wait_ge(consts_in, 16 * len(loads))
            for b in range(B):
                for half in range(2):
                    ins = pe.matmul(ps[b][:, half * BANK:half * BANK + 3 * D], silu_cb[:, b, :],
                                    wmod[:, half * 3 * D:(half + 1) * 3 * D], start=True, stop=True)
                ins.then_inc(mod_ps_ready, 1)
            pe.wait_ge(ident_ready, 2)
            pe.wait_ge(mod_ready, 1)
            h_in, h_t_in = Count(), Count()
            with pe.Fori(0, B):
                pe.wait_ge(h_ready, h_in.more())
                for i in range(NT):
                    ins = pe.transpose(ps_t[:, i * P:(i + 1) * P], h[:, i, :], k["ident"][:])
                    if i % 4 == 3:
                        ins.then_inc(h_t_ps_ready, 1)
                pe.wait_ge(h_t_ready, h_t_in.more(2))
                for w, out in ((wq, ps_q), (wk, ps_k)):
                    for c in range(2):
                        ins = pe.matmul(out[:, c * BANK:(c + 1) * BANK], w[:], h_t[:, c * BANK:(c + 1) * BANK],
                                        start=True, stop=True)
                    ins.then_inc(qk_ps_ready, 1)
                for i in range(NT):
                    ins = pe.matmul(ps_v[:, i * P:(i + 1) * P], h_t[:, i * P:(i + 1) * P], wv[:],
                                    start=True, stop=True)
                ins.then_inc(v_ps_ready, 1)
                pe.sem_inc(h_ready, h_in.back(1))
                pe.sem_inc(h_t_ready, h_t_in.back(2))


def attend(nc, t, k):
    with ExitStack() as ctx:
        def sb(name, shape, dt=F32):
            return ctx.enter_context(nc.sbuf_tensor(name, shape, dt))

        def psum(name, shape, dt=F32):
            return ctx.enter_context(nc.psum_tensor(name, shape, dt))

        def sem(name):
            return ctx.enter_context(nc.semaphore(name))

        q_max, k_max, q_exp, k_exp, v_grp = (k[name] for name in ("q_max", "k_max", "q_exp", "k_exp", "v_grp"))
        probs = sb("probs", [P, RING, GH, BANK])
        row_max = [sb(f"row_max{i}", [P, GH, NT]) for i in range(2)]
        neg_rest = sb("neg_rest", [P, GH, NT])
        neg_parts = [sb(f"neg_parts{i}", [P, GH, 3, NT], BF16) for i in range(2)]
        neg_rows = [sb(f"neg_rows{i}", [GH * 3 * NT, P], BF16) for i in range(2)]
        ctx_t = [sb(f"ctx_t{i}", [P, BANK]) for i in range(2)]
        inv_sum = sb("inv_sum", [P, 4 * GH])
        ps_max = [psum(f"ps_max{i}", [P, 2 * BANK]) for i in range(2)]
        ps_scores = [psum(f"ps_scores{i}", [P, BANK]) for i in range(2)]
        ps_ctx = psum("ps_ctx", [P, BANK])
        ps_turn = psum("ps_turn", [P, BANK])

        max_in = [sem(f"max_in{i}") for i in range(2)]
        exp_in = [sem(f"exp_in{i}") for i in range(2)]
        rows_in = [sem(f"rows_in{i}") for i in range(2)]
        v_ready = sem("v_ready")
        v_used = sem("v_used")
        exp_operands_used = sem("exp_operands_used")
        max_scores_ready = sem("max_scores_ready")
        max_taken = sem("max_taken")
        neg_step = sem("neg_step")
        neg_parts_ready = sem("neg_parts_ready")
        neg_turned = sem("neg_turned")
        neg_rows_ready = sem("neg_rows_ready")
        scores_ready = sem("scores_ready")
        probs_ready = sem("probs_ready")
        ctx_added = sem("ctx_added")
        ctx_t_ready = sem("ctx_t_ready")
        ctx_turned = sem("ctx_turned")
        sums_inverted = sem("sums_inverted")
        ctx_ready = sem("ctx_ready")
        block = ctx.enter_context(nc.Block())

        SETS = ((q_max, k_max, max_in), (q_exp, k_exp, exp_in))
        LOADS = 8
        PAIRS = NG // 2
        FIRST = 2

        def unit(n):
            n %= UNITS
            return 2 * (n // 2 % 2) + 1 - n % 2, n // 4

        def units(s):
            return (UNITS + LEAD + 2 * s, UNITS + LEAD + 2 * s + 1)

        def chain_step(s):
            after = s + LEAD // 2 + 1
            return after // STEPS if after % STEPS == 0 else None

        @block.sync
        def _(sp):
            def load(which, parity, group):
                q_of, k_of, loaded = SETS[which]
                for dst, src, blocks in ((q_of[parity], k["q_terms"], 1), (k_of[parity], k["k_terms"], 2)):
                    for r in range(2):
                        block = 2 * r * (blocks - 1)
                        for half in range(2):
                            row = 64 * r + 32 * half
                            sp.dma_start(dst[row:row + HALF_ROWS, block:block + 2, :],
                                         src[group, half, :, r].rearrange("t f u n -> t f (u n)")).then_inc(loaded[parity], 16)

            def negated_rows(parity):
                for head in range(GH):
                    row = 64 * (head % 2) + MAX_ROW
                    sp.dma_start(q_exp[parity][row:row + 3, head // 2, :],
                                 neg_rows[parity][head * 3 * NT:(head + 1) * 3 * NT, :]).then_inc(rows_in[parity], 16)

            rows, used = Count(), Count()
            for g in range(2):
                load(0, g, g)
                load(1, g, g)
            sp.wait_ge(neg_rows_ready, rows.more())
            negated_rows(0)
            load(0, 0, 2)
            sp.sem_inc(neg_rows_ready, rows.back())
            with sp.Fori(0, PAIRS - 1) as p:
                sp.wait_ge(neg_rows_ready, rows.more())
                negated_rows(1)
                load(0, 1, 2 * p + 3)
                sp.wait_ge(exp_operands_used, used.more())
                load(1, 0, 2 * p + 2)
                sp.wait_ge(neg_rows_ready, rows.more())
                negated_rows(0)
                load(0, 0, (2 * p + 4) % NG)
                sp.wait_ge(exp_operands_used, used.more())
                load(1, 1, 2 * p + 3)
                sp.sem_inc(neg_rows_ready, rows.back(2))
                sp.sem_inc(exp_operands_used, used.back(2))
            sp.wait_ge(neg_rows_ready, rows.more())
            negated_rows(1)

        @block.gpsimd
        def _(pool):
            def fill(parity, group):
                pool.tensor_copy(v_grp[parity][:, :, :, 0:HD].rearrange("p t h f -> p (t h) f"),
                                 k["v"][:, group].rearrange("p t (h f) -> p (t h) f", h=GH)).then_inc(v_ready, 1)

            for g in range(2):
                fill(g, g)
            used = Count()
            with pool.Fori(0, PAIRS - 1) as p:
                for g in range(2):
                    pool.wait_ge(v_used, used.more())
                    fill(g, 2 * p + 2 + g)
                pool.sem_inc(v_used, used.back(2))

        @block.tensor
        def _(pe):
            maxima_in = [Count(), Count()]
            exps_in = [Count(), Count()]
            rows = [Count(), Count()]
            taken, probs_in = Count(), Count()
            negs, v_in = Count(), Count()
            evacuated, normed = Count(), Count()

            def max_scores(n):
                head, tile = unit(n)
                g = n // UNITS
                if n % UNITS == 0:
                    pe.wait_ge(max_in[g % 2], maxima_in[g % 2].at(16 * LOADS * (g // 2 + 1)))
                if n >= 2:
                    pe.wait_ge(max_taken, taken.at(n - 1))
                r, u = head % 2, head // 2
                for c in range(2):
                    ins = pe.matmul(ps_max[n % 2][:, c * BANK:(c + 1) * BANK],
                                    q_max[g % 2][:, u, tile * P:(tile + 1) * P],
                                    k_max[g % 2][:, 2 * r + u, c * BANK:(c + 1) * BANK],
                                    start=True, stop=True)
                ins.then_inc(max_scores_ready, 1)

            def scores(s, place):
                head, g, c, tile = place, s // STEPS, s // NT % 2, s % NT
                if s % STEPS == 0 and place == 0:
                    pe.wait_ge(exp_in[g % 2], exps_in[g % 2].at(16 * LOADS * (g // 2 + 1)))
                    pe.wait_ge(rows_in[g % 2], rows[g % 2].at(16 * GH * (g // 2 + 1)))
                n = GH * s + place
                if n >= 2:
                    pe.wait_ge(probs_ready, probs_in.at(n - 1))
                r, u = head % 2, head // 2
                pe.matmul(ps_scores[n % 2][:], k_exp[g % 2][:, 2 * r + u, tile * P:(tile + 1) * P],
                          q_exp[g % 2][:, u, c * BANK:(c + 1) * BANK],
                          start=True, stop=True).then_inc(scores_ready, 1)

            def add_ctx(s, signal_v):
                g, tile = s // STEPS, s % NT
                pe.wait_ge(probs_ready, probs_in.at(GH * (s + 1)))
                if s % STEPS == 0:
                    pe.wait_ge(v_ready, v_in.at(g + 1))
                if tile == 0 and s:
                    pe.wait_ge(ctx_t_ready, evacuated.at(s // NT))
                for place in range(GH):
                    head = place
                    ins = pe.matmul(ps_ctx[32 * head:32 * head + 32, :], v_grp[g % 2][:, tile, head, :],
                                    probs[:, s % RING, head, :], start=tile == 0, stop=tile == NT - 1)
                    if place == 0 and s % STEPS == STEPS - 1:
                        ins.then_inc(exp_operands_used, 1)
                    if place == 0 and signal_v:
                        ins.then_inc(v_used, 1)
                ins.then_inc(ctx_added, 1)

            def turn_negated(g):
                pe.wait_ge(neg_parts_ready, negs.at(g + 1))
                pe.transpose(ps_turn[:].bitcast(BF16)[0:GH * 3 * NT, 0:P],
                             neg_parts[g % 2][:].rearrange("p h c t -> p (h c t)"),
                             k["ident16"][:]).then_inc(neg_turned, 1)

            def turn_ctx(chunk):
                pe.wait_ge(ctx_t_ready, evacuated.at(chunk + 1))
                pe.wait_ge(ctx_ready, normed.at(chunk + 1))
                for i in range(4):
                    ins = pe.transpose(ps_turn[:, i * P:(i + 1) * P], ctx_t[chunk % 2][:, i * P:(i + 1) * P],
                                       k["ident"][:])
                ins.then_inc(ctx_turned, 1)

            def step(s, last=False, signal_v=False):
                more_scores = not (last and s == PAIR - 1)
                more_units = not (last and units(s)[0] >= 2 * UNITS)
                if more_scores:
                    scores(s + 1, 0)
                    scores(s + 1, 1)
                add_ctx(s, signal_v)
                if more_scores:
                    scores(s + 1, 2)
                    scores(s + 1, 3)
                if more_units:
                    max_scores(units(s)[0])
                    max_scores(units(s)[1])
                if s % NT == 0 and s:
                    turn_ctx(s // NT - 1)
                if (g := chain_step(s - 1)) is not None and not (last and g == 2):
                    pe.wait_ge(ctx_ready, normed.at(s // NT + 1))
                    turn_negated(g)

            pe.sem_inc(ctx_ready, 1)
            for n in range(UNITS):
                max_scores(n)
            turn_negated(0)
            for n in range(UNITS, UNITS + LEAD):
                max_scores(n)
            for place in range(GH):
                scores(0, place)
            for s in range(FIRST):
                step(s)
            with pe.Fori(0, PAIRS - 1):
                for s in range(FIRST, FIRST + PAIR):
                    step(s, signal_v=s % STEPS == 0)
                pe.sem_inc(max_taken, taken.back(2 * UNITS))
                pe.sem_inc(probs_ready, probs_in.back(GH * PAIR))
                pe.sem_inc(neg_parts_ready, negs.back(2))
                pe.sem_inc(v_ready, v_in.back(2))
                pe.sem_inc(ctx_t_ready, evacuated.back(4))
                pe.sem_inc(ctx_ready, normed.back(4))
                for i in range(2):
                    pe.sem_inc(max_in[i], maxima_in[i].back(16 * LOADS))
                    pe.sem_inc(exp_in[i], exps_in[i].back(16 * LOADS))
                    pe.sem_inc(rows_in[i], rows[i].back(16 * GH))
            for s in range(FIRST, PAIR):
                step(s, last=True)
            turn_ctx(3)
            pe.wait_ge(max_in[0], maxima_in[0].more(16 * LOADS))

        @block.scalar
        def _(act):
            scores_in, added, turned = Count(), Count(), Count()

            def exps(s, evacuate=None):
                for place in range(GH):
                    if place == 2 and evacuate is not None:
                        copy_ctx(evacuate)
                    n = GH * s + place
                    act.wait_ge(scores_ready, scores_in.at(n + 1))
                    if s >= RING and place == 0:
                        act.wait_ge(ctx_added, added.at(s - RING + 1))
                    act.activation(probs[:, s % RING, place, :], ps_scores[n % 2][:], ACT.Exp,
                                   scale=float(HD) ** -0.5).then_inc(probs_ready, 1)

            def copy_ctx(chunk):
                act.wait_ge(ctx_added, added.at(NT * (chunk + 1)))
                act.copy(ctx_t[chunk % 2][:], ps_ctx[:]).then_inc(ctx_t_ready, 1)

            def copy_negated(g):
                act.wait_ge(neg_turned, turned.at(g + 1))
                act.copy(neg_rows[g % 2][:], ps_turn[:].bitcast(BF16)[0:GH * 3 * NT, 0:P]).then_inc(neg_rows_ready, 1)

            def step(s, last=False):
                if (g := chain_step(s - 2)) is not None and not (last and g == 2):
                    copy_negated(g)
                chunk = s // NT if s % NT == NT - 1 else None
                if last and s == PAIR - 1:
                    copy_ctx(chunk)
                else:
                    exps(s + 1, chunk)

            copy_negated(0)
            exps(0)
            for s in range(FIRST):
                step(s)
            with act.Fori(0, PAIRS - 1):
                for s in range(FIRST, FIRST + PAIR):
                    step(s)
                act.sem_inc(scores_ready, scores_in.back(GH * PAIR))
                act.sem_inc(ctx_added, added.back(PAIR))
                act.sem_inc(neg_turned, turned.back(2))
            for s in range(FIRST, PAIR):
                step(s, last=True)

        @block.vector
        def _(dve):
            scored, own = Count(), Count()
            turned, inverted = Count(), Count()

            def take_max(n):
                head, tile = unit(n)
                g = n // UNITS
                dve.wait_ge(max_scores_ready, scored.at(n + 1))
                dve.reduce_max(row_max[g % 2][:, head, tile:tile + 1], ps_max[n % 2][:],
                               axis=AX.X).then_inc(max_taken, 1)

            def split_negated(g):
                top, out = row_max[g % 2], neg_parts[g % 2]
                dve.drain().then_inc(neg_step, 1)
                dve.wait_ge(neg_step, own.more())
                dve.tensor_scalar(out[:, :, 0, :], top[:], -1.0, None, ALU.mult).then_inc(neg_step, 1)
                dve.wait_ge(neg_step, own.more())
                dve.scalar_tensor_tensor(out=neg_rest[:], in0=top[:], scalar=-1.0, in1=out[:, :, 0, :],
                                         op0=ALU.mult, op1=ALU.subtract).then_inc(neg_step, 1)
                dve.wait_ge(neg_step, own.more())
                dve.tensor_copy(out[:, :, 1, :], neg_rest[:]).then_inc(neg_step, 1)
                dve.wait_ge(neg_step, own.more())
                dve.tensor_tensor(out[:, :, 2, :], neg_rest[:], out[:, :, 1, :],
                                  ALU.subtract).then_inc(neg_parts_ready, 1)

            def norm_ctx(chunk, pair):
                dve.wait_ge(ctx_turned, turned.at(chunk + 1))
                view = ps_turn[:].rearrange("p (t c) -> p t c", c=32)
                dve.reciprocal(inv_sum[:], view[:, :, HD]).then_inc(sums_inverted, 1)
                dve.wait_ge(sums_inverted, inverted.more())
                out = k["ctx"][:, 2 * pair + chunk // 2].rearrange("p (c t) (h f) -> p c (t h) f", c=2, h=GH)
                dve.tensor_tensor(out[:, chunk % 2], view[:, :, 0:HD],
                                  inv_sum[:].unsqueeze(2).to_broadcast([P, 4 * GH, HD]),
                                  ALU.mult).then_inc(ctx_ready, 1)

            def step(s, pair, last=False):
                more_units = not (last and units(s)[0] >= 2 * UNITS)
                if more_units:
                    take_max(units(s)[0])
                if s % NT == 1 and s > NT:
                    norm_ctx(s // NT - 1, pair)
                if more_units:
                    take_max(units(s)[1])
                if (g := chain_step(s)) is not None and not (last and g == 2):
                    split_negated(g)

            for n in range(UNITS):
                take_max(n)
            split_negated(0)
            for n in range(UNITS, UNITS + LEAD):
                take_max(n)
            for s in range(FIRST):
                step(s, 0)
            dve.sem_inc(neg_step, own.back())
            with dve.Fori(0, PAIRS - 1) as p:
                for s in range(FIRST, FIRST + PAIR):
                    step(s, p)
                dve.sem_inc(max_scores_ready, scored.back(2 * UNITS))
                dve.sem_inc(neg_step, own.back(8))
                dve.sem_inc(ctx_turned, turned.back(4))
                dve.sem_inc(sums_inverted, inverted.back(4))
            for s in range(FIRST, PAIR):
                step(s, PAIRS - 1, last=True)
            norm_ctx(3, PAIRS - 1)


def mix(nc, t, k):
    with ExitStack() as ctx:
        def sb(name, shape, dt=F32):
            return ctx.enter_context(nc.sbuf_tensor(name, shape, dt))

        def psum(name, shape, dt=F32):
            return ctx.enter_context(nc.psum_tensor(name, shape, dt))

        def sem(name):
            return ctx.enter_context(nc.semaphore(name))

        W_UP, W_DOWN, W_B1, W_B2, W_END = 0, HID, 2 * HID, 2 * HID + HC, 2 * HID + HC + D
        w_all = sb("w_all", [P, NE, W_END])
        w_tile = [sb(f"w_tile{i}", [P, W_END]) for i in range(WRING)]
        slots_in = [sb(f"slots_in{i}", [P, QUAD, D]) for i in range(2)]
        slots_t = [sb(f"slots_t{i}", [P, P]) for i in range(2)]
        hid = [sb(f"hid{i}", [P, HC, P]) for i in range(2)]
        y = sb("y", [P, TILES_B, D])
        wo, rw1, rw2 = sb("wo", [P, D]), sb("rw1", [P, D]), sb("rw2", [P, NE])
        rb1, rb2 = sb("rb1", [P, 1]), sb("rb2", [P, NE])
        ctx_s = sb("ctx_s", [P, NT, GROUPS, GF])
        ctx_t = sb("ctx_t_all", [P, S])
        gated = sb("gated", [P, NT, D])
        stats, mean_var = sb("stats2", [P, NT, 6]), sb("mean_var2", [P, NT, 2])
        var_eps, scale = sb("var_eps2", [P, NT]), sb("scale2", [P, NT])
        xn, xm, h = (sb(name, [P, NT, D]) for name in ("xn2", "xm2", "h2"))
        gated_h = sb("gated_h", [P, NT, D])
        h_t, router_act = sb("h_t2", [P, S]), sb("router_act", [P, S])
        wide = [P, NT, NE]
        order = sb("order", [P, NE])
        lower = sb("lower", [P, NE, NE])
        tile_no = sb("tile_no", [P, TILES_B, NE])
        before = sb("before", [P, P])
        ones = sb("ones", [P, P])
        slot_base = sb("slot_base", [P, B, 1])
        logit, left = sb("logit", wide), sb("left", wide)
        cand, chosen = [sb(f"cand{i}", wide) for i in range(2)], [sb(f"chosen{i}", wide) for i in range(2)]
        both = sb("both", [P, NT + 1, NE])
        top = [sb(f"top{i}", [P, NT]) for i in range(2)]
        first = [sb(f"first{i}", [P, NT]) for i in range(2)]
        gap, tanh_gap = sb("gap", [P, NT]), sb("tanh_gap", [P, NT])
        weight = sb("weight", [P, B, 2, NT])
        tiles_i, tiles_s, tiles_f = sb("tiles_i", [P, NE], I32), sb("tiles_s", [P, NE], I32), sb("tiles_f", [P, NE])
        lower_tiles = sb("lower_tiles", [P, NE, NE])
        start, end, start_slot = sb("start", [P, NE]), sb("end", [P, NE]), sb("start_slot", [P, NE])
        place_all = sb("place_all", wide)
        place_of = [sb(f"place_of{i}", wide) for i in range(2)]
        place = sb("place", [P, 2, NT])
        slot = sb("slot", [P, B, 2, NT], I32)
        slot_now = sb("slot_now", [P, 2, NT], I32)
        slot_back = sb("slot_back", [P, 2, NT], I32)
        ended = sb("ended", [P, TILES_B, NE])
        expert_f, expert = sb("expert_f", [P, TILES_B]), sb("expert", [P, TILES_B], I32)
        rows = [sb(f"rows{i}", [P, NT, D]) for i in range(2)]
        scaled_rows = [sb(f"scaled_rows{i}", [P, NT, D]) for i in range(2)]
        mixed, mixed_g = sb("mixed", [P, NT, D]), sb("mixed_g", [P, NT, D])
        ps_t = [psum(f"ps_slots_t{i}", [P, BANK]) for i in range(2)]
        ps_up = [psum(f"ps_up{i}", [P, BANK]) for i in range(2)]
        ps_down = [psum(f"ps_down{i}", [P, BANK]) for i in range(2)]
        ps_r = psum("ps_route", [P, 2 * BANK])

        consts_in = sem("mix_consts_in")
        tables_ready = sem("tables_ready")
        scattered = sem("scattered")
        slots_loaded = [sem(f"slots_loaded{i}") for i in range(2)]
        slots_used = sem("slots_used")
        slots_turned = sem("slots_turned")
        slots_t_ready = sem("slots_t_ready")
        w_ready = sem("w_ready")
        up_ready = sem("up_ready")
        hid_ready = sem("hid_ready")
        down_ready = sem("down_ready")
        y_done = sem("y_done")
        last_bank_free = sem("last_bank_free")
        y_ready = sem("y_ready")
        y_stored = sem("y_stored")
        y_free = sem("y_free")
        y_landed = sem("y_landed")
        ctx_s_ready = sem("ctx_s_ready")
        turned = sem("route_turned")
        copied = sem("route_copied")
        attn_ready = sem("attn_ready")
        dve_done = sem("mix_dve_done")
        var_ready = sem("var2_ready")
        scale_ready = sem("scale2_ready")
        h_ready = sem("h2_ready")
        h_ready_pool = sem("h2_ready_pool")
        gated_h_ready = sem("gated_h_ready")
        x_updated = sem("x_updated")
        router_ps_ready = sem("router_ps_ready")
        router_act_ready = sem("router_act_ready")
        logits_ready = sem("logits_ready")
        both_ready = sem("both_ready")
        counts_ready = sem("counts_ready")
        gap_ready = sem("gap_ready")
        tanh_ready = sem("tanh_ready")
        slot_ready = sem("slot_ready")
        slot_now_ready = sem("slot_now_ready")
        slot_back_ready = sem("slot_back_ready")
        gathered = sem("gathered")
        out_ready = sem("out_ready")
        out_stored = sem("out_stored")
        block = ctx.enter_context(nc.Block())
        loads = [(wo[:], t["wo_t"]), (rw1[:], t["rw1"]), (rw2[:], t["rw2"]), (rb1[:], t["rb1"]),
                 (rb2[:], t["rb2"].to_broadcast([P, NE])), (before[:], t["before"]),
                 (w_all[:, :, W_UP:W_DOWN], t["we1"].rearrange("e d h -> d e h")),
                 (w_all[:, :, W_B1:W_B2], t["be1"])]
        loads += [(w_all[:, e, W_DOWN:W_B1].rearrange("p (c d) -> p c d", d=D),
                   t["we2"][e].rearrange("(c p) d -> p c d", p=P)) for e in range(NE)]
        loads += [(w_all[:, e, W_B2:W_END], t["be2"][e:e + 1, :].to_broadcast([P, D])) for e in range(NE)]
        NTABLES = 3 + NE + TILES_B + B + NE

        @block.sync
        def _(sp):
            for dst, src in loads:
                sp.dma_start(dst, src).then_inc(consts_in, 16)
            used, ready = Count(), Count()
            y_in, stored, outs = Count(), Count(), Count()
            quad_in = k["slots"].rearrange("(b q s p) d -> b q p s d", b=B, s=QUAD, p=P)
            quad_out = k["y_slots"].rearrange("(b q s p) d -> b q p s d", b=B, s=QUAD, p=P)
            out = t["out"].rearrange("b (t p) d -> b p t d", p=P)

            def body(b, combine):
                sp.wait_ge(scattered, 16 * 2 * NT * (b + 1))
                for q in range(QUADS):
                    sp.wait_ge(slots_used, used.more())
                    sp.dma_start(slots_in[q % 2][:], quad_in[b, q]).then_inc(slots_loaded[q % 2], 16)
                    if q:
                        sp.wait_ge(y_ready, ready.more())
                        sp.dma_start(quad_out[b, q - 1], y[:, QUAD * (q - 1):QUAD * q, :]).then_inc(y_stored, 16)
                    if combine and q == QUADS - 1:
                        sp.wait_ge(out_ready, outs.more())
                        sp.dma_start(out[b - 1], k["x"][:, b - 1]).then_inc(out_stored, 16)
                        sp.sem_inc(out_ready, outs.back())
                sp.wait_ge(y_ready, ready.more())
                sp.dma_start(quad_out[b, QUADS - 1], y[:, TILES_B - QUAD:TILES_B, :]).then_inc(y_stored, 16)
                sp.wait_ge(y_stored, stored.more(16 * QUADS))
                sp.sem_inc(y_free, 1)
                sp.sem_inc(y_landed, 1)
                sp.sem_inc(slots_used, used.back())
                sp.sem_inc(y_ready, ready.back())
                sp.sem_inc(y_stored, stored.back())

            sp.sem_inc(slots_used, 2)
            sp.sem_inc(y_free, 1)
            body(0, False)
            with sp.Fori(1, B) as b:
                body(b, True)
            sp.wait_ge(out_ready, outs.more())
            sp.dma_start(out[B - 1], k["x"][:, B - 1]).then_inc(out_stored, 16)
            sp.wait_ge(out_stored, 16 * B)

        @block.gpsimd
        def _(pool):
            pool.memset(ones[:], 1.0).then_inc(tables_ready, 1)
            pool.memset(both[:], 0.0).then_inc(tables_ready, 1)
            pool.memset(lower[:], 0.0).then_inc(tables_ready, 1)
            pool.wait_ge(tables_ready, 3)
            for e in range(NE):
                pool.memset(order[:, e:e + 1], float(NE - e)).then_inc(tables_ready, 1)
                pool.memset(lower[:, e, 0:max(e, 1)], float(e > 0)).then_inc(tables_ready, 1)
            for n in range(TILES_B):
                pool.memset(tile_no[:, n, :], float(n)).then_inc(tables_ready, 1)
            for b in range(B):
                pool.memset(slot_base[:, b, :], float(b * SLOTS_B)).then_inc(tables_ready, 1)
            var, h_in, slot_in = Count(), Count(), Count()
            now, back, landed, gated_in = Count(), Count(), Count(), Count()

            def route_scale():
                pool.wait_ge(var_ready, var.more())
                pool.tensor_tensor(scale[:], var_eps[:], k["rsqrt_exp"][:], ALU.pow).then_inc(scale_ready, 1)
                pool.sem_inc(var_ready, var.back())

            def route_scatter(b):
                pool.wait_ge(h_ready_pool, h_in.more())
                pool.tensor_tensor(gated_h[:], h[:], k["mod"][:, b, 5, :].unsqueeze(1).to_broadcast([P, NT, D]),
                                   ALU.mult).then_inc(gated_h_ready, 1)
                pool.wait_ge(gated_h_ready, gated_in.more())
                pool.tensor_tensor(k["x"][:, b], k["x"][:, b], gated_h[:], ALU.add).then_inc(x_updated, 1)
                pool.wait_ge(slot_ready, slot_in.more())
                pool.tensor_copy(slot_now[:], slot[:, b]).then_inc(slot_now_ready, 1)
                pool.wait_ge(slot_now_ready, now.more())
                for n in range(2):
                    for i in range(NT):
                        pool.indirect_dma_start(k["slots"], bass.IndirectOffsetOnAxis(slot_now[:, n, i:i + 1], axis=0),
                                                h[:, i, :], None).then_inc(scattered, 16)
                pool.sem_inc(h_ready_pool, h_in.back())
                pool.sem_inc(gated_h_ready, gated_in.back())
                pool.sem_inc(slot_ready, slot_in.back())
                pool.sem_inc(slot_now_ready, now.back())

            def combine_gather(b):
                pool.wait_ge(y_landed, landed.more())
                pool.tensor_copy(slot_back[:], slot[:, b]).then_inc(slot_back_ready, 1)
                pool.wait_ge(slot_back_ready, back.more())
                for n in range(2):
                    for i in range(NT):
                        pool.indirect_dma_start(rows[n][:, i, :], None, k["y_slots"],
                                                bass.IndirectOffsetOnAxis(slot_back[:, n, i:i + 1], axis=0)
                                                ).then_inc(gathered, 16)
                pool.sem_inc(slot_back_ready, back.back())
                pool.sem_inc(y_landed, landed.back())

            route_scale()
            route_scatter(0)
            route_scale()
            route_scatter(1)
            with pool.Fori(1, B - 1) as b:
                route_scale()
                combine_gather(b - 1)
                route_scatter(b + 1)
            combine_gather(B - 2)
            combine_gather(B - 1)

        @block.scalar
        def _(act):
            act.wait_ge(consts_in, 16 * len(loads))
            turns, routed, gaps = Count(), Count(), Count()
            slots, ups = Count(), Count()
            ctx_of = k["ctx"].rearrange("p (b g) t f -> p b t g f", b=B)

            def route_ctx(b):
                act.copy(ctx_s[:], ctx_of[:, b]).then_inc(ctx_s_ready, 1)

            def route_copy(dst):
                act.wait_ge(turned, turns.more())
                act.copy(dst[:], ps_r[:]).then_inc(copied, 1)

            def route_silu():
                act.wait_ge(router_ps_ready, routed.more())
                act.activation(router_act[:], ps_r[:], ACT.Silu, bias=rb1[:]).then_inc(router_act_ready, 1)

            def route_tanh():
                act.wait_ge(gap_ready, gaps.more())
                act.activation(tanh_gap[:], gap[:], ACT.Tanh, scale=0.5).then_inc(tanh_ready, 1)

            def finish():
                act.sem_inc(turned, turns.back())
                act.sem_inc(router_ps_ready, routed.back())
                act.sem_inc(gap_ready, gaps.back())

            def body(b, route):
                if route:
                    route_ctx(b + 1)
                for n in range(-2, TILES_B):
                    if n + 2 < TILES_B:
                        act.wait_ge(slots_turned, slots.more())
                        act.copy(slots_t[n % 2][:], ps_t[n % 2][:, 0:P]).then_inc(slots_t_ready, 1)
                    if 0 <= n + 1 < TILES_B:
                        act.wait_ge(up_ready, ups.more())
                        for c in range(HC):
                            ins = act.activation(hid[(n + 1) % 2][:, c, :], ps_up[(n + 1) % 2][:, c * P:(c + 1) * P],
                                                 ACT.Silu, bias=w_tile[(n + 1) % WRING][:, W_B1 + c:W_B1 + c + 1])
                        ins.then_inc(hid_ready, 1)
                    if route and n == AT_CTX:
                        route_copy(ctx_t)
                    if route and n == AT_H:
                        route_copy(h_t)
                    if route and n == AT_ROUTER:
                        route_silu()
                    if route and n == AT_COUNT:
                        route_tanh()
                act.sem_inc(slots_turned, slots.back())
                act.sem_inc(up_ready, ups.back())
                if route:
                    finish()

            route_ctx(0)
            route_copy(ctx_t)
            route_copy(h_t)
            route_silu()
            route_tanh()
            finish()
            with act.Fori(0, B - 1) as b:
                body(b, True)
            body(B - 1, False)

        @block.vector
        def _(dve):
            dve.wait_ge(consts_in, 16 * len(loads))
            dve.wait_ge(tables_ready, NTABLES)
            own, scaled, attn, logits = Count(), Count(), Count(), Count()
            counts, tanhs, updated = Count(), Count(), Count()
            downs, ys, y_room = Count(), Count(), Count()

            def over_d(v):
                return v.unsqueeze(2).to_broadcast([P, NT, D])

            def mod(b, i):
                return k["mod"][:, b, i, :].unsqueeze(1).to_broadcast([P, NT, D])

            def over_e(v):
                return v[:].unsqueeze(2).to_broadcast(wide)

            def link(ins):
                ins.then_inc(dve_done, 1)
                dve.wait_ge(dve_done, own.more())

            def route_residual(b):
                dve.wait_ge(attn_ready, attn.more())
                link(dve.tensor_tensor(gated[:], ps_r[:].rearrange("p (t d) -> p t d", d=D), mod(b, 2), ALU.mult))
                link(dve.tensor_tensor(k["x"][:, b], k["x"][:, b], gated[:], ALU.add))

            def route_stats(b):
                for i in range(NT):
                    dve.bn_stats(stats[:, i, :], k["x"][:, b, i, :]).then_inc(dve_done, 1)
                dve.wait_ge(dve_done, own.more(NT))

            def route_variance():
                for i in range(NT):
                    dve.bn_aggr(mean_var[:, i, :], stats[:, i, :]).then_inc(dve_done, 1)
                dve.wait_ge(dve_done, own.more(NT))
                dve.tensor_scalar(var_eps[:], mean_var[:, :, 1], EPS, None, ALU.add).then_inc(var_ready, 1)

            def route_norm(b):
                dve.wait_ge(scale_ready, scaled.more())
                for i in range(NT):
                    dve.tensor_scalar(xn[:, i, :], k["x"][:, b, i, :], mean_var[:, i, 0:1], scale[:, i:i + 1],
                                      ALU.subtract, ALU.mult).then_inc(dve_done, 1)
                dve.wait_ge(dve_done, own.more(NT))

            def route_modulate(b):
                link(dve.tensor_tensor(xm[:], xn[:], mod(b, 4), ALU.mult))
                dve.tensor_tensor(h[:], xm[:], mod(b, 3), ALU.add).then_inc(h_ready, 1)
                dve.drain().then_inc(h_ready_pool, 1)

            def route_top(n):
                of = logit if n == 0 else left
                link(dve.tensor_reduce(top[n][:], of[:], axis=AX.X, op=ALU.max))
                link(dve.tensor_tensor(cand[0][:], of[:], over_e(top[n]), ALU.is_equal))
                link(dve.tensor_tensor(cand[1][:], cand[0][:], order[:].unsqueeze(1).to_broadcast(wide), ALU.mult))
                link(dve.tensor_reduce(first[n][:], cand[1][:], axis=AX.X, op=ALU.max))
                link(dve.tensor_tensor(chosen[n][:], cand[1][:], over_e(first[n]), ALU.is_equal))

            def route_first():
                dve.wait_ge(logits_ready, logits.more())
                link(dve.tensor_tensor(logit[:], ps_r[:, 0:NT * NE].rearrange("p (t e) -> p t e", e=NE),
                                       rb2[:].unsqueeze(1).to_broadcast(wide), ALU.add))
                route_top(0)
                link(dve.scalar_tensor_tensor(out=left[:], in0=chosen[0][:], scalar=-3e38, in1=logit[:],
                                              op0=ALU.mult, op1=ALU.add))

            def route_second():
                route_top(1)
                dve.tensor_tensor(both[:, 0:NT, :], chosen[0][:], chosen[1][:], ALU.add).then_inc(both_ready, 1)
                dve.tensor_tensor(gap[:], top[0][:], top[1][:], ALU.subtract).then_inc(gap_ready, 1)

            def route_slots(b):
                dve.wait_ge(counts_ready, counts.more())
                count = ps_r[:, BANK:BANK + (NT + 1) * NE].rearrange("p (t e) -> p t e", e=NE)
                link(dve.tensor_scalar(tiles_i[:], count[:, NT, :], float(P - 1), None, ALU.add))
                link(dve.tensor_scalar(tiles_s[:], tiles_i[:], P.bit_length() - 1, None, ALU.logical_shift_right))
                link(dve.tensor_copy(tiles_f[:], tiles_s[:]))
                link(dve.tensor_tensor(lower_tiles[:], lower[:], tiles_f[:].unsqueeze(1).to_broadcast([P, NE, NE]),
                                       ALU.mult))
                link(dve.tensor_reduce(start[:], lower_tiles[:], axis=AX.X, op=ALU.add))
                dve.tensor_tensor(end[:], start[:], tiles_f[:], ALU.add).then_inc(dve_done, 1)
                dve.tensor_scalar(start_slot[:], start[:], float(P), slot_base[:, b, :], ALU.mult,
                                  ALU.add).then_inc(dve_done, 1)
                dve.wait_ge(dve_done, own.more(2))
                link(dve.tensor_tensor(place_all[:], count[:, 0:NT, :], start_slot[:].unsqueeze(1).to_broadcast(wide),
                                       ALU.add))
                for n in range(2):
                    dve.tensor_tensor(place_of[n][:], chosen[n][:], place_all[:], ALU.mult).then_inc(dve_done, 1)
                dve.wait_ge(dve_done, own.more(2))
                for n in range(2):
                    dve.tensor_reduce(place[:, n, :], place_of[n][:], axis=AX.X, op=ALU.add).then_inc(dve_done, 1)
                dve.wait_ge(dve_done, own.more(2))
                dve.tensor_copy(slot[:, b], place[:]).then_inc(slot_ready, 1)

            def route_weights(b):
                dve.wait_ge(tanh_ready, tanhs.more())
                dve.tensor_scalar(weight[:, b, 0, :], tanh_gap[:], 0.5, 0.5, ALU.mult, ALU.add)
                dve.tensor_scalar(weight[:, b, 1, :], tanh_gap[:], -0.5, 0.5, ALU.mult, ALU.add)
                link(dve.tensor_tensor(ended[:], end[:].unsqueeze(1).to_broadcast([P, TILES_B, NE]), tile_no[:],
                                       ALU.is_le))
                link(dve.tensor_reduce(expert_f[:], ended[:], axis=AX.X, op=ALU.add))
                dve.wait_ge(x_updated, updated.more())

            def route_experts():
                link(dve.tensor_scalar(expert[:], expert_f[:], float(NE - 1), None, ALU.min))

            def finish():
                dve.sem_inc(attn_ready, attn.back())
                dve.sem_inc(scale_ready, scaled.back())
                dve.sem_inc(logits_ready, logits.back())
                dve.sem_inc(counts_ready, counts.back())
                dve.sem_inc(tanh_ready, tanhs.back())
                dve.sem_inc(x_updated, updated.back())
                dve.sem_inc(dve_done, own.back())

            def copy_w(n):
                e = dve.value_load(expert[0:1, n:n + 1], min_val=0, max_val=NE - 1)
                dve.tensor_copy(w_tile[n % WRING][:], w_all[:, e, :]).then_inc(w_ready, 1)

            def combine_scale(b):
                dve.wait_ge(gathered, 16 * 2 * NT * (b + 1))
                for n in range(2):
                    dve.tensor_tensor(scaled_rows[n][:], rows[n][:], over_d(weight[:, b, n, :]),
                                      ALU.mult).then_inc(dve_done, 1)
                dve.wait_ge(dve_done, own.more(2))

            def combine_add():
                link(dve.tensor_tensor(mixed[:], scaled_rows[0][:], scaled_rows[1][:], ALU.add))

            def combine_gate(b):
                link(dve.tensor_tensor(mixed_g[:], mixed[:], mod(b, 5), ALU.mult))
                dve.tensor_tensor(k["x"][:, b], k["x"][:, b], mixed_g[:], ALU.add).then_inc(out_ready, 1)

            def body(b, route, combine):
                for n in range(WRING - 1):
                    copy_w(n)
                for n in range(TILES_B):
                    if n == 0:
                        dve.wait_ge(y_free, y_room.more())
                    dve.wait_ge(down_ready, downs.more())
                    dve.tensor_tensor(y[:, n, :], ps_down[n % 2][:, 0:D], w_tile[n % WRING][:, W_B2:W_END],
                                      ALU.add).then_inc(y_done, 1)
                    if n:
                        dve.wait_ge(y_done, ys.more())
                    if n and n % QUAD == 0:
                        dve.sem_inc(y_ready, 1)
                    if n == TILES_B - 2:
                        dve.sem_inc(last_bank_free, 1)
                    if n + WRING - 1 < TILES_B:
                        copy_w(n + WRING - 1)
                    if route:
                        if n == 1:
                            route_residual(b + 1)
                        if n == 2:
                            route_stats(b + 1)
                        if n == 3:
                            route_variance()
                        if n == 4:
                            route_norm(b + 1)
                        if n == 5:
                            route_modulate(b + 1)
                        if n == AT_ROUTER + 2:
                            route_first()
                        if n == AT_ROUTER + 3:
                            route_second()
                        if n == AT_COUNT + 1:
                            route_slots(b + 1)
                        if n == AT_COUNT + 2:
                            route_weights(b + 1)
                        if n == TILES_B - 1:
                            route_experts()
                    if combine:
                        if n == AT_COUNT + 3:
                            combine_scale(b - 1)
                        if n == AT_COUNT + 5:
                            combine_add()
                        if n == AT_COUNT + 6:
                            combine_gate(b - 1)
                dve.wait_ge(y_done, ys.more())
                dve.sem_inc(y_ready, 1)
                dve.sem_inc(y_done, ys.back())
                dve.sem_inc(y_free, y_room.back())
                dve.sem_inc(down_ready, downs.back())
                if route:
                    finish()
                elif combine:
                    dve.sem_inc(dve_done, own.back())

            route_residual(0)
            route_stats(0)
            route_variance()
            route_norm(0)
            route_modulate(0)
            route_first()
            route_second()
            route_slots(0)
            route_weights(0)
            route_experts()
            finish()
            body(0, True, False)
            with dve.Fori(1, B - 1) as b:
                body(b, True, True)
            body(B - 1, False, True)
            combine_scale(B - 1)
            combine_add()
            combine_gate(B - 1)

        @block.tensor
        def _(pe):
            pe.wait_ge(consts_in, 16 * len(loads))
            pe.wait_ge(tables_ready, NTABLES)
            staged, copies, h_in, acts, chosen_in = Count(), Count(), Count(), Count(), Count()
            loaded = [Count(), Count()]
            slots, ws, hids, banks = Count(), Count(), Count(), Count()

            def turn(src):
                for i in range(NT):
                    ins = pe.transpose(ps_r[:, i * P:(i + 1) * P], src[:, i], k["ident"][:])
                ins.then_inc(turned, 1)

            def route_turn_ctx():
                pe.wait_ge(ctx_s_ready, staged.more())
                turn(ctx_s[:].rearrange("p t g f -> p t (g f)"))

            def route_project():
                pe.wait_ge(copied, copies.more())
                for i in range(NT):
                    ins = pe.matmul(ps_r[:, i * P:(i + 1) * P], ctx_t[:, i * P:(i + 1) * P], wo[:],
                                    start=True, stop=True)
                ins.then_inc(attn_ready, 1)

            def route_turn_h():
                pe.wait_ge(h_ready, h_in.more())
                turn(h[:])

            def route_router():
                pe.wait_ge(copied, copies.more())
                for c in range(2):
                    ins = pe.matmul(ps_r[:, c * BANK:(c + 1) * BANK], rw1[:], h_t[:, c * BANK:(c + 1) * BANK],
                                    start=True, stop=True)
                ins.then_inc(router_ps_ready, 1)

            def route_logits():
                pe.wait_ge(router_act_ready, acts.more())
                for i in range(NT):
                    ins = pe.matmul(ps_r[:, i * NE:(i + 1) * NE], router_act[:, i * P:(i + 1) * P], rw2[:],
                                    start=True, stop=True)
                ins.then_inc(logits_ready, 1)

            def route_counts():
                pe.wait_ge(both_ready, chosen_in.more())
                count = ps_r[:, BANK:BANK + (NT + 1) * NE]
                pe.matmul(count, before[:], both[:].rearrange("p t e -> p (t e)"), start=True, stop=False)
                for i in range(NT):
                    ins = pe.matmul(count[:, (i + 1) * NE:].rearrange("p (t e) -> p t e", e=NE), ones[:],
                                    both[:, i:i + 1, :].to_broadcast([P, NT - i, NE]),
                                    start=False, stop=i == NT - 1)
                ins.then_inc(counts_ready, 1)

            def finish():
                pe.sem_inc(ctx_s_ready, staged.back())
                pe.sem_inc(copied, copies.back())
                pe.sem_inc(h_ready, h_in.back())
                pe.sem_inc(router_act_ready, acts.back())
                pe.sem_inc(both_ready, chosen_in.back())

            def turn_slots(n):
                q = n // QUAD
                if n % QUAD == 0:
                    pe.wait_ge(slots_loaded[q % 2], loaded[q % 2].more(16))
                ins = pe.transpose(ps_t[n % 2][:, 0:P], slots_in[q % 2][:, n % QUAD, :], k["ident"][:])
                ins.then_inc(slots_turned, 1)

            def up(n):
                pe.wait_ge(w_ready, ws.more())
                pe.wait_ge(slots_t_ready, slots.more())
                for c in range(HC):
                    ins = pe.matmul(ps_up[n % 2][:, c * P:(c + 1) * P], w_tile[n % WRING][:, c * P:(c + 1) * P],
                                    slots_t[n % 2][:], start=True, stop=True)
                    if c == 0 and n % QUAD == QUAD - 1:
                        ins.then_inc(slots_used, 1)
                ins.then_inc(up_ready, 1)

            def down(n):
                pe.wait_ge(hid_ready, hids.more())
                if n == TILES_B - 1:
                    pe.wait_ge(last_bank_free, banks.more())
                for c in range(HC):
                    at = W_DOWN + c * D
                    ins = pe.matmul(ps_down[n % 2][:, 0:D], hid[n % 2][:, c, :], w_tile[n % WRING][:, at:at + D],
                                    start=c == 0, stop=c == HC - 1)
                ins.then_inc(down_ready, 1)

            def body(route):
                for n in range(-2, TILES_B):
                    if n + 2 < TILES_B:
                        turn_slots(n + 2)
                    if 0 <= n + 1 < TILES_B:
                        up(n + 1)
                    if n >= 0:
                        down(n)
                    if route:
                        if n == AT_CTX:
                            route_turn_ctx()
                        if n == AT_CTX + 1:
                            route_project()
                        if n == AT_H:
                            route_turn_h()
                        if n == AT_ROUTER:
                            route_router()
                        if n == AT_ROUTER + 1:
                            route_logits()
                        if n == AT_COUNT:
                            route_counts()
                pe.sem_inc(w_ready, ws.back())
                pe.sem_inc(slots_t_ready, slots.back())
                pe.sem_inc(hid_ready, hids.back())
                pe.sem_inc(last_bank_free, banks.back())
                for i in range(2):
                    pe.sem_inc(slots_loaded[i], loaded[i].back())
                if route:
                    finish()

            route_turn_ctx()
            route_project()
            route_turn_h()
            route_router()
            route_logits()
            route_counts()
            finish()
            with pe.Fori(0, B - 1):
                body(True)
            body(False)


def head_order():
    order, angle, is_sin = [], [], []
    for g in range(GROUPS):
        for r in range(2):
            for f in range(HD):
                for u in range(2):
                    order.append((GH * g + 2 * u + r) * HD + f // 2 * 2)
                    angle.append(f // 2)
                    is_sin.append(f % 2)
    return np.array(order), np.array(angle), np.array(is_sin)


def rope_table():
    _, angle, is_sin = head_order()
    freqs = np.exp(np.arange(0, HD, 2, dtype=np.float32) * np.float32(-np.log(10000.0) / HD)).astype(np.float32)
    angles = (np.arange(S, dtype=np.float32)[None, :] * freqs[angle][:, None]).astype(np.float32).astype(np.float64)
    return np.where(is_sin[:, None] == 1, -np.sin(angles), np.cos(angles)).astype(np.float32)


def kernel(**inputs):
    from concourse import bacc
    from concourse.bass_utils import run_bass_kernel_spmd

    i = {name.removeprefix("L0_"): np.asarray(a) for name, a in inputs.items()}
    order, _, _ = head_order()
    arrays = {
        "x": i["attn_x"], "c_t": i["c"].T, "wmod": i["wmod"],
        "wq_t": i["attn_Wq"][order].T, "wk_t": i["attn_Wk"][order].T, "wv_t": i["attn_Wv"].T,
        "wo_t": i["attn_Wo"].T, "rope": rope_table(), "before": np.triu(np.ones((P, P), np.float32), 1),
        "rw1": i["ffn_rw1"], "rb1": i["ffn_rb1"][:, None], "rw2": i["ffn_rw2"], "rb2": i["ffn_rb2"][None, :],
        "we1": i["ffn_we1"], "we2": i["ffn_we2"],
        "be1": i["ffn_be1"].reshape(NE, HID // P, P).transpose(2, 0, 1), "be2": i["ffn_be2"],
    }
    arrays = {name: np.ascontiguousarray(a) for name, a in arrays.items()}
    nc = bacc.Bacc("TRN2", target_bir_lowering=False, num_devices=1)
    t = {name: nc.dram_tensor(f"in_{name}", a.shape, F32, kind="ExternalInput").ap() for name, a in arrays.items()}
    t["out"] = nc.dram_tensor("out", (B, S, D), F32, kind="ExternalOutput").ap()
    build(nc, t)
    return run_bass_kernel_spmd(nc, [{f"in_{name}": a for name, a in arrays.items()}], core_ids=[0]).results[0]["out"]
```

```python
from contextlib import ExitStack

import concourse.bass as bass
import concourse.mybir as mybir
import numpy as np

F32 = mybir.dt.float32
BF16 = mybir.dt.bfloat16
I32 = mybir.dt.int32
ALU = mybir.AluOpType
ACT = mybir.ActivationFunctionType
AX = mybir.AxisListType

P = 128
B, S, D = 4, 1024, 128
HEADS, HD = 16, 8
NE, HID = 8, 512
NT = S // P
GH = 4
GROUPS = HEADS // GH
NG = B * GROUPS
GF = GH * HD
EPS = 1e-5
BANK = 512

TERMS = ((0, 0), (0, 1), (1, 0), (1, 1), (0, 2), (2, 0))
HALF_ROWS = 3 * HD
MAX_ROW = HALF_ROWS

STEPS = 16
PAIR = 2 * STEPS
LEAD = 8
UNITS = GH * NT
RING = 4

HC = HID // P
QUAD = 4
TILES_B = -(-(2 * S // P + NE - 1) // QUAD) * QUAD
QUADS = TILES_B // QUAD
SLOTS_B = TILES_B * P
WRING = 4
QRING = 3
assert TILES_B % WRING == 0 and QUADS % QRING == 0
assert B == 4


class Count:

    def __init__(self):
        self.seen = 0

    def at(self, n):
        self.seen = max(self.seen, n)
        return n

    def more(self, n=1):
        return self.at(self.seen + n)

    def back(self, n=None):
        n = self.seen if n is None else n
        self.seen -= n
        return -n


def build(nc, t):
    with ExitStack() as ctx:
        def sb(name, shape, dt=F32):
            return ctx.enter_context(nc.sbuf_tensor(name, shape, dt))

        def scratch(name, shape, dt):
            return nc.dram_tensor(name, shape, dt, kind="Internal").ap()

        k = {
            "q_terms": scratch("q_terms", [NG, 2, len(TERMS) // 2, 2, HD, 2, S], BF16),
            "k_terms": scratch("k_terms", [NG, 2, len(TERMS) // 2, 2, HD, 2, S], BF16),
            "slots": scratch("slots", [B * SLOTS_B, D], F32),
            "y_slots": scratch("y_slots", [B * SLOTS_B, D], F32),
            "x": sb("x_sb", [P, B, NT, D]),
            "mod": sb("mod", [P, B, 6, D]),
            "ident": sb("ident", [P, P]),
            "ident16": sb("ident16", [P, P], BF16),
            "rsqrt_exp": sb("rsqrt_exp", [P, NT]),
            "wo": sb("wo", [P, D]), "rw1": sb("rw1", [P, D]), "rw2": sb("rw2", [P, NE]),
            "rb1": sb("rb1", [P, 1]), "rb2": sb("rb2", [P, NE]),
            "before": sb("before", [P, P]),
            "v": sb("v", [P, NG, NT, GF]),
            "ctx": sb("ctx", [P, NG, NT, GF]),
        }
        k["routing"] = routing(nc, ctx, k)
        with ExitStack() as operands:
            for name, blocks in (("q_max", 2), ("q_exp", 2), ("k_max", GH), ("k_exp", GH)):
                k[name] = [operands.enter_context(nc.sbuf_tensor(f"{name}{i}", [P, blocks, S], BF16))
                           for i in range(2)]
            k["v_grp"] = [operands.enter_context(nc.sbuf_tensor(f"v_grp{i}", [P, NT, GH, 32], F32))
                          for i in range(2)]
            for which in ("max", "exp"):
                k[f"in_{which}"] = [operands.enter_context(nc.semaphore(f"{which}_in{i}")) for i in range(2)]
            k["parts"] = [operands.enter_context(nc.sbuf_tensor(f"parts{i}", [P, 3, S], BF16)) for i in range(2)]
            for name in ("parts_ready", "parts_stored"):
                k[name] = operands.enter_context(nc.semaphore(name))
            prepare(nc, t, k)
            attend(nc, t, k)
        mix(nc, t, k)


LOADS = 8


def load_operands(sp, k, which, parity, group):
    q_of, k_of, loaded = (k[f"{name}_{which}"] for name in ("q", "k", "in"))
    for dst, src, blocks in ((q_of[parity], k["q_terms"], 1), (k_of[parity], k["k_terms"], 2)):
        for r in range(2):
            block = 2 * r * (blocks - 1)
            for half in range(2):
                row = 64 * r + 32 * half
                sp.dma_start(dst[row:row + HALF_ROWS, block:block + 2, :],
                             src[group, half, :, r].rearrange("t f u n -> t f (u n)")).then_inc(loaded[parity], 16)


def store_parts(sp, k, b):
    for qk, name in enumerate(("q_terms", "k_terms")):
        terms = k[name].rearrange("(b g) h t r f u n -> b h t g (r f u) n", b=B)
        sp.wait_ge(k["parts_ready"], qk + 1)
        for n, term in enumerate(TERMS):
            sp.dma_start(terms[b, n // 3, n % 3], k["parts"][qk][:, term[qk], :]).then_inc(k["parts_stored"], 16)
    sp.sem_inc(k["parts_ready"], -2)


def prepare(nc, t, k):
    with ExitStack() as ctx:
        def sb(name, shape, dt=F32):
            return ctx.enter_context(nc.sbuf_tensor(name, shape, dt))

        def sem(name):
            return ctx.enter_context(nc.semaphore(name))

        c_t = sb("c_t", [P, B])
        silu_c = sb("silu_c", [P, B])
        silu_cb = sb("silu_cb", [P, B, P])
        wmod = sb("wmod", [P, 6 * D])
        wq, wk, wv = sb("wq", [P, D]), sb("wk", [P, D]), sb("wv", [P, D])
        rope = sb("rope", [P, S])
        g_sign = sb("g_sign", [P, B * 2, D])
        g_size = sb("g_size", [P, B * 2, D])
        stats = sb("stats", [P, NT, 6])
        mean_var = sb("mean_var", [P, NT, 2])
        var_eps = sb("var_eps", [P, NT])
        scale = sb("scale", [P, NT])
        xn = sb("xn", [P, NT, D])
        xm = sb("xm", [P, NT, D])
        h = sb("h", [P, NT, D])
        h_t = sb("h_t1", [P, S])
        rot = [sb(f"rot{i}", [P, S]) for i in range(2)]
        rest = [sb(f"rest{i}", [P, S]) for i in range(2)]
        parts, parts_stored = k["parts"], k["parts_stored"]
        CLEAR = 8
        CLEARS = B * SLOTS_B // (P * CLEAR)
        zero_rows = sb("zero_rows", [P, CLEAR * D])
        ps = [ctx.enter_context(nc.psum_tensor(f"prep{i}", [P, 2 * BANK], F32)) for i in range(4)]
        ps_t, ps_q, ps_k, ps_v = ps

        consts_in = sem("consts_in")
        x_in = sem("x_in")
        ident_ready = sem("ident_ready")
        silu_c_ready = sem("silu_c_ready")
        zero_rows_ready = sem("zero_rows_ready")
        slots_cleared = sem("slots_cleared")
        later_consts_in = sem("later_consts_in")
        zeros_ready = sem("zeros_ready")
        silu_cb_ready = sem("silu_cb_ready")
        mod_ps_ready = sem("mod_ps_ready")
        mod_ready = sem("mod_ready")
        dve_done = sem("prep_dve_done")
        pool_done = sem("prep_pool_done")
        var_ready = sem("var_ready")
        scale_ready = sem("scale_ready")
        xn_ready = sem("xn_ready")
        xn_used = sem("xn_used")
        h_ready = sem("h_ready")
        h_used = sem("h_used")
        h_t_ps_ready = sem("h_t_ps_ready")
        h_t_ready = sem("h_t_ready")
        qk_ps_ready = sem("qk_ps_ready")
        v_ps_ready = sem("v_ps_ready")
        rot_ready = sem("rot_ready")
        part0_ready = sem("part0_ready")
        rest_ready = sem("rest_ready")
        part1_ready = sem("part1_ready")
        parts_ready = k["parts_ready"]
        block = ctx.enter_context(nc.Block())

        loads = [(c_t, t["c_t"]), (wmod, t["wmod"]), (wq, t["wq_t"]), (wk, t["wk_t"]), (wv, t["wv_t"]),
                 (rope, t["rope"])]
        later_loads = [(k["wo"], t["wo_t"]), (k["rw1"], t["rw1"]), (k["rw2"], t["rw2"]), (k["rb1"], t["rb1"]),
                       (k["rb2"], t["rb2"].to_broadcast([P, NE])), (k["before"], t["before"])]

        @block.sync
        def _(sp):
            for dst, src in loads:
                sp.dma_start(dst[:], src).then_inc(consts_in, 16)
            sp.dma_start(k["x"][:], t["x"].rearrange("b (t p) d -> p b t d", p=P)).then_inc(x_in, 16)
            for dst, src in later_loads:
                sp.dma_start(dst[:], src).then_inc(later_consts_in, 16)
            sp.wait_ge(zero_rows_ready, 1)
            for name in ("slots", "y_slots"):
                clear = k[name].rearrange("(n p r) d -> n p (r d)", p=P, r=CLEAR)
                for n in range(CLEARS):
                    sp.dma_start(clear[n], zero_rows[:]).then_inc(slots_cleared, 16)

            with sp.Fori(0, 2) as b:
                store_parts(sp, k, b)
            load_operands(sp, k, "max", 0, 0)
            sp.wait_ge(slots_cleared, 16 * 2 * CLEARS)
            with sp.Fori(2, B - 1) as b:
                store_parts(sp, k, b)
            sp.wait_ge(later_consts_in, 16 * len(later_loads))

        @block.gpsimd
        def _(pool):
            own = Count()
            pool.memset(zero_rows[:], 0.0).then_inc(zero_rows_ready, 1)
            pool.memset(k["rsqrt_exp"][:], -0.5).then_inc(pool_done, 1)
            pool.memset(k["ident"][:], 0.0).then_inc(pool_done, 1)
            pool.memset(k["ident16"][:], 0.0).then_inc(pool_done, 1)
            pool.wait_ge(pool_done, own.more(3))
            for m in ("ident", "ident16"):
                pool.affine_select(out=k[m][:], in_=k[m][:], compare_op=ALU.not_equal, fill=1.0, base=0,
                                   pattern=[[-1, P]], channel_multiplier=1).then_inc(ident_ready, 1)
            pool.sem_inc(pool_done, own.back())
            var, normed = Count(), Count()

            def norm_scale():
                pool.wait_ge(var_ready, var.more())
                pool.tensor_tensor(scale[:], var_eps[:], k["rsqrt_exp"][:], ALU.pow).then_inc(scale_ready, 1)
                pool.sem_inc(var_ready, var.back())

            pool.sem_inc(h_used, 1)

            def modulate(b):
                shape = [P, NT // 2, D]
                for half in range(2):
                    tiles = slice(half * NT // 2, (half + 1) * NT // 2)
                    pool.wait_ge(xn_ready, normed.more())
                    pool.tensor_tensor(xm[:, tiles], xn[:, tiles], k["mod"][:, b, 1, :].unsqueeze(1).to_broadcast(shape),
                                       ALU.mult).then_inc(pool_done, 1)
                    pool.wait_ge(pool_done, own.more())
                    if half == 0:
                        pool.wait_ge(h_used, 1)
                        pool.sem_inc(h_used, -1)
                    else:
                        pool.sem_inc(xn_used, 1)
                    pool.tensor_tensor(h[:, tiles], xm[:, tiles], k["mod"][:, b, 0, :].unsqueeze(1).to_broadcast(shape),
                                       ALU.add).then_inc(h_ready, 1)
                pool.sem_inc(xn_ready, normed.back(2))
                pool.sem_inc(pool_done, own.back(2))

            for i in range(2):
                for name in ("q_max", "q_exp", "k_max", "k_exp", "v_grp"):
                    pool.memset(k[name][i][:], 0.0).then_inc(zeros_ready, 1)
                if i == 0:
                    norm_scale()
            pool.wait_ge(mod_ready, 1)
            with pool.Fori(0, B - 1) as b:
                modulate(b)
                norm_scale()
            modulate(B - 1)

        @block.scalar
        def _(act):
            act.wait_ge(consts_in, 16 * len(loads))
            act.activation(silu_c[:], c_t[:], ACT.Silu).then_inc(silu_c_ready, 1)
            h_t_ps, v_ps = Count(), Count()
            rotated, rests, stored = Count(), Count(), Count()
            act.sem_inc(parts_stored, 16 * 2 * len(TERMS))
            with act.Fori(0, B) as b:
                for c in range(2):
                    act.wait_ge(h_t_ps_ready, h_t_ps.more())
                    act.copy(h_t[:, c * BANK:(c + 1) * BANK],
                             ps_t[:, c * BANK:(c + 1) * BANK]).then_inc(h_t_ready, 1)
                act.wait_ge(parts_stored, stored.more(16 * 2 * len(TERMS)))
                for qk in range(2):
                    act.wait_ge(rot_ready, rotated.more())
                    act.copy(parts[qk][:, 0, :], rot[qk][:]).then_inc(part0_ready, 1)
                for qk in range(2):
                    act.wait_ge(rest_ready, rests.more())
                    act.copy(parts[qk][:, 1, :], rest[qk][:]).then_inc(part1_ready, 1)
                act.wait_ge(v_ps_ready, v_ps.more())
                v_of = k["v"].rearrange("p (b g) t f -> p b g t f", b=B)
                act.copy(v_of[:, b], ps_v[:].rearrange("p (t g f) -> p g t f", t=NT, g=GROUPS))
                act.sem_inc(h_t_ps_ready, h_t_ps.back(2))
                act.sem_inc(parts_stored, stored.back(16 * 2 * len(TERMS)))
                act.sem_inc(rot_ready, rotated.back(2))
                act.sem_inc(rest_ready, rests.back(2))
                act.sem_inc(v_ps_ready, v_ps.back(1))

        @block.vector
        def _(dve):
            own, scaled = Count(), Count()

            def link(ins):
                ins.then_inc(dve_done, 1)
                dve.wait_ge(dve_done, own.more())

            def norm_variance(b):
                for i in range(NT):
                    dve.bn_stats(stats[:, i, :], k["x"][:, b, i, :]).then_inc(dve_done, 1)
                dve.wait_ge(dve_done, own.more(NT))
                for i in range(NT):
                    dve.bn_aggr(mean_var[:, i, :], stats[:, i, :]).then_inc(dve_done, 1)
                dve.wait_ge(dve_done, own.more(NT))
                dve.tensor_scalar(var_eps[:], mean_var[:, :, 1], EPS, None, ALU.add).then_inc(var_ready, 1)

            def norm_rows(b):
                dve.wait_ge(scale_ready, scaled.more())
                dve.wait_ge(xn_used, 1)
                dve.sem_inc(xn_used, -1)
                for i in range(NT):
                    ins = dve.tensor_scalar(xn[:, i, :], k["x"][:, b, i, :], mean_var[:, i, 0:1],
                                            scale[:, i:i + 1], ALU.subtract, ALU.mult)
                    if i % 4 == 3:
                        ins.then_inc(xn_ready, 1)
                dve.sem_inc(dve_done, own.back())
                dve.sem_inc(scale_ready, scaled.back())

            dve.sem_inc(xn_used, 1)
            dve.wait_ge(x_in, 16)
            norm_variance(0)
            dve.wait_ge(silu_c_ready, 1)
            dve.tensor_copy(silu_cb[:], silu_c[:].unsqueeze(2).to_broadcast([P, B, P])).then_inc(silu_cb_ready, 1)
            norm_rows(0)
            mod = k["mod"][:].rearrange("p b s d -> p (b s d)")
            for b in range(B):
                dve.wait_ge(mod_ps_ready, b + 1)
                for half in range(2):
                    at = (2 * b + half) * 3 * D
                    dve.tensor_copy(mod[:, at:at + 3 * D],
                                    ps[b][:, half * BANK:half * BANK + 3 * D]).then_inc(dve_done, 1)
            dve.wait_ge(dve_done, own.more(2 * B))
            trio = k["mod"][:].rearrange("p b (u s) d -> p (b u) s d", u=2)
            gate, one_c = trio[:, :, 2, :], trio[:, :, 1, :]
            link(dve.tensor_scalar(g_sign[:], gate, 0.0, 2.0, ALU.is_ge, ALU.mult))
            link(dve.scalar_tensor_tensor(out=g_size[:], in0=gate, scalar=-1.0, in1=gate, op0=ALU.mult, op1=ALU.max))
            link(dve.tensor_scalar(g_size[:], g_size[:], 0.25, None, ALU.max))
            link(dve.tensor_scalar(one_c, one_c, 1.0, None, ALU.add))
            dve.scalar_tensor_tensor(out=gate, in0=g_sign[:], scalar=-1.0, in1=g_size[:], op0=ALU.add,
                                     op1=ALU.mult).then_inc(mod_ready, 1)
            dve.sem_inc(dve_done, own.back())
            dve.wait_ge(consts_in, 16 * len(loads))
            qk_ps = Count()
            part0, part1 = Count(), Count()

            def split(b, norm_next):
                if norm_next:
                    norm_variance(b + 1)
                    norm_rows(b + 1)
                for qk in range(2):
                    dve.wait_ge(qk_ps_ready, qk_ps.more())
                    dve.tensor_tensor(rot[qk][:], ps[1 + qk][:], rope[:], ALU.mult).then_inc(rot_ready, 1)
                for qk in range(2):
                    dve.wait_ge(part0_ready, part0.more())
                    dve.tensor_tensor(rest[qk][:], rot[qk][:], parts[qk][:, 0, :],
                                      ALU.subtract).then_inc(rest_ready, 1)
                for qk in range(2):
                    dve.wait_ge(part1_ready, part1.more())
                    dve.tensor_tensor(parts[qk][:, 2, :], rest[qk][:], parts[qk][:, 1, :],
                                      ALU.subtract).then_inc(parts_ready, 1)
                dve.sem_inc(qk_ps_ready, qk_ps.back())
                dve.sem_inc(part0_ready, part0.back())
                dve.sem_inc(part1_ready, part1.back())

            dve.wait_ge(zeros_ready, 10)
            for i in range(2):
                dve.memset(k["v_grp"][i][:, :, :, HD:HD + 1], 1.0)
                for r in range(2):
                    dve.memset(k["k_exp"][i][64 * r:64 * r + 32, 2 * r:2 * r + 2, :], 1.0)
            with dve.Fori(0, B - 1) as b:
                split(b, True)
            split(B - 1, False)

        @block.tensor
        def _(pe):
            pe.wait_ge(silu_cb_ready, 1)
            pe.wait_ge(consts_in, 16 * len(loads))
            for b in range(B):
                for half in range(2):
                    ins = pe.matmul(ps[b][:, half * BANK:half * BANK + 3 * D], silu_cb[:, b, :],
                                    wmod[:, half * 3 * D:(half + 1) * 3 * D], start=True, stop=True)
                ins.then_inc(mod_ps_ready, 1)
            pe.wait_ge(ident_ready, 2)
            pe.wait_ge(mod_ready, 1)
            h_in, h_t_in = Count(), Count()
            with pe.Fori(0, B):
                for i in range(NT):
                    if i % 4 == 0:
                        pe.wait_ge(h_ready, h_in.more())
                    ins = pe.transpose(ps_t[:, i * P:(i + 1) * P], h[:, i, :], k["ident"][:])
                    if i % 4 == 3:
                        ins.then_inc(h_t_ps_ready, 1)
                pe.wait_ge(h_t_ready, h_t_in.more(2))
                for w, out in ((wq, ps_q), (wk, ps_k)):
                    for c in range(2):
                        ins = pe.matmul(out[:, c * BANK:(c + 1) * BANK], w[:], h_t[:, c * BANK:(c + 1) * BANK],
                                        start=True, stop=True)
                        if w is wq and c == 0:
                            ins.then_inc(h_used, 1)
                    ins.then_inc(qk_ps_ready, 1)
                for i in range(NT):
                    ins = pe.matmul(ps_v[:, i * P:(i + 1) * P], h_t[:, i * P:(i + 1) * P], wv[:],
                                    start=True, stop=True)
                ins.then_inc(v_ps_ready, 1)
                pe.sem_inc(h_ready, h_in.back(2))
                pe.sem_inc(h_t_ready, h_t_in.back(2))


def attend(nc, t, k):
    with ExitStack() as ctx:
        def sb(name, shape, dt=F32):
            return ctx.enter_context(nc.sbuf_tensor(name, shape, dt))

        def psum(name, shape, dt=F32):
            return ctx.enter_context(nc.psum_tensor(name, shape, dt))

        def sem(name):
            return ctx.enter_context(nc.semaphore(name))

        q_max, k_max, q_exp, k_exp, v_grp = (k[name] for name in ("q_max", "k_max", "q_exp", "k_exp", "v_grp"))
        probs = sb("probs", [P, RING, GH, BANK])
        row_max = [sb(f"row_max{i}", [P, GH, NT]) for i in range(2)]
        neg_rest = sb("neg_rest", [P, GH, NT])
        neg_parts = [sb(f"neg_parts{i}", [P, GH, 3, NT], BF16) for i in range(2)]
        neg_rows = [sb(f"neg_rows{i}", [GH * 3 * NT, P], BF16) for i in range(2)]
        ctx_t = [sb(f"ctx_t{i}", [P, BANK]) for i in range(2)]
        inv_sum = sb("inv_sum", [P, 4 * GH])
        ps_max = [psum(f"ps_max{i}", [P, 2 * BANK]) for i in range(2)]
        ps_scores = [psum(f"ps_scores{i}", [P, BANK]) for i in range(2)]
        ps_ctx = psum("ps_ctx", [P, BANK])
        ps_turn = psum("ps_turn", [P, BANK])

        max_in, exp_in = k["in_max"], k["in_exp"]
        rows_in = [sem(f"rows_in{i}") for i in range(2)]
        v_ready = sem("v_ready")
        v_used = sem("v_used")
        exp_operands_used = sem("exp_operands_used")
        max_scores_ready = sem("max_scores_ready")
        max_taken = sem("max_taken")
        neg_step = sem("neg_step")
        neg_parts_ready = sem("neg_parts_ready")
        neg_turned = sem("neg_turned")
        neg_rows_ready = sem("neg_rows_ready")
        scores_ready = sem("scores_ready")
        probs_ready = sem("probs_ready")
        ctx_added = sem("ctx_added")
        ctx_t_ready = sem("ctx_t_ready")
        ctx_turned = sem("ctx_turned")
        sums_inverted = sem("sums_inverted")
        ctx_ready = sem("ctx_ready")
        spare = [part[:].rearrange("p a s -> p (a s)").bitcast(F32)[:, 0:S] for part in k["parts"]]
        r = route_buffers(k["routing"], sb, "_attend", spare[0], spare[1].rearrange("p (t d) -> p t d", d=D))
        banks, early_banks = ((ps[:, 0:BANK], ps[:, BANK:]) for ps in ps_max)
        MAX_DONE = (UNITS - LEAD) // 2
        NTABLES = 3 + 2 * NE + TILES_B + B
        block = ctx.enter_context(nc.Block())

        PAIRS = NG // 2
        FIRST = 2

        def unit(n):
            n %= UNITS
            return 2 * (n // 2 % 2) + 1 - n % 2, n // 4

        def units(s):
            return (UNITS + LEAD + 2 * s, UNITS + LEAD + 2 * s + 1)

        def chain_step(s):
            after = s + LEAD // 2 + 1
            return after // STEPS if after % STEPS == 0 else None

        @block.sync
        def _(sp):
            def load(which, parity, group):
                load_operands(sp, k, which, parity, group)

            def negated_rows(parity):
                for head in range(GH):
                    row = 64 * (head % 2) + MAX_ROW
                    sp.dma_start(q_exp[parity][row:row + 3, head // 2, :],
                                 neg_rows[parity][head * 3 * NT:(head + 1) * 3 * NT, :]).then_inc(rows_in[parity], 16)

            rows, used = Count(), Count()
            load("max", 1, 1)
            for g in range(2):
                load("exp", g, g)
            store_parts(sp, k, B - 1)
            sp.wait_ge(neg_rows_ready, rows.more())
            negated_rows(0)
            load("max", 0, 2)
            sp.wait_ge(k["parts_stored"], 16 * 2 * len(TERMS))
            sp.sem_inc(neg_rows_ready, rows.back())
            with sp.Fori(0, PAIRS - 1) as p:
                sp.wait_ge(neg_rows_ready, rows.more())
                negated_rows(1)
                load("max", 1, 2 * p + 3)
                sp.wait_ge(exp_operands_used, used.more())
                load("exp", 0, 2 * p + 2)
                sp.wait_ge(neg_rows_ready, rows.more())
                negated_rows(0)
                load("max", 0, (2 * p + 4) % NG)
                sp.wait_ge(exp_operands_used, used.more())
                load("exp", 1, 2 * p + 3)
                sp.sem_inc(neg_rows_ready, rows.back(2))
                sp.sem_inc(exp_operands_used, used.back(2))
            sp.wait_ge(neg_rows_ready, rows.more())
            negated_rows(1)

        @block.gpsimd
        def _(pool):
            def fill(parity, group):
                pool.tensor_copy(v_grp[parity][:, :, :, 0:HD].rearrange("p t h f -> p (t h) f"),
                                 k["v"][:, group].rearrange("p t (h f) -> p (t h) f", h=GH)).then_inc(v_ready, 1)

            for g in range(2):
                fill(g, g)
            pool.memset(r.ones[:], 1.0).then_inc(r.tables_ready, 1)
            pool.memset(r.both[:], 0.0).then_inc(r.tables_ready, 1)
            pool.memset(r.lower[:], 0.0).then_inc(r.tables_ready, 1)
            pool.wait_ge(r.tables_ready, 3)
            for e in range(NE):
                pool.memset(r.order[:, e:e + 1], float(NE - e)).then_inc(r.tables_ready, 1)
                pool.memset(r.lower[:, e, 0:max(e, 1)], float(e > 0)).then_inc(r.tables_ready, 1)
            for n in range(TILES_B):
                pool.memset(r.tile_no[:, n, :], float(n)).then_inc(r.tables_ready, 1)
            for b in range(B):
                pool.memset(r.slot_base[:, b, :], float(b * SLOTS_B)).then_inc(r.tables_ready, 1)
            used = Count()
            with pool.Fori(0, PAIRS - 1) as p:
                for g in range(2):
                    pool.wait_ge(v_used, used.more())
                    fill(g, 2 * p + 2 + g)
                pool.sem_inc(v_used, used.back(2))
            route = route_on_pool(pool, k, r, banks)
            route.norm_scale()
            route.update(0, r.h)
            route.norm_scale()
            route.scatter_start(0)
            route.scatter(0)
            route.scatter(1)

        @block.tensor
        def _(pe):
            maxima_in = [Count(), Count()]
            exps_in = [Count(), Count()]
            rows = [Count(), Count()]
            taken, probs_in = Count(), Count()
            negs, v_in = Count(), Count()
            evacuated, normed = Count(), Count()

            def max_scores(n):
                head, tile = unit(n)
                g = n // UNITS
                if n % UNITS == 0:
                    pe.wait_ge(max_in[g % 2], maxima_in[g % 2].at(16 * LOADS * (g // 2 + 1)))
                if n >= 2:
                    pe.wait_ge(max_taken, taken.at(n - 1))
                r, u = head % 2, head // 2
                for c in range(2):
                    ins = pe.matmul(ps_max[n % 2][:, c * BANK:(c + 1) * BANK],
                                    q_max[g % 2][:, u, tile * P:(tile + 1) * P],
                                    k_max[g % 2][:, 2 * r + u, c * BANK:(c + 1) * BANK],
                                    start=True, stop=True)
                ins.then_inc(max_scores_ready, 1)

            def scores(s, place):
                head, g, c, tile = place, s // STEPS, s // NT % 2, s % NT
                if s % STEPS == 0 and place == 0:
                    pe.wait_ge(exp_in[g % 2], exps_in[g % 2].at(16 * LOADS * (g // 2 + 1)))
                    pe.wait_ge(rows_in[g % 2], rows[g % 2].at(16 * GH * (g // 2 + 1)))
                n = GH * s + place
                if n >= 2:
                    pe.wait_ge(probs_ready, probs_in.at(n - 1))
                r, u = head % 2, head // 2
                pe.matmul(ps_scores[n % 2][:], k_exp[g % 2][:, 2 * r + u, tile * P:(tile + 1) * P],
                          q_exp[g % 2][:, u, c * BANK:(c + 1) * BANK],
                          start=True, stop=True).then_inc(scores_ready, 1)

            def add_ctx(s, signal_v):
                g, tile = s // STEPS, s % NT
                pe.wait_ge(probs_ready, probs_in.at(GH * (s + 1)))
                if s % STEPS == 0:
                    pe.wait_ge(v_ready, v_in.at(g + 1))
                if tile == 0 and s:
                    pe.wait_ge(ctx_t_ready, evacuated.at(s // NT))
                for place in range(GH):
                    head = place
                    ins = pe.matmul(ps_ctx[32 * head:32 * head + 32, :], v_grp[g % 2][:, tile, head, :],
                                    probs[:, s % RING, head, :], start=tile == 0, stop=tile == NT - 1)
                    if place == 0 and s % STEPS == STEPS - 1:
                        ins.then_inc(exp_operands_used, 1)
                    if place == 0 and signal_v:
                        ins.then_inc(v_used, 1)
                ins.then_inc(ctx_added, 1)

            def turn_negated(g):
                pe.wait_ge(neg_parts_ready, negs.at(g + 1))
                pe.transpose(ps_turn[:].bitcast(BF16)[0:GH * 3 * NT, 0:P],
                             neg_parts[g % 2][:].rearrange("p h c t -> p (h c t)"),
                             k["ident16"][:]).then_inc(neg_turned, 1)

            def turn_ctx(chunk):
                pe.wait_ge(ctx_t_ready, evacuated.at(chunk + 1))
                pe.wait_ge(ctx_ready, normed.at(chunk + 1))
                for i in range(4):
                    ins = pe.transpose(ps_turn[:, i * P:(i + 1) * P], ctx_t[chunk % 2][:, i * P:(i + 1) * P],
                                       k["ident"][:])
                ins.then_inc(ctx_turned, 1)

            def step(s, last=False, signal_v=False):
                more_scores = not (last and s == PAIR - 1)
                more_units = not (last and units(s)[0] >= 2 * UNITS)
                if more_scores:
                    scores(s + 1, 0)
                    scores(s + 1, 1)
                if (g := chain_step(s - 2)) is not None and not (last and g == 2):
                    pe.wait_ge(ctx_ready, normed.at((s - 1) // NT + 1))
                    turn_negated(g)
                add_ctx(s, signal_v)
                if more_scores:
                    scores(s + 1, 2)
                    scores(s + 1, 3)
                if more_units:
                    max_scores(units(s)[0])
                    max_scores(units(s)[1])
                if s % NT == 0 and s:
                    turn_ctx(s // NT - 1)
                if last and s >= MAX_DONE:
                    route_step(s - MAX_DONE)

            route = route_on_pe(pe, k, r, banks)

            def route_step(n):
                if n == 0:
                    pe.wait_ge(max_taken, taken.at(2 * UNITS))
                    pe.wait_ge(r.tables_ready, NTABLES)
                    route.turn_ctx()
                if n == 2:
                    route.project()
                if n == 4:
                    route.turn_ctx(early_banks, wait=False)
                if n == 6:
                    route.project(early_banks)
                if n == 7:
                    route.turn_h()
                if n == 9:
                    route.router()
                if n == 10:
                    route.logits()
                if n == 11:
                    route.counts()
                    route.finish()

            pe.sem_inc(ctx_ready, 1)
            for n in range(UNITS):
                max_scores(n)
            turn_negated(0)
            for n in range(UNITS, UNITS + LEAD):
                max_scores(n)
            for place in range(GH):
                scores(0, place)
            for s in range(FIRST):
                step(s)
            with pe.Fori(0, PAIRS - 1):
                for s in range(FIRST, FIRST + PAIR):
                    step(s, signal_v=s % STEPS == 0)
                pe.sem_inc(max_taken, taken.back(2 * UNITS))
                pe.sem_inc(probs_ready, probs_in.back(GH * PAIR))
                pe.sem_inc(neg_parts_ready, negs.back(2))
                pe.sem_inc(v_ready, v_in.back(2))
                pe.sem_inc(ctx_t_ready, evacuated.back(4))
                pe.sem_inc(ctx_ready, normed.back(4))
                for i in range(2):
                    pe.sem_inc(max_in[i], maxima_in[i].back(16 * LOADS))
                    pe.sem_inc(exp_in[i], exps_in[i].back(16 * LOADS))
                    pe.sem_inc(rows_in[i], rows[i].back(16 * GH))
            for s in range(FIRST, PAIR):
                step(s, last=True)
            turn_ctx(3)
            pe.wait_ge(max_in[0], maxima_in[0].more(16 * LOADS))

        @block.scalar
        def _(act):
            scores_in, added, turned = Count(), Count(), Count()

            def exps(s, evacuate=None):
                for place in range(GH):
                    if place == 2 and evacuate is not None:
                        copy_ctx(evacuate)
                    n = GH * s + place
                    act.wait_ge(scores_ready, scores_in.at(n + 1))
                    if s >= RING and place == 0:
                        act.wait_ge(ctx_added, added.at(s - RING + 1))
                    act.activation(probs[:, s % RING, place, :], ps_scores[n % 2][:], ACT.Exp,
                                   scale=float(HD) ** -0.5).then_inc(probs_ready, 1)

            def copy_ctx(chunk):
                act.wait_ge(ctx_added, added.at(NT * (chunk + 1)))
                act.copy(ctx_t[chunk % 2][:], ps_ctx[:]).then_inc(ctx_t_ready, 1)

            def copy_negated(g):
                act.wait_ge(neg_turned, turned.at(g + 1))
                act.copy(neg_rows[g % 2][:], ps_turn[:].bitcast(BF16)[0:GH * 3 * NT, 0:P]).then_inc(neg_rows_ready, 1)

            def step(s, last=False):
                if (g := chain_step(s - 2)) is not None and not (last and g == 2):
                    copy_negated(g)
                chunk = s // NT if s % NT == NT - 1 else None
                if last and s == PAIR - 1:
                    copy_ctx(chunk)
                else:
                    exps(s + 1, chunk)
                if last and s >= MAX_DONE - 1:
                    route_step(s - MAX_DONE)

            route = route_on_act(act, k, r, banks)

            def route_step(n):
                if n == -1:
                    route.ctx(0)
                if n == 1:
                    route.copy(r.ctx_t)
                if n == 2:
                    route.ctx(1)
                if n == 5:
                    route.copy(r.ctx_t, early_banks)
                if n == 8:
                    route.copy(r.h_t)
                if n == 10:
                    route.silu()
                    route.finish()

            copy_negated(0)
            exps(0)
            for s in range(FIRST):
                step(s)
            with act.Fori(0, PAIRS - 1):
                for s in range(FIRST, FIRST + PAIR):
                    step(s)
                act.sem_inc(scores_ready, scores_in.back(GH * PAIR))
                act.sem_inc(ctx_added, added.back(PAIR))
                act.sem_inc(neg_turned, turned.back(2))
            for s in range(FIRST, PAIR):
                step(s, last=True)

        @block.vector
        def _(dve):
            scored, own = Count(), Count()
            turned, inverted = Count(), Count()

            def take_max(n):
                head, tile = unit(n)
                g = n // UNITS
                dve.wait_ge(max_scores_ready, scored.at(n + 1))
                dve.reduce_max(row_max[g % 2][:, head, tile:tile + 1], ps_max[n % 2][:],
                               axis=AX.X).then_inc(max_taken, 1)

            def split_negated(g):
                top, out = row_max[g % 2], neg_parts[g % 2]
                dve.drain().then_inc(neg_step, 1)
                dve.wait_ge(neg_step, own.more())
                dve.tensor_scalar(out[:, :, 0, :], top[:], -1.0, None, ALU.mult).then_inc(neg_step, 1)
                dve.wait_ge(neg_step, own.more())
                dve.scalar_tensor_tensor(out=neg_rest[:], in0=top[:], scalar=-1.0, in1=out[:, :, 0, :],
                                         op0=ALU.mult, op1=ALU.subtract).then_inc(neg_step, 1)
                dve.wait_ge(neg_step, own.more())
                dve.tensor_copy(out[:, :, 1, :], neg_rest[:]).then_inc(neg_step, 1)
                dve.wait_ge(neg_step, own.more())
                dve.tensor_tensor(out[:, :, 2, :], neg_rest[:], out[:, :, 1, :],
                                  ALU.subtract).then_inc(neg_parts_ready, 1)

            def norm_ctx(chunk, pair):
                dve.wait_ge(ctx_turned, turned.at(chunk + 1))
                view = ps_turn[:].rearrange("p (t c) -> p t c", c=32)
                dve.reciprocal(inv_sum[:], view[:, :, HD]).then_inc(sums_inverted, 1)
                dve.wait_ge(sums_inverted, inverted.more())
                out = k["ctx"][:, 2 * pair + chunk // 2].rearrange("p (c t) (h f) -> p c (t h) f", c=2, h=GH)
                dve.tensor_tensor(out[:, chunk % 2], view[:, :, 0:HD],
                                  inv_sum[:].unsqueeze(2).to_broadcast([P, 4 * GH, HD]),
                                  ALU.mult).then_inc(ctx_ready, 1)

            def step(s, pair, last=False):
                more_units = not (last and units(s)[0] >= 2 * UNITS)
                if more_units:
                    take_max(units(s)[0])
                    take_max(units(s)[1])
                if s % NT == 1 and s > NT:
                    norm_ctx(s // NT - 1, pair)
                if (g := chain_step(s)) is not None and not (last and g == 2):
                    split_negated(g)
                if last and s >= MAX_DONE:
                    route_step(s - MAX_DONE)

            route = route_on_dve(dve, k, r, banks)

            def route_step(n):
                if n == 0:
                    dve.wait_ge(r.tables_ready, NTABLES)
                    dve.sem_inc(r.ps_r_free, 1)
                if n == 3:
                    route.gate(0)
                    route.residual(0)
                    route.stats(0, 0)
                    route.stats(0, 1)
                    route.variance()
                if n == 5:
                    route.norm(0, 0)
                    route.norm(0, 1)
                    route.modulate(0)
                    route.shift(0, early=True)
                if n == 7:
                    route.gate(1, early_banks)
                    route.residual(1)
                    route.stats(1, 0)
                    route.stats(1, 1)
                    route.variance()
                if n == 12:
                    route.first_choice()
                    route.second_choice()
                    route.slots(0)
                if n == 13:
                    route.norm(1, 0)
                    route.norm(1, 1)
                if n == 15:
                    route.modulate(1)
                    route.shift(1, r.xm, early=True)
                    route.finish(batches=0)

            for n in range(UNITS):
                take_max(n)
            split_negated(0)
            for n in range(UNITS, UNITS + LEAD):
                take_max(n)
            for s in range(FIRST):
                step(s, 0)
            dve.sem_inc(neg_step, own.back())
            with dve.Fori(0, PAIRS - 1) as p:
                for s in range(FIRST, FIRST + PAIR):
                    step(s, p)
                dve.sem_inc(max_scores_ready, scored.back(2 * UNITS))
                dve.sem_inc(neg_step, own.back(8))
                dve.sem_inc(ctx_turned, turned.back(4))
                dve.sem_inc(sums_inverted, inverted.back(4))
            for s in range(FIRST, PAIR):
                step(s, PAIRS - 1, last=True)
            norm_ctx(3, PAIRS - 1)


class Routing:
    pass


class Steps:
    pass


def routing(nc, ctx, k):
    def sb(name, shape, dt=F32):
        return ctx.enter_context(nc.sbuf_tensor(name, shape, dt))

    def sem(name):
        return ctx.enter_context(nc.semaphore(name))

    r = Routing()
    r.wo, r.rw1, r.rw2, r.rb1, r.rb2, r.before = (k[name] for name in ("wo", "rw1", "rw2", "rb1", "rb2", "before"))
    r.xm, r.h = sb("xm2", [P, NT, D]), sb("h2", [P, NT, D])
    r.stats, r.mean_var = sb("stats2", [P, NT, 6]), sb("mean_var2", [P, NT, 2])
    r.var_eps, r.scale = sb("var_eps2", [P, NT]), sb("scale2", [P, NT])
    wide = [P, NT, NE]
    r.order = sb("order", [P, NE])
    r.lower = sb("lower", [P, NE, NE])
    r.tile_no = sb("tile_no", [P, TILES_B, NE])
    r.ones = sb("ones", [P, P])
    r.slot_base = sb("slot_base", [P, B, 1])
    r.logit, r.left = sb("logit", wide), sb("left", wide)
    r.cand, r.chosen = [sb(f"cand{i}", wide) for i in range(2)], [sb(f"chosen{i}", wide) for i in range(2)]
    r.both = sb("both", [P, NT + 1, NE])
    r.top = [sb(f"top{i}", [P, NT]) for i in range(2)]
    r.first = [sb(f"first{i}", [P, NT]) for i in range(2)]
    r.gap, r.tanh_gap = sb("gap", [P, NT]), sb("tanh_gap", [P, NT])
    r.weight = sb("weight", [P, B, 2, NT])
    r.tiles_i, r.tiles_s, r.tiles_f = sb("tiles_i", [P, NE], I32), sb("tiles_s", [P, NE], I32), sb("tiles_f", [P, NE])
    r.lower_tiles = sb("lower_tiles", [P, NE, NE])
    r.start, r.end, r.start_slot = sb("start", [P, NE]), sb("end", [P, NE]), sb("start_slot", [P, NE])
    r.place_all = sb("place_all", wide)
    r.place_of = [sb(f"place_of{i}", wide) for i in range(2)]
    r.place = sb("place", [P, 2, NT])
    r.slot = sb("slot", [P, B, 2, NT], I32)
    r.slot_now = sb("slot_now", [P, 2, NT], I32)
    r.ended = sb("ended", [P, TILES_B, NE])
    r.expert_f = sb("expert_f", [P, TILES_B])
    r.expert = sb("expert", [P, B, TILES_B], I32)
    r.tables_ready = sem("tables_ready")
    r.scattered = sem("scattered")
    r.ctx_s_ready = sem("ctx_s_ready")
    r.turned = sem("route_turned")
    r.copied = sem("route_copied")
    r.attn_ready = sem("attn_ready")
    r.dve_done = sem("mix_dve_done")
    r.var_ready = sem("var2_ready")
    r.scale_ready = sem("scale2_ready")
    r.h_ready = sem("h2_ready")
    r.h_ready_pool = sem("h2_ready_pool")
    r.gated_h_ready = sem("gated_h_ready")
    r.x_updated = sem("x_updated")
    r.router_ps_ready = sem("router_ps_ready")
    r.router_act_ready = sem("router_act_ready")
    r.logits_ready = sem("logits_ready")
    r.both_ready = sem("both_ready")
    r.counts_ready = sem("counts_ready")
    r.gap_ready = sem("gap_ready")
    r.tanh_ready = sem("tanh_ready")
    r.slot_ready = sem("slot_ready")
    r.ps_r_used = sem("ps_route_used")
    r.ps_r_free = sem("ps_route_free")
    r.slot_now_ready = sem("slot_now_ready")
    return r


def route_buffers(r, sb, suffix, ctx_t=None, gated=None):
    r.ctx_s = sb(f"ctx_s{suffix}", [P, NT, GROUPS, GF])
    r.ctx_t = sb(f"route_ctx_t{suffix}", [P, S]) if ctx_t is None else ctx_t
    r.gated = sb(f"gated{suffix}", [P, NT, D]) if gated is None else gated
    r.xn = sb(f"route_xn{suffix}", [P, NT, D])
    r.gated_h = sb(f"gated_h{suffix}", [P, NT, D])
    r.h_t, r.router_act = sb(f"route_h_t{suffix}", [P, S]), sb(f"router_act{suffix}", [P, S])
    return r


def route_on_pool(pool, k, r, banks):
    var, h_in, slot_in, now, gated_in = (Count() for _ in range(5))

    def norm_scale():
        pool.wait_ge(r.var_ready, var.more())
        pool.tensor_tensor(r.scale[:], r.var_eps[:], k["rsqrt_exp"][:], ALU.pow).then_inc(r.scale_ready, 1)
        pool.sem_inc(r.var_ready, var.back())

    def update(b, h):
        pool.wait_ge(r.h_ready_pool, h_in.more())
        pool.tensor_tensor(r.gated_h[:], h[:], k["mod"][:, b, 5, :].unsqueeze(1).to_broadcast([P, NT, D]),
                           ALU.mult).then_inc(r.gated_h_ready, 1)
        pool.wait_ge(r.gated_h_ready, gated_in.more())
        pool.tensor_tensor(k["x"][:, b], k["x"][:, b], r.gated_h[:], ALU.add).then_inc(r.x_updated, 1)
        pool.sem_inc(r.h_ready_pool, h_in.back())
        pool.sem_inc(r.gated_h_ready, gated_in.back())

    def scatter_start(b):
        pool.wait_ge(r.slot_ready, slot_in.more())
        pool.tensor_copy(r.slot_now[:], r.slot[:, b]).then_inc(r.slot_now_ready, 1)
        pool.wait_ge(r.slot_now_ready, now.more())
        pool.sem_inc(r.slot_ready, slot_in.back())
        pool.sem_inc(r.slot_now_ready, now.back())

    def scatter(n):
        for i in range(NT):
            pool.indirect_dma_start(k["slots"], bass.IndirectOffsetOnAxis(r.slot_now[:, n, i:i + 1], axis=0),
                                    r.h[:, i, :], None).then_inc(r.scattered, 16)

    steps = Steps()
    steps.norm_scale = norm_scale
    steps.update = update
    steps.scatter_start = scatter_start
    steps.scatter = scatter
    return steps


def route_on_act(act, k, r, banks):
    turns, routed, gaps = Count(), Count(), Count()
    ctx_of = k["ctx"].rearrange("p (b g) t f -> p b t g f", b=B)

    def ctx(b):
        act.copy(r.ctx_s[:], ctx_of[:, b]).then_inc(r.ctx_s_ready, 1)

    def copy(dst, banks=banks):
        for c in range(2):
            act.wait_ge(r.turned, turns.more())
            act.copy(dst[:, c * BANK:(c + 1) * BANK], banks[c]).then_inc(r.copied, 1)

    def silu():
        for c in range(2):
            act.wait_ge(r.router_ps_ready, routed.more())
            act.activation(r.router_act[:, c * BANK:(c + 1) * BANK], banks[c], ACT.Silu,
                           bias=r.rb1[:]).then_inc(r.router_act_ready, 1)

    def tanh():
        act.wait_ge(r.gap_ready, gaps.more())
        act.activation(r.tanh_gap[:], r.gap[:], ACT.Tanh, scale=0.5).then_inc(r.tanh_ready, 1)

    def finish():
        if turns.seen:
            act.sem_inc(r.turned, turns.back())
        if routed.seen:
            act.sem_inc(r.router_ps_ready, routed.back())
        if gaps.seen:
            act.sem_inc(r.gap_ready, gaps.back())

    steps = Steps()
    steps.ctx = ctx
    steps.copy = copy
    steps.silu = silu
    steps.tanh = tanh
    steps.finish = finish
    return steps


def route_on_dve(dve, k, r, banks):
    wide = [P, NT, NE]
    own, scaled, attn, logits_in, count_in, tanhs, updated, ps_read = (Count() for _ in range(8))

    def mod(b, i):
        return k["mod"][:, b, i, :].unsqueeze(1).to_broadcast([P, NT, D])

    def over_e(v):
        return v[:].unsqueeze(2).to_broadcast(wide)

    def link(ins):
        ins.then_inc(r.dve_done, 1)
        dve.wait_ge(r.dve_done, own.more())

    def gate(b, banks=banks):
        for i, bank in enumerate(banks):
            tiles = slice(i * NT // 2, (i + 1) * NT // 2)
            dve.wait_ge(r.attn_ready, attn.more())
            dve.tensor_tensor(r.gated[:, tiles], bank.rearrange("p (t d) -> p t d", d=D),
                              mod(b, 2)[:, tiles], ALU.mult).then_inc(r.dve_done, 1)
        dve.wait_ge(r.dve_done, own.more(2))

    def residual(b):
        link(dve.tensor_tensor(k["x"][:, b], k["x"][:, b], r.gated[:], ALU.add))

    def stats(b, half):
        for i in range(half * NT // 2, (half + 1) * NT // 2):
            dve.bn_stats(r.stats[:, i, :], k["x"][:, b, i, :]).then_inc(r.dve_done, 1)
        dve.wait_ge(r.dve_done, own.more(NT // 2))

    def variance():
        for i in range(NT):
            dve.bn_aggr(r.mean_var[:, i, :], r.stats[:, i, :]).then_inc(r.dve_done, 1)
        dve.wait_ge(r.dve_done, own.more(NT))
        dve.tensor_scalar(r.var_eps[:], r.mean_var[:, :, 1], EPS, None, ALU.add).then_inc(r.var_ready, 1)

    def norm(b, half):
        if half == 0:
            dve.wait_ge(r.scale_ready, scaled.more())
        for i in range(half * NT // 2, (half + 1) * NT // 2):
            dve.tensor_scalar(r.xn[:, i, :], k["x"][:, b, i, :], r.mean_var[:, i, 0:1], r.scale[:, i:i + 1],
                              ALU.subtract, ALU.mult).then_inc(r.dve_done, 1)
        dve.wait_ge(r.dve_done, own.more(NT // 2))

    def modulate(b):
        link(dve.tensor_tensor(r.xm[:], r.xn[:], mod(b, 4), ALU.mult))

    def shift(b, h=r.h, early=False):
        if not early:
            dve.wait_ge(r.scattered, 16 * 2 * NT * b)
        dve.tensor_tensor(h[:], r.xm[:], mod(b, 3), ALU.add).then_inc(r.h_ready, 1)
        dve.drain().then_inc(r.h_ready_pool, 1)

    def top(n):
        of = r.logit if n == 0 else r.left
        link(dve.tensor_reduce(r.top[n][:], of[:], axis=AX.X, op=ALU.max))
        link(dve.tensor_tensor(r.cand[0][:], of[:], over_e(r.top[n]), ALU.is_equal))
        link(dve.tensor_tensor(r.cand[1][:], r.cand[0][:], r.order[:].unsqueeze(1).to_broadcast(wide), ALU.mult))
        link(dve.tensor_reduce(r.first[n][:], r.cand[1][:], axis=AX.X, op=ALU.max))
        link(dve.tensor_tensor(r.chosen[n][:], r.cand[1][:], over_e(r.first[n]), ALU.is_equal))

    def first_choice():
        dve.wait_ge(r.logits_ready, logits_in.more())
        link(dve.tensor_tensor(r.logit[:], banks[0][:, 0:NT * NE].rearrange("p (t e) -> p t e", e=NE),
                               r.rb2[:].unsqueeze(1).to_broadcast(wide), ALU.add))
        top(0)
        link(dve.scalar_tensor_tensor(out=r.left[:], in0=r.chosen[0][:], scalar=-3e38, in1=r.logit[:],
                                      op0=ALU.mult, op1=ALU.add))

    def second_choice():
        top(1)
        dve.tensor_tensor(r.both[:, 0:NT, :], r.chosen[0][:], r.chosen[1][:], ALU.add).then_inc(r.both_ready, 1)
        dve.tensor_tensor(r.gap[:], r.top[0][:], r.top[1][:], ALU.subtract).then_inc(r.gap_ready, 1)

    def slots(b):
        dve.wait_ge(r.counts_ready, count_in.more())
        count = banks[1][:, 0:(NT + 1) * NE].rearrange("p (t e) -> p t e", e=NE)
        link(dve.tensor_scalar(r.tiles_i[:], count[:, NT, :], float(P - 1), None, ALU.add))
        link(dve.tensor_scalar(r.tiles_s[:], r.tiles_i[:], P.bit_length() - 1, None, ALU.logical_shift_right))
        link(dve.tensor_copy(r.tiles_f[:], r.tiles_s[:]))
        link(dve.tensor_tensor(r.lower_tiles[:], r.lower[:], r.tiles_f[:].unsqueeze(1).to_broadcast([P, NE, NE]),
                               ALU.mult))
        link(dve.tensor_reduce(r.start[:], r.lower_tiles[:], axis=AX.X, op=ALU.add))
        dve.tensor_tensor(r.end[:], r.start[:], r.tiles_f[:], ALU.add).then_inc(r.dve_done, 1)
        dve.tensor_scalar(r.start_slot[:], r.start[:], float(P), r.slot_base[:, b, :], ALU.mult,
                          ALU.add).then_inc(r.dve_done, 1)
        dve.wait_ge(r.dve_done, own.more(2))
        dve.tensor_tensor(r.place_all[:], count[:, 0:NT, :], r.start_slot[:].unsqueeze(1).to_broadcast(wide),
                          ALU.add).then_inc(r.ps_r_used, 1)
        dve.wait_ge(r.ps_r_used, ps_read.more())
        dve.sem_inc(r.ps_r_free, 1)
        for n in range(2):
            dve.tensor_tensor(r.place_of[n][:], r.chosen[n][:], r.place_all[:], ALU.mult).then_inc(r.dve_done, 1)
        dve.wait_ge(r.dve_done, own.more(2))
        for n in range(2):
            dve.tensor_reduce(r.place[:, n, :], r.place_of[n][:], axis=AX.X, op=ALU.add).then_inc(r.dve_done, 1)
        dve.wait_ge(r.dve_done, own.more(2))
        dve.tensor_copy(r.slot[:, b], r.place[:]).then_inc(r.slot_ready, 1)

    def weights(b):
        dve.wait_ge(r.tanh_ready, tanhs.more())
        dve.tensor_scalar(r.weight[:, b, 0, :], r.tanh_gap[:], 0.5, 0.5, ALU.mult, ALU.add)
        dve.tensor_scalar(r.weight[:, b, 1, :], r.tanh_gap[:], -0.5, 0.5, ALU.mult, ALU.add)
        link(dve.tensor_tensor(r.ended[:], r.end[:].unsqueeze(1).to_broadcast([P, TILES_B, NE]), r.tile_no[:],
                               ALU.is_le))
        link(dve.tensor_reduce(r.expert_f[:], r.ended[:], axis=AX.X, op=ALU.add))
        link(dve.tensor_scalar(r.expert[:, b, :], r.expert_f[:], float(NE - 1), None, ALU.min))

    def finish(batches=1):
        if attn.seen:
            dve.sem_inc(r.attn_ready, attn.back())
        if scaled.seen:
            dve.sem_inc(r.scale_ready, scaled.back())
        if logits_in.seen:
            dve.sem_inc(r.logits_ready, logits_in.back())
        if count_in.seen:
            dve.sem_inc(r.counts_ready, count_in.back())
        if ps_read.seen:
            dve.sem_inc(r.ps_r_used, ps_read.back())
        if tanhs.seen:
            dve.sem_inc(r.tanh_ready, tanhs.back())
        for _ in range(batches):
            dve.wait_ge(r.x_updated, updated.more())
        if updated.seen:
            dve.sem_inc(r.x_updated, updated.back())
        if own.seen:
            dve.sem_inc(r.dve_done, own.back())

    steps = Steps()
    steps.mod = mod
    steps.over_e = over_e
    steps.link = link
    steps.gate = gate
    steps.residual = residual
    steps.stats = stats
    steps.variance = variance
    steps.norm = norm
    steps.modulate = modulate
    steps.shift = shift
    steps.first_choice = first_choice
    steps.second_choice = second_choice
    steps.slots = slots
    steps.weights = weights
    steps.finish = finish
    steps.own = own
    return steps


def route_on_pe(pe, k, r, banks):
    staged, copies, h_in, acts, chosen_in, frees = (Count() for _ in range(6))

    def turn(to, src):
        for i in range(NT):
            at = i * P % BANK
            ins = pe.transpose(to[i * P // BANK][:, at:at + P], src[:, i], k["ident"][:])
            if at + P == BANK:
                ins.then_inc(r.turned, 1)

    def turn_ctx(banks=banks, wait=True):
        if wait:
            pe.wait_ge(r.ps_r_free, frees.more())
        pe.wait_ge(r.ctx_s_ready, staged.more())
        turn(banks, r.ctx_s[:].rearrange("p t g f -> p t (g f)"))

    def project(banks=banks):
        for i in range(NT):
            at = i * P % BANK
            if at == 0:
                pe.wait_ge(r.copied, copies.more())
            ins = pe.matmul(banks[i * P // BANK][:, at:at + P], r.ctx_t[:, i * P:(i + 1) * P], r.wo[:],
                            start=True, stop=True)
            if at + P == BANK:
                ins.then_inc(r.attn_ready, 1)

    def turn_h(h=r.h):
        pe.wait_ge(r.h_ready, h_in.more())
        turn(banks, h[:])

    def router():
        for c in range(2):
            pe.wait_ge(r.copied, copies.more())
            pe.matmul(banks[c], r.rw1[:], r.h_t[:, c * BANK:(c + 1) * BANK],
                      start=True, stop=True).then_inc(r.router_ps_ready, 1)

    def logits():
        pe.wait_ge(r.router_act_ready, acts.more(2))
        for i in range(NT):
            ins = pe.matmul(banks[0][:, i * NE:(i + 1) * NE], r.router_act[:, i * P:(i + 1) * P], r.rw2[:],
                            start=True, stop=True)
        ins.then_inc(r.logits_ready, 1)

    def counts():
        pe.wait_ge(r.both_ready, chosen_in.more())
        count = banks[1][:, 0:(NT + 1) * NE]
        pe.matmul(count, r.before[:], r.both[:].rearrange("p t e -> p (t e)"), start=True, stop=False)
        for i in range(NT):
            ins = pe.matmul(count[:, (i + 1) * NE:].rearrange("p (t e) -> p t e", e=NE), r.ones[:],
                            r.both[:, i:i + 1, :].to_broadcast([P, NT - i, NE]),
                            start=False, stop=i == NT - 1)
        ins.then_inc(r.counts_ready, 1)

    def finish():
        if frees.seen:
            pe.sem_inc(r.ps_r_free, frees.back())
        if staged.seen:
            pe.sem_inc(r.ctx_s_ready, staged.back())
        if copies.seen:
            pe.sem_inc(r.copied, copies.back())
        if h_in.seen:
            pe.sem_inc(r.h_ready, h_in.back())
        if acts.seen:
            pe.sem_inc(r.router_act_ready, acts.back())
        if chosen_in.seen:
            pe.sem_inc(r.both_ready, chosen_in.back())

    steps = Steps()
    steps.turn_ctx = turn_ctx
    steps.project = project
    steps.turn_h = turn_h
    steps.router = router
    steps.logits = logits
    steps.counts = counts
    steps.finish = finish
    steps.frees = frees
    return steps


def mix(nc, t, k):
    with ExitStack() as ctx:
        def sb(name, shape, dt=F32):
            return ctx.enter_context(nc.sbuf_tensor(name, shape, dt))

        def psum(name, shape, dt=F32):
            return ctx.enter_context(nc.psum_tensor(name, shape, dt))

        def sem(name):
            return ctx.enter_context(nc.semaphore(name))

        W_UP, W_B1, W_B2, W_END = 0, HID, HID + HC, HID + HC + D
        w_all = sb("w_all", [P, NE, W_END])
        w_down = sb("w_down", [P, NE, HC, D])
        w_tile = [sb(f"w_tile{i}", [P, W_END]) for i in range(WRING)]
        slots_in = [sb(f"slots_in{i}", [P, QUAD, D]) for i in range(QRING)]
        slots_t = [sb(f"slots_t{i}", [P, P]) for i in range(2)]
        hid = [sb(f"hid{i}", [P, HC, P]) for i in range(2)]
        y = sb("y", [P, TILES_B, D])
        slot_back = sb("slot_back", [P, 2, NT], I32)
        rows = [sb(f"rows{i}", [P, NT, D]) for i in range(2)]
        scaled_rows = [sb(f"scaled_rows{i}", [P, NT, D]) for i in range(2)]
        mixed, mixed_g = sb("mixed", [P, NT, D]), sb("mixed_g", [P, NT, D])
        ps_t = [psum(f"ps_slots_t{i}", [P, BANK]) for i in range(2)]
        ps_up = [psum(f"ps_up{i}", [P, BANK]) for i in range(2)]
        ps_down = [psum(f"ps_down{i}", [P, BANK]) for i in range(2)]
        ps_r = psum("ps_route", [P, 2 * BANK])

        up_weights_in = sem("up_weights_in")
        down_weights_in = sem("down_weights_in")
        slots_loaded = [sem(f"slots_loaded{i}") for i in range(QRING)]
        slots_used = sem("slots_used")
        slots_turned = sem("slots_turned")
        slots_t_ready = sem("slots_t_ready")
        w_ready = sem("w_ready")
        up_ready = sem("up_ready")
        hid_ready = sem("hid_ready")
        down_ready = sem("down_ready")
        y_done = sem("y_done")
        last_bank_free = sem("last_bank_free")
        y_ready = sem("y_ready")
        y_stored = sem("y_stored")
        y_free = sem("y_free")
        y_landed = sem("y_landed")
        h_moved = sem("h_moved")
        slot_back_ready = sem("slot_back_ready")
        gathered = [sem(f"gathered{i}") for i in range(2)]
        rows_used = sem("rows_used")
        out_ready = sem("out_ready")
        out_stored = sem("out_stored")
        r = route_buffers(k["routing"], sb, "_mix")
        banks = (ps_r[:, 0:BANK], ps_r[:, BANK:])
        block = ctx.enter_context(nc.Block())
        up_loads = [(w_all[:, :, W_UP:W_B1], t["we1"].rearrange("e d h -> d e h")), (w_all[:, :, W_B1:W_B2], t["be1"])]
        up_loads += [(w_all[:, e, W_B2:W_END], t["be2"][e:e + 1, :].to_broadcast([P, D])) for e in range(NE)]
        down_loads = [(w_down[:, e], t["we2"][e].rearrange("(c p) d -> p c d", p=P)) for e in range(NE)]

        @block.sync
        def _(sp):
            for dst, src in up_loads:
                sp.dma_start(dst, src).then_inc(up_weights_in, 16)
            used, ready = Count(), Count()
            stored = Count()
            quad_in = k["slots"].rearrange("(b q s p) d -> b q p s d", b=B, s=QUAD, p=P)
            quad_out = k["y_slots"].rearrange("(b q s p) d -> b q p s d", b=B, s=QUAD, p=P)
            out = t["out"].rearrange("b (t p) d -> b p t d", p=P)

            def load(b, q):
                sp.wait_ge(slots_used, used.more())
                sp.dma_start(slots_in[q % QRING][:], quad_in[b, q]).then_inc(slots_loaded[q % QRING], 16)

            def load_first(b):
                sp.wait_ge(r.scattered, 16 * 2 * NT * (b + 1))
                for q in range(QRING - 1):
                    load(b, q)

            def body(b, more, finished):
                for q in range(QUADS):
                    if q + QRING - 1 < QUADS:
                        load(b, q + QRING - 1)
                    if q == QUADS - 1 and more:
                        load_first(b + 1)
                    sp.wait_ge(y_ready, ready.more())
                    sp.dma_start(quad_out[b, q], y[:, QUAD * q:QUAD * (q + 1), :]).then_inc(y_stored, 16)
                    if q in finished:
                        store_out(finished[q])
                sp.wait_ge(y_stored, stored.more(16 * QUADS))
                sp.sem_inc(y_free, 1)
                sp.sem_inc(y_landed, 1)
                sp.sem_inc(slots_used, used.back(QUADS))
                sp.sem_inc(y_ready, ready.back())
                sp.sem_inc(y_stored, stored.back())

            def store_out(b):
                for half in range(2):
                    tiles = slice(half * NT // 2, (half + 1) * NT // 2)
                    sp.wait_ge(out_ready, 2 * b + half + 1)
                    sp.dma_start(out[b, :, tiles], k["x"][:, b, tiles]).then_inc(out_stored, 16)

            sp.sem_inc(slots_used, QRING)
            sp.sem_inc(y_free, 1)
            load_first(0)
            for dst, src in down_loads:
                sp.dma_start(dst, src).then_inc(down_weights_in, 16)
            with sp.Fori(0, B - 2) as b:
                body(b, True, {})
            body(B - 2, True, {QUADS - 1: 0})
            body(B - 1, False, {2: 1, QUADS - 1: 2})
            store_out(B - 1)
            sp.wait_ge(out_stored, 16 * 2 * B)

        @block.gpsimd
        def _(pool):
            route = route_on_pool(pool, k, r, banks)

            def scatter_and_route(b):
                route.scatter_start(b)
                route.scatter(0)
                route.scatter(1)
                route.norm_scale()
                route.update(b + 1, r.h)

            def combine_gather(b):
                pool.wait_ge(y_landed, b + 1)
                if b:
                    pool.wait_ge(rows_used, b)
                pool.tensor_copy(slot_back[:], r.slot[:, b]).then_inc(slot_back_ready, 1)
                pool.wait_ge(slot_back_ready, b + 1)
                for i in range(NT):
                    for n in range(2):
                        pool.indirect_dma_start(rows[n][:, i, :], None, k["y_slots"],
                                                bass.IndirectOffsetOnAxis(slot_back[:, n, i:i + 1], axis=0)
                                                ).then_inc(gathered[2 * i // NT], 16)

            route.update(1, r.xm)
            pool.wait_ge(h_moved, 1)
            with pool.Fori(0, B - 2) as b:
                scatter_and_route(b + 1)
            route.scatter_start(B - 1)
            route.scatter(0)
            route.scatter(1)
            for b in range(B):
                combine_gather(b)

        @block.scalar
        def _(act):
            slots, ups = Count(), Count()
            route = route_on_act(act, k, r, banks)

            def turned_rows(n):
                act.wait_ge(slots_turned, slots.more())
                act.copy(slots_t[n % 2][:], ps_t[n % 2][:, 0:P]).then_inc(slots_t_ready, 1)

            def hidden(n):
                act.wait_ge(up_ready, ups.more())
                for c in range(HC):
                    ins = act.activation(hid[n % 2][:, c, :], ps_up[n % 2][:, c * P:(c + 1) * P], ACT.Silu,
                                         bias=w_tile[n % WRING][:, W_B1 + c:W_B1 + c + 1])
                ins.then_inc(hid_ready, 1)

            def body(b, more, routed):
                if routed:
                    route.ctx(b + 2)
                for n in range(TILES_B):
                    if n + 2 < TILES_B or more:
                        turned_rows((n + 2) % TILES_B)
                    if n + 1 < TILES_B or more:
                        hidden((n + 1) % TILES_B)
                    if routed and n == 1:
                        route.copy(r.ctx_t)
                    if routed and n == 13:
                        route.copy(r.h_t)
                    if routed and n == 15:
                        route.silu()
                    if routed and n == 20:
                        route.tanh()
                act.sem_inc(slots_turned, slots.back(TILES_B if more else None))
                act.sem_inc(up_ready, ups.back(TILES_B if more else None))
                if routed:
                    route.finish()

            route.tanh()
            route.copy(r.h_t)
            route.silu()
            route.tanh()
            act.wait_ge(r.scattered, 16 * 2 * NT)
            act.copy(r.h[:], r.xm[:]).then_inc(h_moved, 1)
            route.finish()
            turned_rows(0)
            turned_rows(1)
            hidden(0)
            with act.Fori(0, B - 2) as b:
                body(b, True, True)
            body(B - 2, True, False)
            body(B - 1, False, False)

        @block.vector
        def _(dve):
            route = route_on_dve(dve, k, r, banks)
            mod, link, own = route.mod, route.link, route.own
            downs, ys, y_room = Count(), Count(), Count()

            def expert_of(b, n):
                return dve.value_load(r.expert[0:1, b, n:n + 1], min_val=0, max_val=NE - 1)

            def copy_w(n, e):
                dve.tensor_copy(w_tile[n % WRING][:], w_all[:, e, :]).then_inc(w_ready, 1)

            def combine_scale(b, half):
                dve.wait_ge(gathered[half], 16 * NT * (b + 1))
                tiles = slice(half * NT // 2, (half + 1) * NT // 2)
                for n in range(2):
                    w = r.weight[:, b, n, tiles].unsqueeze(2).to_broadcast([P, NT // 2, D])
                    dve.tensor_tensor(scaled_rows[n][:, tiles], rows[n][:, tiles], w, ALU.mult).then_inc(r.dve_done, 1)
                dve.wait_ge(r.dve_done, own.more(2))
                if half:
                    dve.sem_inc(rows_used, 1)

            def combine_add(half):
                tiles = slice(half * NT // 2, (half + 1) * NT // 2)
                link(dve.tensor_tensor(mixed[:, tiles], scaled_rows[0][:, tiles], scaled_rows[1][:, tiles], ALU.add))

            def combine_gate(b, half):
                tiles = slice(half * NT // 2, (half + 1) * NT // 2)
                link(dve.tensor_tensor(mixed_g[:, tiles], mixed[:, tiles], mod(b, 5)[:, tiles], ALU.mult))
                dve.tensor_tensor(k["x"][:, b, tiles], k["x"][:, b, tiles], mixed_g[:, tiles],
                                  ALU.add).then_inc(out_ready, 1)

            def body(b, more, routed, combines):
                for n in range(TILES_B):
                    if n == 0:
                        dve.wait_ge(y_free, y_room.more())
                    ahead = n + WRING - 1
                    if ahead < TILES_B or more:
                        e = expert_of(b + ahead // TILES_B, ahead % TILES_B)
                    dve.wait_ge(down_ready, downs.more())
                    dve.tensor_tensor(y[:, n, :], ps_down[n % 2][:, 0:D], w_tile[n % WRING][:, W_B2:W_END],
                                      ALU.add).then_inc(y_done, 1)
                    if n:
                        dve.wait_ge(y_done, ys.more())
                    if n and n % QUAD == 0:
                        dve.sem_inc(y_ready, 1)
                    if n == TILES_B - 2 and not more:
                        dve.sem_inc(last_bank_free, 1)
                    if ahead < TILES_B or more:
                        copy_w(ahead % TILES_B, e)
                    if routed:
                        if n == 3:
                            route.gate(b + 2)
                        if n == 4:
                            route.residual(b + 2)
                        if n in (5, 6):
                            route.stats(b + 2, n - 5)
                        if n == 7:
                            route.variance()
                        if n in (8, 9):
                            route.norm(b + 2, n - 8)
                        if n == 10:
                            route.modulate(b + 2)
                        if n == 11:
                            route.shift(b + 2)
                        if n == 17:
                            route.first_choice()
                        if n == 18:
                            route.second_choice()
                        if n == 21:
                            route.slots(b + 2)
                        if n == 22:
                            route.weights(b + 2)
                    for half in range(2):
                        at = n - 4 * half
                        if at in combines:
                            combine_scale(combines[at], half)
                        if at - 1 in combines:
                            combine_add(half)
                        if at - 2 in combines:
                            combine_gate(combines[at - 2], half)
                dve.wait_ge(y_done, ys.more())
                dve.sem_inc(y_ready, 1)
                dve.sem_inc(y_done, ys.back())
                dve.sem_inc(y_free, y_room.back())
                dve.sem_inc(down_ready, downs.back())
                if routed:
                    route.finish()

            route.weights(0)
            route.first_choice()
            route.second_choice()
            dve.wait_ge(up_weights_in, 16 * len(up_loads))
            for n in range(WRING - 1):
                copy_w(n, expert_of(0, n))
            route.slots(1)
            route.weights(1)
            route.finish(batches=2)
            dve.wait_ge(h_moved, 1)
            with dve.Fori(0, B - 2) as b:
                body(b, True, True, {})
            body(B - 2, True, False, {16: 0})
            body(B - 1, False, False, {3: 1, 13: 2})
            for half in range(2):
                combine_scale(B - 1, half)
                combine_add(half)
                combine_gate(B - 1, half)

        @block.tensor
        def _(pe):
            route = route_on_pe(pe, k, r, banks)
            loaded = [Count() for _ in range(QRING)]
            slots, ws, hids, banks_in = (Count() for _ in range(4))

            def turn_slots(n):
                q = n // QUAD
                if n % QUAD == 0:
                    pe.wait_ge(slots_loaded[q % QRING], loaded[q % QRING].more(16))
                ins = pe.transpose(ps_t[n % 2][:, 0:P], slots_in[q % QRING][:, n % QUAD, :], k["ident"][:])
                ins.then_inc(slots_turned, 1)

            def up(n):
                pe.wait_ge(w_ready, ws.more())
                pe.wait_ge(slots_t_ready, slots.more())
                for c in range(HC):
                    ins = pe.matmul(ps_up[n % 2][:, c * P:(c + 1) * P], w_tile[n % WRING][:, c * P:(c + 1) * P],
                                    slots_t[n % 2][:], start=True, stop=True)
                    if c == 0 and n % QUAD == QUAD - 1:
                        ins.then_inc(slots_used, 1)
                ins.then_inc(up_ready, 1)

            def down(b, n, last):
                e = pe.value_load(r.expert[0:1, b, n:n + 1], min_val=0, max_val=NE - 1)
                pe.wait_ge(hid_ready, hids.more())
                if n == TILES_B - 1 and last:
                    pe.wait_ge(last_bank_free, banks_in.more())
                for c in range(HC):
                    ins = pe.matmul(ps_down[n % 2][:, 0:D], hid[n % 2][:, c, :], w_down[:, e, c, :],
                                    start=c == 0, stop=c == HC - 1)
                ins.then_inc(down_ready, 1)

            def body(b, more, routed):
                for n in range(TILES_B):
                    if n + 2 < TILES_B or more:
                        turn_slots((n + 2) % TILES_B)
                    if n + 1 < TILES_B or more:
                        up((n + 1) % TILES_B)
                    down(b, n, not more)
                    if routed:
                        if n == 0:
                            route.turn_ctx()
                        if n == 2:
                            route.project()
                        if n == 12:
                            route.turn_h()
                        if n == 14:
                            route.router()
                        if n == 16:
                            route.logits()
                        if n == 20:
                            route.counts()
                pe.sem_inc(w_ready, ws.back(TILES_B if more else None))
                pe.sem_inc(slots_t_ready, slots.back(TILES_B if more else None))
                pe.sem_inc(hid_ready, hids.back())
                for i in range(QRING):
                    pe.sem_inc(slots_loaded[i], loaded[i].back(16 * QUADS // QRING if more else None))
                if routed:
                    route.finish()

            pe.wait_ge(r.ps_r_free, route.frees.more())
            route.turn_h(r.xm)
            route.router()
            route.logits()
            route.counts()
            route.finish()
            turn_slots(0)
            turn_slots(1)
            up(0)
            pe.wait_ge(down_weights_in, 16 * len(down_loads))
            with pe.Fori(0, B - 2) as b:
                body(b, True, True)
            body(B - 2, True, False)
            body(B - 1, False, False)


def head_order():
    order, angle, is_sin = [], [], []
    for g in range(GROUPS):
        for r in range(2):
            for f in range(HD):
                for u in range(2):
                    order.append((GH * g + 2 * u + r) * HD + f // 2 * 2)
                    angle.append(f // 2)
                    is_sin.append(f % 2)
    return np.array(order), np.array(angle), np.array(is_sin)


def rope_table():
    _, angle, is_sin = head_order()
    freqs = np.exp(np.arange(0, HD, 2, dtype=np.float32) * np.float32(-np.log(10000.0) / HD)).astype(np.float32)
    angles = (np.arange(S, dtype=np.float32)[None, :] * freqs[angle][:, None]).astype(np.float32).astype(np.float64)
    return np.where(is_sin[:, None] == 1, -np.sin(angles), np.cos(angles)).astype(np.float32)


def kernel(**inputs):
    from concourse import bacc
    from concourse.bass_utils import run_bass_kernel_spmd

    i = {name.removeprefix("L0_"): np.asarray(a) for name, a in inputs.items()}
    order, _, _ = head_order()
    arrays = {
        "x": i["attn_x"], "c_t": i["c"].T, "wmod": i["wmod"],
        "wq_t": i["attn_Wq"][order].T, "wk_t": i["attn_Wk"][order].T, "wv_t": i["attn_Wv"].T,
        "wo_t": i["attn_Wo"].T, "rope": rope_table(), "before": np.triu(np.ones((P, P), np.float32), 1),
        "rw1": i["ffn_rw1"], "rb1": i["ffn_rb1"][:, None], "rw2": i["ffn_rw2"], "rb2": i["ffn_rb2"][None, :],
        "we1": i["ffn_we1"], "we2": i["ffn_we2"],
        "be1": i["ffn_be1"].reshape(NE, HID // P, P).transpose(2, 0, 1), "be2": i["ffn_be2"],
    }
    arrays = {name: np.ascontiguousarray(a) for name, a in arrays.items()}
    nc = bacc.Bacc("TRN2", target_bir_lowering=False, num_devices=1)
    t = {name: nc.dram_tensor(f"in_{name}", a.shape, F32, kind="ExternalInput").ap() for name, a in arrays.items()}
    t["out"] = nc.dram_tensor("out", (B, S, D), F32, kind="ExternalOutput").ap()
    build(nc, t)
    return run_bass_kernel_spmd(nc, [{f"in_{name}": a for name, a in arrays.items()}], core_ids=[0]).results[0]["out"]
```
